# Optimizing a Trainium2 kernel written in Bass

```python
import numpy as np
import jax
import jax.numpy as jnp

def _softmax(x, axis=-1):
    return jax.nn.softmax(x, axis=axis)

def _gelu(x):
    return jax.nn.gelu(x, approximate=True)

def _silu(x):
    return jax.nn.silu(x)

def _sigmoid(x):
    return jax.nn.sigmoid(x)

def _layernorm(x, axis=-1, eps=1e-05):
    m = jnp.mean(x, axis=axis, keepdims=True)
    v = jnp.var(x, axis=axis, keepdims=True)
    return (x - m) / jnp.sqrt(v + eps)

def _scatter_add(tgt, idx, src, axis=0):
    return tgt.at[idx].add(src)

def _segment_sum(src, seg, n):
    return jax.ops.segment_sum(src, seg, n)
kernel_name = 'mk_cond_seq_d4_seqx_r8_7ae296'

def setup_inputs(seed: int=0):
    np.random.seed(seed)
    _w = jnp.asarray

    def _rec_inputs():
        import jax
        import jax.numpy as jnp
        _rk = jax.random.key(seed)
        x = 1.648e-05 + 1 * jax.random.normal(jax.random.fold_in(_rk, 1), (32, 128, 144), jnp.float32)
        _lenS = 128 - jax.random.randint(jax.random.fold_in(_rk, 7), (32,), 0, max(1, 128 // 4) + 1, jnp.int32)
        _lenS2 = 128 - jax.random.randint(jax.random.fold_in(_rk, 8), (32,), 0, max(1, 128 // 4) + 1, jnp.int32)
        cond_1152 = 0.00914911 + 1.00357 * jax.random.normal(jax.random.fold_in(_rk, 11), (32, 144), jnp.float32)
        return (x, cond_1152)
    x, cond_1152 = _rec_inputs()

    def _L0_cond_setup():
        import jax, jax.numpy as jnp
        import numpy as np
        DIM = 144
        HEADS = 16
        HEAD_DIM = DIM // HEADS
        HIDDEN = int(DIM * 4.0)
        EPS = 1e-12

        def rmsnorm(x, g, d):
            n = jnp.linalg.norm(x, axis=-1, keepdims=True)
            return x / jnp.maximum(n, EPS) * d ** 0.5 * g

        def modulate(x, scale, shift):
            return x * (1.0 + scale[:, None, :]) + shift[:, None, :]
        key = jax.random.key(seed)
        ks = jax.random.split(key, 12)
        B, N = (8, 128)
        s = 0.02
        return {'x': jax.random.normal(ks[0], (B, N, DIM), jnp.float32), 'c': jax.random.normal(ks[1], (B, DIM), jnp.float32), 'g1': jnp.ones((1,), jnp.float32), 'g2': jnp.ones((1,), jnp.float32), 'qkv_w': jax.random.normal(ks[2], (3 * DIM, DIM), jnp.float32) * s, 'qkv_b': jnp.zeros((3 * DIM,), jnp.float32), 'qg': jnp.ones((1,), jnp.float32), 'kg': jnp.ones((1,), jnp.float32), 'proj_w': jax.random.normal(ks[3], (DIM, DIM), jnp.float32) * s, 'proj_b': jnp.zeros((DIM,), jnp.float32), 'fc1_w': jax.random.normal(ks[4], (HIDDEN, DIM), jnp.float32) * s, 'fc1_b': jnp.zeros((HIDDEN,), jnp.float32), 'fc2_w': jax.random.normal(ks[5], (DIM, HIDDEN), jnp.float32) * s, 'fc2_b': jnp.zeros((DIM,), jnp.float32), 'ada_w': jax.random.normal(ks[6], (6 * DIM, DIM), jnp.float32) * s, 'ada_b': jnp.zeros((6 * DIM,), jnp.float32)}
    _L0_cond_all = _L0_cond_setup()
    _L0_cond_in = {k: v for k, v in _L0_cond_all.items() if k in ('g1', 'g2', 'qkv_w', 'qkv_b', 'qg', 'kg', 'proj_w', 'proj_b', 'fc1_w', 'fc1_b', 'fc2_w', 'fc2_b', 'ada_w', 'ada_b')}
    del _L0_cond_all

    def _L1_cond_setup():
        import jax, jax.numpy as jnp
        import numpy as np
        B, N, D = (8, 128, 144)
        H = 16
        HD = D // H
        HID = 4 * D
        EPS = 1e-06

        def _ln(x):
            mu = jnp.mean(x, axis=-1, keepdims=True)
            var = jnp.mean(jnp.square(x - mu), axis=-1, keepdims=True)
            return (x - mu) * jax.lax.rsqrt(var + EPS)

        def _modulate(x, shift, scale):
            return x * (1.0 + scale[:, None, :]) + shift[:, None, :]

        def _attn(x, w_qkv, b_qkv, w_proj, b_proj):
            b, n, d = x.shape
            qkv = (x @ w_qkv + b_qkv).reshape(b, n, 3, H, HD)
            q = qkv[:, :, 0].transpose(0, 2, 1, 3)
            k = qkv[:, :, 1].transpose(0, 2, 1, 3)
            v = qkv[:, :, 2].transpose(0, 2, 1, 3)
            scores = jnp.einsum('bhnd,bhmd->bhnm', q, k) * HD ** (-0.5)
            attn = jax.nn.softmax(scores, axis=-1)
            out = jnp.einsum('bhnm,bhmd->bhnd', attn, v)
            out = out.transpose(0, 2, 1, 3).reshape(b, n, d)
            return out @ w_proj + b_proj
        key = jax.random.key(seed)
        ks = jax.random.split(key, 12)
        s = 0.02
        return {'x': jax.random.normal(ks[0], (B, N, D), jnp.float32), 't_emb': jax.random.normal(ks[1], (B, D), jnp.float32), 'w_qkv': jax.random.normal(ks[2], (D, 3 * D), jnp.float32) * s, 'b_qkv': jax.random.normal(ks[3], (3 * D,), jnp.float32) * s, 'w_proj': jax.random.normal(ks[4], (D, D), jnp.float32) * s, 'b_proj': jax.random.normal(ks[5], (D,), jnp.float32) * s, 'w_fc1': jax.random.normal(ks[6], (D, HID), jnp.float32) * s, 'b_fc1': jax.random.normal(ks[7], (HID,), jnp.float32) * s, 'w_fc2': jax.random.normal(ks[8], (HID, D), jnp.float32) * s, 'b_fc2': jax.random.normal(ks[9], (D,), jnp.float32) * s, 'w_ada': jax.random.normal(ks[10], (D, 6 * D), jnp.float32) * s, 'b_ada': jax.random.normal(ks[11], (6 * D,), jnp.float32) * s}
    _L1_cond_all = _L1_cond_setup()
    _L1_cond_in = {k: v for k, v in _L1_cond_all.items() if k in ('w_qkv', 'b_qkv', 'w_proj', 'b_proj', 'w_fc1', 'b_fc1', 'w_fc2', 'b_fc2', 'w_ada', 'b_ada')}
    del _L1_cond_all

    def _L2_cond_setup():
        import math
        import jax, jax.numpy as jnp
        import numpy as np
        B, T, D = (8, 128, 144)
        H = 16
        E = 4
        EPS = 1e-06

        def _layer_norm(x):
            mu = jnp.mean(x, axis=-1, keepdims=True)
            var = jnp.mean(jnp.square(x - mu), axis=-1, keepdims=True)
            return (x - mu) * jax.lax.rsqrt(var + EPS)

        def _modulate(x, shift, scale):
            return x * (1.0 + scale) + shift

        def _attention(y, qkv_w, qkv_b, out_w, out_b):
            b, t, d = y.shape
            hd = d // H
            qkv = y @ qkv_w + qkv_b
            q, k, v = jnp.split(qkv, 3, axis=-1)
            q = q.reshape(b, t, H, hd).transpose(0, 2, 1, 3)
            k = k.reshape(b, t, H, hd).transpose(0, 2, 1, 3)
            v = v.reshape(b, t, H, hd).transpose(0, 2, 1, 3)
            scores = jnp.einsum('bhqd,bhkd->bhqk', q, k) / math.sqrt(hd)
            attn = jax.nn.softmax(scores, axis=-1)
            out = jnp.einsum('bhqk,bhkd->bhqd', attn, v)
            out = out.transpose(0, 2, 1, 3).reshape(b, t, d)
            return out @ out_w + out_b
        key = jax.random.key(seed)
        ks = jax.random.split(key, 12)
        std = 0.02
        return {'x': jax.random.normal(ks[0], (B, T, D), dtype=jnp.float32), 'c': jax.random.normal(ks[1], (B, D), dtype=jnp.float32), 'qkv_w': jax.random.normal(ks[2], (D, 3 * D), dtype=jnp.float32) * std, 'qkv_b': jnp.zeros((3 * D,), dtype=jnp.float32), 'out_w': jax.random.normal(ks[3], (D, D), dtype=jnp.float32) * std, 'out_b': jnp.zeros((D,), dtype=jnp.float32), 'w1': jax.random.normal(ks[4], (D, E * D), dtype=jnp.float32) * std, 'b1': jnp.zeros((E * D,), dtype=jnp.float32), 'w2': jax.random.normal(ks[5], (E * D, D), dtype=jnp.float32) * std, 'b2': jnp.zeros((D,), dtype=jnp.float32), 'ada_w': jax.random.normal(ks[6], (D, 6 * D), dtype=jnp.float32) * std, 'ada_b': jnp.zeros((6 * D,), dtype=jnp.float32)}
    _L2_cond_all = _L2_cond_setup()
    _L2_cond_in = {k: v for k, v in _L2_cond_all.items() if k in ('qkv_w', 'qkv_b', 'out_w', 'out_b', 'w1', 'b1', 'w2', 'b2', 'ada_w', 'ada_b')}
    del _L2_cond_all

    def _L3_cond_setup():
        import jax, jax.numpy as jnp
        import numpy as np
        N, T, D, H = (32, 128, 144, 16)
        DH = D // H
        MLP = int(D * 4.0)
        EPS = 1e-06

        def _layernorm(x):
            m = jnp.mean(x, axis=-1, keepdims=True)
            v = jnp.var(x, axis=-1, keepdims=True)
            return (x - m) * jax.lax.rsqrt(v + EPS)

        def _modulate(x, shift, scale):
            return x * (1.0 + scale[:, None, :]) + shift[:, None, :]

        def _attention(x, qkv_w, qkv_b, proj_w, proj_b):
            n, t, d = x.shape
            scale = DH ** (-0.5)
            qkv = x @ qkv_w + qkv_b
            qkv = qkv.reshape(n, t, 3, H, DH)
            q, k, v = (qkv[:, :, 0], qkv[:, :, 1], qkv[:, :, 2])
            attn = jnp.einsum('nthd,ntkd->nthk', q * scale, k)
            attn = jax.nn.softmax(attn, axis=-1)
            out = jnp.einsum('nthk,ntkd->nthd', attn, v)
            out = out.transpose(0, 2, 1, 3).reshape(n, t, d)
            return out @ proj_w + proj_b

        def _mlp(x, fc1_w, fc1_b, fc2_w, fc2_b):
            h = jax.nn.gelu(x @ fc1_w + fc1_b, approximate=False)
            return h @ fc2_w + fc2_b
        key = jax.random.key(seed)
        ks = jax.random.split(key, 14)
        s = 0.02
        return {'x': jax.random.normal(ks[0], (N, T, D), jnp.float32), 'c': jax.random.normal(ks[1], (N, D), jnp.float32), 'qkv_w': jax.random.normal(ks[2], (D, 3 * D), jnp.float32) * s, 'qkv_b': jax.random.normal(ks[3], (3 * D,), jnp.float32) * s, 'proj_w': jax.random.normal(ks[4], (D, D), jnp.float32) * s, 'proj_b': jax.random.normal(ks[5], (D,), jnp.float32) * s, 'fc1_w': jax.random.normal(ks[6], (D, MLP), jnp.float32) * s, 'fc1_b': jax.random.normal(ks[7], (MLP,), jnp.float32) * s, 'fc2_w': jax.random.normal(ks[8], (MLP, D), jnp.float32) * s, 'fc2_b': jax.random.normal(ks[9], (D,), jnp.float32) * s, 'ada_w': jax.random.normal(ks[10], (D, 6 * D), jnp.float32) * s, 'ada_b': jax.random.normal(ks[11], (6 * D,), jnp.float32) * s}
    _L3_cond_all = _L3_cond_setup()
    _L3_cond_in = {k: v for k, v in _L3_cond_all.items() if k in ('qkv_w', 'qkv_b', 'proj_w', 'proj_b', 'fc1_w', 'fc1_b', 'fc2_w', 'fc2_b', 'ada_w', 'ada_b')}
    del _L3_cond_all
    return {'x': x, 'cond_1152': cond_1152, 'L0_cond_g1': _L0_cond_in['g1'], 'L0_cond_g2': _L0_cond_in['g2'], 'L0_cond_qkv_w': _L0_cond_in['qkv_w'], 'L0_cond_qkv_b': _L0_cond_in['qkv_b'], 'L0_cond_qg': _L0_cond_in['qg'], 'L0_cond_kg': _L0_cond_in['kg'], 'L0_cond_proj_w': _L0_cond_in['proj_w'], 'L0_cond_proj_b': _L0_cond_in['proj_b'], 'L0_cond_fc1_w': _L0_cond_in['fc1_w'], 'L0_cond_fc1_b': _L0_cond_in['fc1_b'], 'L0_cond_fc2_w': _L0_cond_in['fc2_w'], 'L0_cond_fc2_b': _L0_cond_in['fc2_b'], 'L0_cond_ada_w': _L0_cond_in['ada_w'], 'L0_cond_ada_b': _L0_cond_in['ada_b'], 'L1_cond_w_qkv': _L1_cond_in['w_qkv'], 'L1_cond_b_qkv': _L1_cond_in['b_qkv'], 'L1_cond_w_proj': _L1_cond_in['w_proj'], 'L1_cond_b_proj': _L1_cond_in['b_proj'], 'L1_cond_w_fc1': _L1_cond_in['w_fc1'], 'L1_cond_b_fc1': _L1_cond_in['b_fc1'], 'L1_cond_w_fc2': _L1_cond_in['w_fc2'], 'L1_cond_b_fc2': _L1_cond_in['b_fc2'], 'L1_cond_w_ada': _L1_cond_in['w_ada'], 'L1_cond_b_ada': _L1_cond_in['b_ada'], 'L2_cond_qkv_w': _L2_cond_in['qkv_w'], 'L2_cond_qkv_b': _L2_cond_in['qkv_b'], 'L2_cond_out_w': _L2_cond_in['out_w'], 'L2_cond_out_b': _L2_cond_in['out_b'], 'L2_cond_w1': _L2_cond_in['w1'], 'L2_cond_b1': _L2_cond_in['b1'], 'L2_cond_w2': _L2_cond_in['w2'], 'L2_cond_b2': _L2_cond_in['b2'], 'L2_cond_ada_w': _L2_cond_in['ada_w'], 'L2_cond_ada_b': _L2_cond_in['ada_b'], 'L3_cond_qkv_w': _L3_cond_in['qkv_w'], 'L3_cond_qkv_b': _L3_cond_in['qkv_b'], 'L3_cond_proj_w': _L3_cond_in['proj_w'], 'L3_cond_proj_b': _L3_cond_in['proj_b'], 'L3_cond_fc1_w': _L3_cond_in['fc1_w'], 'L3_cond_fc1_b': _L3_cond_in['fc1_b'], 'L3_cond_fc2_w': _L3_cond_in['fc2_w'], 'L3_cond_fc2_b': _L3_cond_in['fc2_b'], 'L3_cond_ada_w': _L3_cond_in['ada_w'], 'L3_cond_ada_b': _L3_cond_in['ada_b']}

def reference(x, cond_1152, L0_cond_g1, L0_cond_g2, L0_cond_qkv_w, L0_cond_qkv_b, L0_cond_qg, L0_cond_kg, L0_cond_proj_w, L0_cond_proj_b, L0_cond_fc1_w, L0_cond_fc1_b, L0_cond_fc2_w, L0_cond_fc2_b, L0_cond_ada_w, L0_cond_ada_b, L1_cond_w_qkv, L1_cond_b_qkv, L1_cond_w_proj, L1_cond_b_proj, L1_cond_w_fc1, L1_cond_b_fc1, L1_cond_w_fc2, L1_cond_b_fc2, L1_cond_w_ada, L1_cond_b_ada, L2_cond_qkv_w, L2_cond_qkv_b, L2_cond_out_w, L2_cond_out_b, L2_cond_w1, L2_cond_b1, L2_cond_w2, L2_cond_b2, L2_cond_ada_w, L2_cond_ada_b, L3_cond_qkv_w, L3_cond_qkv_b, L3_cond_proj_w, L3_cond_proj_b, L3_cond_fc1_w, L3_cond_fc1_b, L3_cond_fc2_w, L3_cond_fc2_b, L3_cond_ada_w, L3_cond_ada_b):
    import jax
    import jax.numpy as jnp

    def _L0_cond_ref(x, c, g1, g2, qkv_w, qkv_b, qg, kg, proj_w, proj_b, fc1_w, fc1_b, fc2_w, fc2_b, ada_w, ada_b):
        import jax, jax.numpy as jnp
        import numpy as np
        DIM = 144
        HEADS = 16
        HEAD_DIM = DIM // HEADS
        HIDDEN = int(DIM * 4.0)
        EPS = 1e-12

        def rmsnorm(x, g, d):
            n = jnp.linalg.norm(x, axis=-1, keepdims=True)
            return x / jnp.maximum(n, EPS) * d ** 0.5 * g

        def modulate(x, scale, shift):
            return x * (1.0 + scale[:, None, :]) + shift[:, None, :]
        B, N, D = x.shape
        mod = jax.nn.silu(c) @ ada_w.T + ada_b
        shift_msa, scale_msa, gate_msa, shift_mlp, scale_mlp, gate_mlp = jnp.split(mod, 6, axis=-1)
        gate_msa = jnp.tanh(gate_msa)
        gate_mlp = jnp.tanh(gate_mlp)
        h = modulate(rmsnorm(x, g1, D), scale_msa, shift_msa)
        qkv = h @ qkv_w.T + qkv_b
        qkv = qkv.reshape(B, N, 3, HEADS, HEAD_DIM).transpose(2, 0, 3, 1, 4)
        q, k, v = (qkv[0], qkv[1], qkv[2])
        q = rmsnorm(q, qg, HEAD_DIM)
        k = rmsnorm(k, kg, HEAD_DIM)
        q = q * HEAD_DIM ** (-0.5)
        attn = jax.nn.softmax(jnp.einsum('bhqd,bhkd->bhqk', q, k), axis=-1)
        o = jnp.einsum('bhqk,bhkd->bhqd', attn, v)
        o = o.transpose(0, 2, 1, 3).reshape(B, N, D)
        o = o @ proj_w.T + proj_b
        x = x + gate_msa[:, None, :] * o
        h2 = modulate(rmsnorm(x, g2, D), scale_mlp, shift_mlp)
        m = jax.nn.gelu(h2 @ fc1_w.T + fc1_b, approximate=True) @ fc2_w.T + fc2_b
        x = x + gate_mlp[:, None, :] * m
        return x

    def _L1_cond_ref(x, t_emb, w_qkv, b_qkv, w_proj, b_proj, w_fc1, b_fc1, w_fc2, b_fc2, w_ada, b_ada):
        import jax, jax.numpy as jnp
        import numpy as np
        B, N, D = (8, 128, 144)
        H = 16
        HD = D // H
        HID = 4 * D
        EPS = 1e-06

        def _ln(x):
            mu = jnp.mean(x, axis=-1, keepdims=True)
            var = jnp.mean(jnp.square(x - mu), axis=-1, keepdims=True)
            return (x - mu) * jax.lax.rsqrt(var + EPS)

        def _modulate(x, shift, scale):
            return x * (1.0 + scale[:, None, :]) + shift[:, None, :]

        def _attn(x, w_qkv, b_qkv, w_proj, b_proj):
            b, n, d = x.shape
            qkv = (x @ w_qkv + b_qkv).reshape(b, n, 3, H, HD)
            q = qkv[:, :, 0].transpose(0, 2, 1, 3)
            k = qkv[:, :, 1].transpose(0, 2, 1, 3)
            v = qkv[:, :, 2].transpose(0, 2, 1, 3)
            scores = jnp.einsum('bhnd,bhmd->bhnm', q, k) * HD ** (-0.5)
            attn = jax.nn.softmax(scores, axis=-1)
            out = jnp.einsum('bhnm,bhmd->bhnd', attn, v)
            out = out.transpose(0, 2, 1, 3).reshape(b, n, d)
            return out @ w_proj + b_proj
        ada = jax.nn.silu(t_emb) @ w_ada + b_ada
        shift_a, scale_a, gate_a, shift_f, scale_f, gate_f = jnp.split(ada, 6, axis=-1)
        x = x + gate_a[:, None, :] * _attn(_modulate(_ln(x), shift_a, scale_a), w_qkv, b_qkv, w_proj, b_proj)
        h = _modulate(_ln(x), shift_f, scale_f)
        h = jax.nn.gelu(h @ w_fc1 + b_fc1, approximate=True) @ w_fc2 + b_fc2
        return x + gate_f[:, None, :] * h

    def _L2_cond_ref(x, c, qkv_w, qkv_b, out_w, out_b, w1, b1, w2, b2, ada_w, ada_b):
        import math
        import jax, jax.numpy as jnp
        import numpy as np
        B, T, D = (8, 128, 144)
        H = 16
        E = 4
        EPS = 1e-06

        def _layer_norm(x):
            mu = jnp.mean(x, axis=-1, keepdims=True)
            var = jnp.mean(jnp.square(x - mu), axis=-1, keepdims=True)
            return (x - mu) * jax.lax.rsqrt(var + EPS)

        def _modulate(x, shift, scale):
            return x * (1.0 + scale) + shift

        def _attention(y, qkv_w, qkv_b, out_w, out_b):
            b, t, d = y.shape
            hd = d // H
            qkv = y @ qkv_w + qkv_b
            q, k, v = jnp.split(qkv, 3, axis=-1)
            q = q.reshape(b, t, H, hd).transpose(0, 2, 1, 3)
            k = k.reshape(b, t, H, hd).transpose(0, 2, 1, 3)
            v = v.reshape(b, t, H, hd).transpose(0, 2, 1, 3)
            scores = jnp.einsum('bhqd,bhkd->bhqk', q, k) / math.sqrt(hd)
            attn = jax.nn.softmax(scores, axis=-1)
            out = jnp.einsum('bhqk,bhkd->bhqd', attn, v)
            out = out.transpose(0, 2, 1, 3).reshape(b, t, d)
            return out @ out_w + out_b
        mods = (jax.nn.silu(c) @ ada_w + ada_b)[:, None, :]
        m0, m1, m2, m3, m4, m5 = jnp.split(mods, 6, axis=-1)
        y = _modulate(_layer_norm(x), m0, m1)
        x = x + m2 * _attention(y, qkv_w, qkv_b, out_w, out_b)
        y = _modulate(_layer_norm(x), m3, m4)
        y = jax.nn.gelu(y @ w1 + b1, approximate=True)
        x = x + m5 * (y @ w2 + b2)
        return x

    def _L3_cond_ref(x, c, qkv_w, qkv_b, proj_w, proj_b, fc1_w, fc1_b, fc2_w, fc2_b, ada_w, ada_b):
        import jax, jax.numpy as jnp
        import numpy as np
        N, T, D, H = (32, 128, 144, 16)
        DH = D // H
        MLP = int(D * 4.0)
        EPS = 1e-06

        def _layernorm(x):
            m = jnp.mean(x, axis=-1, keepdims=True)
            v = jnp.var(x, axis=-1, keepdims=True)
            return (x - m) * jax.lax.rsqrt(v + EPS)

        def _modulate(x, shift, scale):
            return x * (1.0 + scale[:, None, :]) + shift[:, None, :]

        def _attention(x, qkv_w, qkv_b, proj_w, proj_b):
            n, t, d = x.shape
            scale = DH ** (-0.5)
            qkv = x @ qkv_w + qkv_b
            qkv = qkv.reshape(n, t, 3, H, DH)
            q, k, v = (qkv[:, :, 0], qkv[:, :, 1], qkv[:, :, 2])
            attn = jnp.einsum('nthd,ntkd->nthk', q * scale, k)
            attn = jax.nn.softmax(attn, axis=-1)
            out = jnp.einsum('nthk,ntkd->nthd', attn, v)
            out = out.transpose(0, 2, 1, 3).reshape(n, t, d)
            return out @ proj_w + proj_b

        def _mlp(x, fc1_w, fc1_b, fc2_w, fc2_b):
            h = jax.nn.gelu(x @ fc1_w + fc1_b, approximate=False)
            return h @ fc2_w + fc2_b
        ada = jax.nn.silu(c) @ ada_w + ada_b
        shift_msa, scale_msa, gate_msa, shift_mlp, scale_mlp, gate_mlp = jnp.split(ada, 6, axis=1)
        x = x + gate_msa[:, None, :] * _attention(_modulate(_layernorm(x), shift_msa, scale_msa), qkv_w, qkv_b, proj_w, proj_b)
        x = x + gate_mlp[:, None, :] * _mlp(_modulate(_layernorm(x), shift_mlp, scale_mlp), fc1_w, fc1_b, fc2_w, fc2_b)
        return x
    x = _L0_cond_ref(x, cond_1152, L0_cond_g1, L0_cond_g2, L0_cond_qkv_w, L0_cond_qkv_b, L0_cond_qg, L0_cond_kg, L0_cond_proj_w, L0_cond_proj_b, L0_cond_fc1_w, L0_cond_fc1_b, L0_cond_fc2_w, L0_cond_fc2_b, L0_cond_ada_w, L0_cond_ada_b)
    x = _L1_cond_ref(x, cond_1152, L1_cond_w_qkv, L1_cond_b_qkv, L1_cond_w_proj, L1_cond_b_proj, L1_cond_w_fc1, L1_cond_b_fc1, L1_cond_w_fc2, L1_cond_b_fc2, L1_cond_w_ada, L1_cond_b_ada)
    x = _L2_cond_ref(x, cond_1152, L2_cond_qkv_w, L2_cond_qkv_b, L2_cond_out_w, L2_cond_out_b, L2_cond_w1, L2_cond_b1, L2_cond_w2, L2_cond_b2, L2_cond_ada_w, L2_cond_ada_b)
    x = _L3_cond_ref(x, cond_1152, L3_cond_qkv_w, L3_cond_qkv_b, L3_cond_proj_w, L3_cond_proj_b, L3_cond_fc1_w, L3_cond_fc1_b, L3_cond_fc2_w, L3_cond_fc2_b, L3_cond_ada_w, L3_cond_ada_b)
    return x

_drawn_inputs = setup_inputs


def setup_inputs(seed=0):
    import zlib

    import numpy as np

    out = dict(_drawn_inputs(seed))
    spreads = {'L0_cond_qkv_b': (0.0, 0.8),
     'L0_cond_proj_b': (0.0, 0.458),
     'L0_cond_fc1_b': (0.0, 0.8),
     'L0_cond_fc2_b': (0.0, 0.489),
     'L0_cond_ada_b': (0.0, 0.52),
     'L2_cond_qkv_b': (0.0, 0.8),
     'L2_cond_out_b': (0.0, 0.45),
     'L2_cond_b1': (0.0, 0.8),
     'L2_cond_b2': (0.0, 0.45),
     'L2_cond_ada_b': (0.0, 0.471)}
    factors = {'L0_cond_qkv_w': 8.0,
     'L0_cond_proj_w': 8.0,
     'L0_cond_fc1_w': 5.243,
     'L0_cond_fc2_w': 5.001,
     'L1_cond_w_qkv': 8.0,
     'L1_cond_b_qkv': 8.0,
     'L1_cond_w_proj': 8.0,
     'L1_cond_b_proj': 8.0,
     'L1_cond_w_fc1': 6.633,
     'L1_cond_b_fc1': 8.0,
     'L1_cond_w_fc2': 6.529,
     'L1_cond_b_fc2': 8.0,
     'L1_cond_w_ada': 5.774,
     'L1_cond_b_ada': 8.0,
     'L2_cond_qkv_w': 8.0,
     'L2_cond_out_w': 8.0,
     'L2_cond_w1': 5.32,
     'L2_cond_w2': 4.87,
     'L3_cond_qkv_w': 8.0,
     'L3_cond_qkv_b': 8.0,
     'L3_cond_proj_w': 8.0,
     'L3_cond_proj_b': 32.849,
     'L3_cond_fc1_w': 6.633,
     'L3_cond_fc1_b': 8.0,
     'L3_cond_fc2_w': 6.527,
     'L3_cond_fc2_b': 40.697,
     'L3_cond_ada_w': 5.739,
     'L3_cond_ada_b': 8.0}
    for name, (base, spread) in spreads.items():
        noise = np.random.default_rng([zlib.crc32(name.encode()), seed]).standard_normal(out[name].shape)
        drawn = base * np.exp(spread * noise) if base else spread * noise
        out[name] = jnp.asarray(drawn.astype(out[name].dtype))
    for name, factor in factors.items():
        out[name] = (out[name] * factor).astype(out[name].dtype)
    return out
```

```python
from contextlib import ExitStack

import concourse.bass as bass
from concourse import mybir

F32 = mybir.dt.float32
BF16 = mybir.dt.bfloat16
ALU = mybir.AluOpType
ACT = mybir.ActivationFunctionType
AX_X = mybir.AxisListType.X

LAYERS = 4
KINDS = "aaat"
SEQS, TOK, DIM = 32, 128, 144
HEADS = 16
HD = DIM // HEADS
HIDDEN = 4 * DIM
REM = DIM - 128
GB = 4
GT = GB * TOK
GROUPS = SEQS // GB
QKM = 96
QKT = 2 * DIM // QKM
FCT = 5
FCM = [128, 128, 128, 128, 64]
Q_PARTS = (0, 0, 0, 1, 1, 2)
K_PARTS = (0, 1, 2, 0, 1, 0)
PARTS = len(Q_PARTS) * HD
STACK = PARTS + 2
CH = 4
CHUNKS = HEADS // CH
STEPS = GB * CHUNKS
AHEAD = 2 * CHUNKS
LAG = 2
PBUFS = 4

LIN_USES = {
    "mT1": (0, "mT_copied", 1), "mT2": (1, "mT_copied", 2), "mT3": (0, "mT_copied", 3),
    "OD0": (1, "oT_ready", 0), "OD1": (0, "oT_ready", 1),
    "T1_0": (1, "h1_ready_act", 3), "T1_1": (0, "h1_ready_dve", 3),
    "OD2": (1, "oT_ready", 2),
    "QK0": (0, "qk_taken", 0), "QK1": (1, "qk_taken", 1), "QK2": (0, "qk_taken", 2),
    "Q0": (0, "tok_ready", 0), "Q1": (1, "tok_ready", 1), "Q2": (0, "tok_ready", 2), "Q3": (1, "tok_ready", 3),
    "OD3": (1, "oT_ready", 3),
    "PJ0": (0, "proj_gated", 0), "PJ1": (1, "proj_gated", 1),
    "V0": (0, "v_ready", 0), "V1": (1, "v_ready", 1),
    "T2_0": (0, "h2_ready_act", 3), "T2_1": (1, "h2_ready_dve", 3),
    "F0": (0, "gelu_ready", 0), "F1": (1, "gelu_ready", 1), "F2": (0, "gelu_ready", 2),
    "F3": (1, "gelu_ready", 3), "F4": (0, "gelu_ready", 4),
    "M0": (1, "mlp_gated", 0), "mT0": (0, "mT_copied", 0), "M1": (1, "mlp_gated", 1),
}
LIN_BANK = {name: use[0] for name, use in LIN_USES.items()}
OF_NEXT = {"T1_0", "T1_1", "QK0", "QK1", "QK2", "Q0", "Q1", "Q2", "Q3", "V0", "V1", "mT0"}


def uses_of(this, nxt):
    first = {"a": ["mT1", "mT2", "mT3", "OD0", "OD1"], "t": ["OD0", "OD1"], None: []}[this]
    flips = ["T1_0", "T1_1"] if nxt else []
    heads = {"a": ["QK0", "QK1", "QK2"], "t": ["Q0", "Q1", "Q2", "Q3"], None: []}[nxt]
    vals = ["V0", "V1"] if nxt == "a" else []
    maxT = ["mT0"] if nxt == "a" else []
    if this is None:
        return flips + heads + vals + maxT
    return (first + flips + ["OD2"] + heads + ["OD3", "PJ0", "PJ1"] + vals + ["T2_0", "T2_1"]
            + [f"F{T}" for T in range(FCT)] + ["M0"] + maxT + ["M1"])


def use_before(use, this, nxt):
    order = uses_of(this, nxt)
    bank = LIN_BANK[use]
    same = [name for name in order[:order.index(use)] if LIN_BANK[name] == bank]
    if same:
        return same[-1], 0
    if this is None:
        return None, 0
    return [name for name in uses_of("a", this) if LIN_BANK[name] == bank][-1], 1


CONSTS = 4 + 1 + QKM // HEADS + 2 + 1 + 1

PER_GROUP = {
    "n1_stats": GB, "n1_aggr": GB, "n1_var": 3, "n1_rstd": 1, "n1_ready": GB,
    "n2_stats": GB, "n2_aggr": GB, "n2_var": 3, "n2_rstd": 1, "n2_ready": GB,
    "t1_done": 2, "t2_done": 2,
    "h1_ready_act": 4, "h1_ready_dve": 4, "h2_ready_act": 4, "h2_ready_dve": 4,
    "qk_done": QKT, "qk_taken": QKT, "qk_high": QKT, "qk_mid": QKT, "qk_low": QKT,
    "v_done": 2, "v_ready": 2,
    "score_done": STEPS, "max_done": STEPS, "max_high": GB, "max_low": GB,
    "mT_done": GB, "mT_copied": GB,
    "st_done": STEPS, "exp_done": STEPS, "pv_done": STEPS,
    "o_copied": GB, "o_tok_done": GB, "o_recip": GB, "o_normed": GB, "o_flip_done": GB, "oT_ready": GB,
    "proj_done": 2, "proj_gated": 2, "x_attn": 2,
    "fc1_done": FCT, "gelu_ready": FCT, "fc2_done": 2, "mlp_gated": 2, "x_mlp": 2,
    "mods1": 2, "mods2": 2,
    "tok_done": GB, "tok_ready": GB, "tok_prod": GB, "tok_scores": GB, "tok_max": GB, "tok_less": GB,
    "tok_exp": GB, "tok_sum": GB, "tok_recip": GB, "tok_weighted": GB, "tok_values": GB, "tok_normed": GB,
    "qk_rest": QKT, "qk_sq": QKT, "norm_done": 1, "norm_max": 1, "norm_ln": 1, "norm_exp": 1, "norm_y2": 1, "norm_t": 1,
    "norm_y": 1, "spread_done": QKT, "qk_scaled": QKT,
}
PER_GROUP_DMA = {"parts_stored": 3, "stack_loaded": 12, "m_loaded0": 2, "m_loaded1": 2, "m_loaded2": 2,
                 "m_loaded3": 2, "gates_loaded": 2,
                 "mixed_stored": 4, "mixed0": 1, "mixed1": 1, "mixed2": 1, "mixed3": 1}
TOKEN_ONLY = {name for name in [*PER_GROUP, *PER_GROUP_DMA] if name.startswith(("tok_", "mixed"))}
FIRST_TOKEN_GROUP = KINDS.index("t") * GROUPS


class Group:

    def __init__(self, base, reg=None):
        self.base, self.reg = base, reg

    def plus(self, n):
        return Group(self.base + n, self.reg)

    def times(self, n, more=0):
        whole = self.base * n + more
        return whole if self.reg is None else self.reg * n + whole

    @property
    def is_first(self):
        return self.reg is None and self.base == 0

    def in_layer(self, n):
        if self.reg is None:
            return (self.base % GROUPS) * n
        return self.reg * n + (self.base % GROUPS) * n


def blocks_kernel(nc, t, out):
    ctx = ExitStack()
    with ctx:
        def sb(name, shape, dt=F32):
            return ctx.enter_context(nc.sbuf_tensor(name, shape, dt))

        def ps(name):
            return ctx.enter_context(nc.psum_tensor(name, [128, 512], F32))

        x = sb("x", [128, SEQS, DIM])
        w_qk = [sb(f"w_qk{l}", [128, 2 * DIM]) for l in range(LAYERS)]
        w_qk_rem = [sb(f"w_qk_rem{l}", [REM + 1, 2 * DIM]) for l in range(LAYERS)]
        w_v = [sb(f"w_v{l}", [128, DIM]) for l in range(LAYERS)]
        w_v_rem = [sb(f"w_v_rem{l}", [REM + 1, DIM]) for l in range(LAYERS)]
        w_o = [sb(f"w_o{l}", [128, DIM]) for l in range(LAYERS)]
        w_o_rem = [sb(f"w_o_rem{l}", [REM + 1, DIM]) for l in range(LAYERS)]
        w_f1 = [sb(f"w_f1{l}", [128, HIDDEN]) for l in range(LAYERS)]
        w_f1_rem = [sb(f"w_f1_rem{l}", [REM + 1, HIDDEN]) for l in range(LAYERS)]
        w_f2 = [sb(f"w_f2{l}", [128, FCT, DIM]) for l in range(LAYERS)]
        mod_main = sb("mod_main", [128, LAYERS, 4, SEQS])
        mod_rem = sb("mod_rem", [REM, LAYERS, 4, SEQS])
        ident = sb("ident", [128, 128])
        ident_b = sb("ident_b", [128, 128], BF16)
        neg_half = sb("neg_half", [128, GB])

        stats = [sb(f"stats{i}", [128, GB, 6]) for i in range(2)]
        moments = [sb(f"moments{i}", [128, GB, 2]) for i in range(2)]
        mean_sq = sb("mean_sq", [128, 2, GB])
        var = [sb(f"var{i}", [128, GB]) for i in range(2)]
        rstd = [sb(f"rstd{i}", [128, GB]) for i in range(2)]
        normed = [sb(f"normed{i}", [128, GB, DIM]) for i in range(2)]
        mods = [sb(f"mods{i}", [128, 2, GB]) for i in range(2)]
        mods_rem = [sb(f"mods_rem{i}", [REM, 2, GB]) for i in range(2)]
        hT = [sb(f"hT{i}", [128, GT]) for i in range(2)]
        hT_rem = [sb(f"hT_rem{i}", [REM + 1, GT]) for i in range(2)]
        part_high = sb("part_high", [QKM, QKT, GT], BF16)
        part_mid = sb("part_mid", [QKM, QKT, GT], BF16)
        part_low = sb("part_low", [QKM, QKT, GT], BF16)
        qk_rest = sb("qk_rest", [QKM, QKT, GT])
        q_room = sb("q_room", [128, HEADS * GT // 2])
        k_room = sb("k_room", [128, HEADS * GT // 2])
        q_stack = q_room[0:64, :].bitcast(BF16).rearrange("p (h n) -> p h n", h=HEADS)
        k_stack = k_room[0:64, :].bitcast(BF16).rearrange("p (h n) -> p h n", h=HEADS)
        v_room = sb("v_room", [128, GB * HEADS * 32])
        v_aug = v_room[:, :].rearrange("p (b h r) -> p b h r", b=GB, h=HEADS)
        maxima = sb("maxima", [128, GB, HEADS])
        max_parts = sb("max_parts", [128, GB, 2, HEADS], BF16)
        max_T = sb("max_T", [2 * HEADS, GB, TOK], BF16)
        p_room = sb("p_room", [128, PBUFS * CH * TOK])
        probs = p_room[:, :].rearrange("p (i n) -> p i n", i=PBUFS)
        o_room = sb("o_room", [128, 2 * CHUNKS * TOK])
        o_feat = o_room[:, :].rearrange("p (i n) -> p i n", i=2)
        o_recip = sb("o_recip", [128, 2, HEADS])
        o_tok = sb("o_tok", [128, 2, DIM])
        oT = sb("oT", [128, GT])
        oT_rem = sb("oT_rem", [REM + 1, GT])
        gates = sb("gates", [128, 2, GB, DIM])
        gated = sb("gated", [128, 2, 2 * DIM])
        gelu = sb("gelu", [128, FCT, GT])

        pick = sb("pick", [QKM, QKT, 2 * HEADS])
        spread = sb("spread", [2 * HEADS, 2 * DIM])
        head_gain = sb("head_gain", [2 * HEADS, 1])
        raw_room = sb("raw_room", [128, 2 * QKT * GT])
        raw2 = raw_room[0:QKM, :].rearrange("p (i t n) -> p i t n", i=2, t=QKT)
        qk_raw, qk_sq = raw2[:, 0], raw2[:, 1]
        qk_fit = sb("qk_fit", [QKM, QKT, GT])
        norm2 = sb("norm2", [2 * HEADS, GT])
        norm_y = sb("norm_y_buf", [2 * HEADS, 2, GT])
        norm_t = sb("norm_t_buf", [2 * HEADS, 2, GT])

        MIX = HEADS * HEADS * HD
        tok_qkv = v_room[:, 0:GB * 3 * DIM].rearrange("p (b n) -> p b n", b=GB)
        tok_prod = q_room[:, 0:MIX]
        tok_weighted = [k_room[:, 0:MIX], raw_room[:, 0:MIX]]
        n0 = 2 * HEADS * HEADS
        tok_e = p_room[:, 0:n0].rearrange("p (i n) -> p i n", i=2)
        tok_less = p_room[:, n0:2 * n0].rearrange("p (i n) -> p i n", i=2)
        tok_o = p_room[:, 2 * n0:2 * n0 + 4 * DIM].rearrange("p (i n) -> p i n", i=4)
        n1 = 2 * n0 + 4 * DIM
        tok_small = p_room[:, n1:n1 + 6 * HEADS].rearrange("p (i n) -> p i n", i=6)
        mixed = o_room[:, 0:GB * DIM].rearrange("p (b n) -> p b n", b=GB)

        cT = sb("cT", [128, SEQS])
        cT_rem = sb("cT_rem", [REM + 1, SEQS])
        c_exp = sb("c_exp", [128, 2, SEQS])
        c_exp_rem = sb("c_exp_rem", [REM, 2, SEQS])
        silu = sb("silu", [128, SEQS])
        silu_rem = sb("silu_rem", [REM + 1, SEQS])
        flat = gelu[:, :, :].rearrange("p t n -> p (t n)")
        w_ada = flat[:, 0:6 * DIM]
        w_ada_rem = flat[0:REM + 1, 2 * GT:2 * GT + 6 * DIM]
        gain = sb("gain", [128, 2])
        gate_rows = sb("gate_rows", [SEQS, 2, DIM])

        score_bank = [ps(f"score_bank{i}") for i in range(2)]
        st_bank = [ps(f"st_bank{i}") for i in range(2)]
        o_bank = [ps(f"o_bank{i}") for i in range(2)]
        lin = [ps(f"lin{i}") for i in range(2)]
        lin_b = [lin[i][:, :].bitcast(BF16) for i in range(2)]

        parts_dram = nc.dram_tensor("parts_dram", [3, 2 * DIM, GT], BF16, kind="Internal").ap()
        gates_dram = nc.dram_tensor("gates_dram", [LAYERS, 2, SEQS, DIM], F32, kind="Internal").ap()

        mix_dram = nc.dram_tensor("mix_dram", [GB, HEADS, TOK, HD], F32, kind="Internal").ap()

        S = {name: ctx.enter_context(nc.semaphore(name)) for name in [*PER_GROUP, *PER_GROUP_DMA]}
        setup = {name: ctx.enter_context(nc.semaphore("set_" + name)) for name in (
            "x", "weights", "c", "ada", "gain", "const", "ones", "c_exp", "silu", "mods_done", "mods_kept",
            "gates_kept", "tanh", "gates_stored", "picks", "carrier", "out")}
        block = ctx.enter_context(nc.Block())

        def need(eng, name, group, k, ago=0):
            unit = 1 if name in PER_GROUP else 16
            if name in TOKEN_ONLY:
                group = group.plus(-FIRST_TOKEN_GROUP)
            n = PER_GROUP[name] if name in PER_GROUP else PER_GROUP_DMA[name]
            value = group.times(unit * n, unit * (n * (1 - ago) + k + 1))
            if group.reg is None and value <= 0:
                return
            eng.wait_ge(S[name], value)

        def start_with(eng, names):
            for name in names:
                eng.sem_inc(S[name], PER_GROUP[name] if name in PER_GROUP else 16 * PER_GROUP_DMA[name])

        def layers(eng, body):
            for l in range(LAYERS):
                with eng.Fori(0, GROUPS - 1) as g:
                    body(Group(l * GROUPS, g), l, l)
                body(Group(l * GROUPS + GROUPS - 1), l, l + 1 if l + 1 < LAYERS else None)

        def h_read_by(i, kinds):
            if i == 1:
                return "fc1_done", FCT - 1
            return ("v_done", 1) if kinds[0] == "a" else ("tok_done", GB - 1)

        @block.sync
        def _(eng):
            start_with(eng, PER_GROUP_DMA)
            eng.dma_start(cT[:, :], t["cT"][0:128, :]).then_inc(setup["c"], 16)
            eng.dma_start(cT_rem[0:REM, :], t["cT"][128:DIM, :]).then_inc(setup["c"], 16)
            for i, name in enumerate(("g1", "g2")):
                eng.dma_start(gain[:, i:i + 1], t[name].partition_broadcast(128)).then_inc(setup["gain"], 16)
            for i, name in enumerate(("qg", "kg")):
                eng.dma_start(head_gain[i * HEADS:(i + 1) * HEADS, :], t[name].partition_broadcast(HEADS))\
                   .then_inc(setup["gain"], 16)
            for l in range(LAYERS):
                if l:
                    eng.wait_ge(setup["mods_done"], l)
                eng.dma_start(w_ada[:, :], t[f"ada_w{l}"][0:128, :]).then_inc(setup["ada"], 16)
                eng.dma_start(w_ada_rem[0:REM, :], t[f"ada_w{l}"][128:DIM, :]).then_inc(setup["ada"], 16)
                eng.dma_start(w_ada_rem[REM:REM + 1, :], t[f"ada_b{l}"].rearrange("(o n) -> o n", o=1))\
                   .then_inc(setup["ada"], 16)
                eng.wait_ge(setup["gates_kept"], l + 1)
                eng.dma_start(gates_dram[l].rearrange("w b n -> b w n"), gate_rows[:, :, :])\
                   .then_inc(setup["gates_stored"], 16)
            eng.wait_ge(setup["gates_stored"], 16 * LAYERS)

            def load_gates(J, l):
                for w in range(2):
                    src = gates_dram[l, w].rearrange("b n -> (b n)")[bass.ds(J.in_layer(GB * DIM), GB * DIM)]
                    eng.dma_start(gates[:, w, :, :].rearrange("p b n -> p (b n)"), src.partition_broadcast(128))\
                       .then_inc(S["gates_loaded"], 16)

            def load_stack(J):
                for i, (part, ready) in enumerate(((part_high, "qk_high"), (part_mid, "qk_mid"),
                                                   (part_low, "qk_low"))):
                    need(eng, ready, J, QKT - 1)
                    if i == 0:
                        need(eng, "stack_loaded", J, 11, ago=1)
                    eng.dma_start(parts_dram[i].rearrange("(t p) n -> p t n", p=QKM), part[:, :, :])\
                       .then_inc(S["parts_stored"], 16)
                need(eng, "parts_stored", J, 2)
                need(eng, "st_done", J, STEPS - 1, ago=1)
                rows = parts_dram.rearrange("i (s d h) n -> i s d (h n)", s=2, d=HD)
                for s, (dst, order) in enumerate(((q_stack, Q_PARTS), (k_stack, K_PARTS))):
                    for r, i in enumerate(order):
                        eng.dma_start(dst[r * HD:(r + 1) * HD, :, :].rearrange("p h n -> p (h n)"), rows[i, s])\
                           .then_inc(S["stack_loaded"], 16)

            def mix(J, b):
                need(eng, "o_flip_done", J, b, ago=1)
                eng.sem_inc(setup["carrier"], 1)
                need(eng, "tok_normed", J, b)
                if b == 0:
                    for i in range(GB):
                        need(eng, f"mixed{i}", J, 0, ago=1)
                eng.dma_start(mix_dram[b].rearrange("h t d -> t h d"),
                              tok_o[:, 2 + b % 2, :].rearrange("p (h d) -> p h d", d=HD))\
                   .then_inc(S["mixed_stored"], 16)
                need(eng, "mixed_stored", J, b)
                eng.dma_start(mixed[:, b, :], mix_dram[b].rearrange("h t d -> (h t d)")
                              .rearrange("(r c) -> r c", c=DIM)).then_inc(S[f"mixed{b}"], 16)

            def load_max(J, b):
                need(eng, "mT_copied", J, b)
                for i in range(2):
                    eng.dma_start(q_stack[PARTS + i:PARTS + i + 1, :, b * TOK:(b + 1) * TOK],
                                  max_T[i * HEADS:(i + 1) * HEADS, b, :]).then_inc(S[f"m_loaded{b}"], 16)

            first = Group(0)
            load_gates(first, 0)
            load_stack(first)
            load_max(first, 0)

            def body(G, l, nxt):
                if KINDS[l] == "a":
                    for b in range(1, GB):
                        load_max(G, b)
                else:
                    for b in range(GB):
                        mix(G, b)
                if nxt is not None and KINDS[nxt] == "a":
                    load_stack(G.plus(1))
                need(eng, "x_mlp", G, 1)
                eng.sem_inc(setup["carrier"], 1)
                if l == LAYERS - 1:
                    at = G.in_layer(GB)
                    eng.dma_start(out[bass.ds(at, GB)].rearrange("b t d -> t b d"), x[:, bass.ds(at, GB), :])\
                       .then_inc(setup["out"], 16)
                if nxt is not None:
                    load_gates(G.plus(1), nxt)
                    if KINDS[nxt] == "a":
                        load_max(G.plus(1), 0)

            layers(eng, body)
            eng.wait_ge(setup["out"], 16 * GROUPS)

        @block.gpsimd
        def _(eng):
            start_with(eng, ("qk_low", "tok_weighted", "n1_rstd", "n2_rstd", "mods1", "mods2"))
            eng.memset(ident[:, :], 0.0).then_inc(setup["const"], 1)
            eng.memset(pick[:, :, :], 0.0).then_inc(setup["const"], 1)
            eng.memset(spread[:, :], 0.0).then_inc(setup["const"], 1)
            eng.memset(neg_half[:, :], -0.5).then_inc(setup["const"], 1)
            eng.wait_ge(setup["const"], 4)
            eng.affine_select(out=ident[:, :], in_=ident[:, :], compare_op=ALU.not_equal, fill=1.0,
                              base=0, pattern=[[-1, 128]], channel_multiplier=1).then_inc(setup["const"], 1)
            heads = pick[:, :, :].rearrange("p t (s h) -> p t s h", s=2)
            for a in range(QKM // HEADS):
                eng.affine_select(out=heads, in_=heads, compare_op=ALU.not_equal, fill=1.0, base=-a * HEADS,
                                  pattern=[[0, QKT], [0, 2], [-1, HEADS]], channel_multiplier=1)\
                   .then_inc(setup["const"], 1)
                eng.wait_ge(setup["const"], 6 + a)
            eng.affine_select(out=heads[:, :, 0, :], in_=heads[:, :, 0, :], compare_op=ALU.is_ge, fill=0.0,
                              base=DIM - 1, pattern=[[-QKM, QKT], [0, HEADS]], channel_multiplier=-1)\
               .then_inc(setup["const"], 1)
            eng.affine_select(out=heads[:, :, 1, :], in_=heads[:, :, 1, :], compare_op=ALU.is_ge, fill=0.0,
                              base=-DIM, pattern=[[QKM, QKT], [0, HEADS]], channel_multiplier=1)\
               .then_inc(setup["const"], 1)
            rows = spread[:, :].rearrange("m (s d h) -> m s d h", s=2, d=HD)
            eng.affine_select(out=rows, in_=rows, compare_op=ALU.not_equal, fill=1.0, base=0,
                              pattern=[[-HEADS, 2], [0, HD], [-1, HEADS]], channel_multiplier=1)\
               .then_inc(setup["const"], 1)
            eng.tensor_copy(ident_b[:, :], ident[:, :]).then_inc(setup["const"], 1)

            def mods_of(J, l, i):
                need(eng, ("h1_ready_act", "h2_ready_act")[i], J, 3, ago=1)
                need(eng, ("h1_ready_dve", "h2_ready_dve")[i], J, 3, ago=1)
                at = J.in_layer(GB)
                name = ("mods1", "mods2")[i]
                eng.tensor_copy(mods[i][:, :, :], mod_main[:, l, 2 * i:2 * i + 2, bass.ds(at, GB)])\
                   .then_inc(S[name], 1)
                eng.tensor_copy(mods_rem[i][:, :, :], mod_rem[:, l, 2 * i:2 * i + 2, bass.ds(at, GB)])\
                   .then_inc(S[name], 1)

            def rstd_of(J, i):
                need(eng, ("n1_var", "n2_var")[i], J, 2)
                need(eng, ("n1_ready", "n2_ready")[i], J, GB - 1, ago=1)
                eng.tensor_tensor(rstd[i][:, :], var[i][:, :], neg_half[:, :], ALU.pow)\
                   .then_inc(S[("n1_rstd", "n2_rstd")[i]], 1)

            def lows(J):
                for T in range(QKT):
                    need(eng, "qk_mid", J, T)
                    if T == 0:
                        need(eng, "parts_stored", J, 2, ago=1)
                    eng.tensor_tensor(part_low[:, T, :], qk_rest[:, T, :], part_mid[:, T, :], ALU.subtract)\
                       .then_inc(S["qk_low"], 1)

            def weight(J, b):
                need(eng, "tok_exp", J, b)
                if b >= 2:
                    need(eng, "tok_values", J, b - 2)
                else:
                    need(eng, "tok_values", J, b + 2, ago=1)
                shape = [128, HEADS, HD, HEADS]
                e = tok_e[:, b % 2, :].rearrange("p (h o k) -> p h o k", h=HEADS, o=1).broadcast_to(shape)
                v = tok_qkv[:, b, 2 * DIM:3 * DIM].rearrange("p (o k d) -> p o d k", o=1, d=HD).broadcast_to(shape)
                eng.tensor_tensor(tok_weighted[b % 2].rearrange("p (h d k) -> p h d k", h=HEADS, d=HD), e, v,
                                  ALU.mult).then_inc(S["tok_weighted"], 1)

            eng.wait_ge(setup["mods_kept"], 2 * LAYERS)
            eng.wait_ge(setup["const"], CONSTS)
            eng.wait_ge(setup["ones"], 6)
            first = Group(0)
            mods_of(first, 0, 0)
            rstd_of(first, 0)
            lows(first)

            def body(G, l, nxt):
                if KINDS[l] == "t":
                    weight(G, 0)
                    weight(G, 1)
                if nxt is not None:
                    mods_of(G.plus(1), nxt, 0)
                    rstd_of(G.plus(1), 0)
                if KINDS[l] == "t":
                    weight(G, 2)
                    weight(G, 3)
                mods_of(G, l, 1)
                if nxt is not None and KINDS[nxt] == "a":
                    lows(G.plus(1))
                rstd_of(G, 1)

            layers(eng, body)

        @block.scalar
        def _(eng):
            start_with(eng, ("h1_ready_act", "h2_ready_act", "qk_high", "v_ready", "mT_copied", "exp_done",
                             "o_copied", "oT_ready", "gelu_ready", "tok_ready", "tok_exp", "qk_sq", "norm_ln", "norm_exp"))
            for h in range(4):
                n = SEQS // 4
                eng.dma_start(x[:, h * n:(h + 1) * n, :], t["x"][h * n:(h + 1) * n].rearrange("b t d -> t b d"))\
                   .then_inc(setup["x"], 16)
            for l in range(LAYERS):
                def load(dst, src):
                    eng.dma_start(dst, src).then_inc(setup["weights"], 16)

                def row(a):
                    return a.rearrange("(o n) -> o n", o=1)

                load(w_qk[l][:, :], t[f"qk_w{l}"][0:128, :])
                load(w_qk_rem[l][0:REM, :], t[f"qk_w{l}"][128:DIM, :])
                load(w_qk_rem[l][REM:REM + 1, :], row(t[f"qk_b{l}"]))
                load(w_v[l][:, :], t[f"v_w{l}"][0:128, :])
                load(w_v_rem[l][0:REM, :], t[f"v_w{l}"][128:DIM, :])
                load(w_v_rem[l][REM:REM + 1, :], row(t[f"v_b{l}"]))
                load(w_o[l][:, :], t[f"o_w{l}"][0:128, :])
                load(w_o_rem[l][0:REM, :], t[f"o_w{l}"][128:DIM, :])
                load(w_o_rem[l][REM:REM + 1, :], row(t[f"o_b{l}"]))
                load(w_f1[l][:, :], t[f"f1_w{l}"][0:128, :])
                load(w_f1_rem[l][0:REM, :], t[f"f1_w{l}"][128:DIM, :])
                load(w_f1_rem[l][REM:REM + 1, :], row(t[f"f1_b{l}"]))
                load(w_f2[l][:, 0:4, :], t[f"f2_w{l}"][0:512, :].rearrange("(t p) n -> p t n", p=128))
                load(w_f2[l][0:64, 4, :], t[f"f2_w{l}"][512:HIDDEN, :])
                load(w_f2[l][64:65, 4, :], row(t[f"f2_b{l}"]))
            eng.wait_ge(setup["c"], 32)
            eng.activation(c_exp[:, 0, :], cT[:, :], ACT.Exp, scale=-1.0).then_inc(setup["c_exp"], 1)
            eng.activation(c_exp_rem[:, 0, :], cT_rem[0:REM, :], ACT.Exp, scale=-1.0)\
               .then_inc(setup["c_exp"], 1)
            eng.wait_ge(setup["mods_done"], 1)
            eng.activation(gate_rows[:, :, :].rearrange("b w n -> b (w n)"), lin[1][0:SEQS, 0:2 * DIM], ACT.Tanh)\
               .then_inc(setup["gates_kept"], 1)
            for l in range(1, LAYERS):
                eng.wait_ge(setup["mods_done"], l + 1)
                eng.wait_ge(setup["gates_stored"], 16 * l)
                eng.activation(gate_rows[:, :, :].rearrange("b w n -> b (w n)"), lin[1][0:SEQS, 0:2 * DIM],
                               ACT.Copy).then_inc(setup["gates_kept"], 1)

            def modulated(J, i, kinds="aa"):
                need(eng, ("mods1", "mods2")[i], J, 1)
                need(eng, ("t1_done", "t2_done")[i], J, 0)
                name, k = h_read_by(i, kinds)
                need(eng, name, J, k, ago=1)
                bank = lin[LIN_BANK[("T1_0", "T2_0")[i]]]
                for b in range(2):
                    c = b * 256
                    eng.activation(hT[i][:, b * TOK:(b + 1) * TOK], bank[:, c:c + TOK], ACT.Identity,
                                   bias=mods[i][:, 0, b:b + 1], scale=mods[i][:, 1, b:b + 1])\
                       .then_inc(S[("h1_ready_act", "h2_ready_act")[i]], 1)
                    eng.activation(hT_rem[i][0:REM, b * TOK:(b + 1) * TOK], bank[0:REM, c + TOK:c + 2 * TOK],
                                   ACT.Identity, bias=mods_rem[i][:, 0, b:b + 1],
                                   scale=mods_rem[i][:, 1, b:b + 1])\
                       .then_inc(S[("h1_ready_act", "h2_ready_act")[i]], 1)

            def highs(J, l):
                if l == 0:
                    for T in range(QKT):
                        need(eng, "qk_taken", J, T)
                        eng.activation(qk_sq[:, T, :], qk_raw[:, T, :], ACT.Square).then_inc(S["qk_sq"], 1)
                    need(eng, "norm_max", J, 0)
                    eng.activation(norm_t[:, 0, :], norm2[:, :], ACT.Ln).then_inc(S["norm_ln"], 1)
                    need(eng, "norm_ln", J, 0)
                    eng.activation(norm_y[:, 0, :], norm_t[:, 0, :], ACT.Exp, scale=-0.5)\
                       .then_inc(S["norm_exp"], 1)
                for T in range(QKT):
                    if T == 0:
                        need(eng, "parts_stored", J, 2, ago=1)
                    if l == 0:
                        need(eng, "qk_scaled", J, T)
                        src = qk_fit[:, T, :]
                    else:
                        need(eng, "qk_done", J, T)
                        src = lin[LIN_BANK[f"QK{T}"]][0:QKM, :]
                    eng.activation(part_high[:, T, :], src, ACT.Copy).then_inc(S["qk_high"], 1)

            def values(J):
                for h in range(2):
                    need(eng, "v_done", J, h)
                    if h == 0:
                        need(eng, "pv_done", J, STEPS - 1, ago=1)
                    bank = lin[LIN_BANK[f"V{h}"]]
                    eng.activation(v_aug[:, 2 * h:2 * h + 2, :, 0:HD],
                                   bank[:, 0:2 * DIM].rearrange("p (b h d) -> p b h d", b=2, d=HD), ACT.Copy)\
                       .then_inc(S["v_ready"], 1)

            def copy_max(J, b):
                need(eng, "mT_done", J, b)
                need(eng, f"m_loaded{b}", J, 1, ago=1)
                eng.activation(max_T[:, b, :], lin_b[LIN_BANK[f"mT{b}"]][0:2 * HEADS, 0:TOK], ACT.Copy)\
                   .then_inc(S["mT_copied"], 1)

            def copy_o(G, b):
                need(eng, "pv_done", G, (b + 1) * CHUNKS - 1)
                if b >= 2:
                    need(eng, "o_tok_done", G, b - 2)
                else:
                    need(eng, "o_tok_done", G, b + 2, ago=1)
                eng.activation(o_feat[:, b % 2, :], o_bank[b % 2][:, :], ACT.Copy).then_inc(S["o_copied"], 1)

            def copy_oT(G, b):
                need(eng, "o_flip_done", G, b)
                if b == 0:
                    need(eng, "proj_done", G, 1, ago=1)
                bank = lin[LIN_BANK[f"OD{b}"]]
                eng.activation(oT_rem[0:REM, b * TOK:(b + 1) * TOK], bank[0:REM, TOK:2 * TOK], ACT.Copy)
                eng.activation(oT[:, b * TOK:(b + 1) * TOK], bank[:, 0:TOK], ACT.Copy).then_inc(S["oT_ready"], 1)

            def token_qkv(J, b):
                need(eng, "tok_done", J, b)
                need(eng, "tok_weighted", J, b, ago=1)
                eng.activation(tok_qkv[:, b, :], lin[LIN_BANK[f"Q{b}"]][:, 0:3 * DIM], ACT.Copy)\
                   .then_inc(S["tok_ready"], 1)

            def token_exp(J, b):
                need(eng, "tok_less", J, b)
                eng.activation(tok_e[:, b % 2, :], tok_less[:, b % 2, :], ACT.Exp, scale=float(HD) ** -0.5)\
                   .then_inc(S["tok_exp"], 1)

            eng.wait_ge(setup["ones"], 6)
            eng.wait_ge(setup["const"], CONSTS)
            first = Group(0)
            modulated(first, 0)
            highs(first, 0)
            values(first)
            copy_max(first, 0)

            def exponentials(G):
                for i in range(STEPS):
                    need(eng, "st_done", G, i)
                    if i >= PBUFS:
                        need(eng, "pv_done", G, i - PBUFS)
                    else:
                        need(eng, "pv_done", G, i - PBUFS + STEPS, ago=1)
                    eng.activation(probs[:, i % PBUFS, :], st_bank[i % 2][:, :], ACT.Exp, scale=float(HD) ** -0.5)\
                       .then_inc(S["exp_done"], 1)
                    if i in (2, 6, 10):
                        copy_max(G, i // 4 + 1)
                    if i >= 6 and i % 4 == 2:
                        copy_o(G, (i - 6) // 4)
                    if i >= 10 and i % 4 == 2:
                        copy_oT(G, (i - 10) // 4)
                copy_o(G, 3)

            def body(G, l, nxt):
                if KINDS[l] == "a":
                    exponentials(G)
                else:
                    token_exp(G, 2)
                    token_exp(G, 3)
                    copy_oT(G, 0)
                    copy_oT(G, 1)
                kinds = KINDS[l] + (KINDS[nxt] if nxt is not None else "-")
                if nxt is not None:
                    modulated(G.plus(1), 0, kinds)
                copy_oT(G, 2)
                if kinds[1] == "a":
                    highs(G.plus(1), nxt)
                elif kinds[1] == "t":
                    for b in range(GB):
                        token_qkv(G.plus(1), b)
                copy_oT(G, 3)
                if kinds[1] == "a":
                    values(G.plus(1))
                modulated(G, 1)
                for T in range(FCT):
                    need(eng, "fc1_done", G, T)
                    if T == 0:
                        need(eng, "fc2_done", G, 1, ago=1)
                    m = FCM[T]
                    eng.activation(gelu[0:m, T, :], lin[LIN_BANK[f"F{T}"]][0:m, :],
                                   ACT.Gelu if l == LAYERS - 1 else ACT.Gelu_apprx_tanh)\
                       .then_inc(S["gelu_ready"], 1)
                if kinds[1] == "a":
                    copy_max(G.plus(1), 0)
                elif kinds[1] == "t":
                    token_exp(G.plus(1), 0)
                    token_exp(G.plus(1), 1)

            layers(eng, body)

        @block.vector
        def _(eng):
            start_with(eng, ("n1_stats", "n1_aggr", "n1_var", "n1_ready", "n2_stats", "n2_aggr", "n2_var",
                             "n2_ready", "h1_ready_dve", "h2_ready_dve", "qk_taken", "qk_mid", "max_done",
                             "max_high", "max_low", "o_recip", "o_normed", "proj_gated", "x_attn",
                             "mlp_gated", "x_mlp", "tok_prod", "tok_scores", "tok_max", "tok_less", "tok_sum",
                             "tok_recip", "tok_values", "tok_normed", "qk_rest", "norm_max", "norm_y2", "norm_t", "norm_y", "qk_scaled"))
            for buf in (hT_rem[0], hT_rem[1], oT_rem):
                eng.memset(buf[:, :], 1.0).then_inc(setup["ones"], 1)
            eng.memset(gelu[64:128, FCT - 1, :], 1.0).then_inc(setup["ones"], 1)
            eng.memset(v_aug[:, :, :, :], 1.0).then_inc(setup["ones"], 1)
            eng.memset(k_stack[32:64, :, :], -1.0).then_inc(setup["ones"], 1)
            eng.wait_ge(setup["c_exp"], 2)
            eng.tensor_scalar(c_exp[:, 1, :], c_exp[:, 0, :], 1.0, None, ALU.add).then_inc(setup["silu"], 1)
            eng.tensor_scalar(c_exp_rem[:, 1, :], c_exp_rem[:, 0, :], 1.0, None, ALU.add).then_inc(setup["silu"], 1)
            eng.memset(silu_rem[:, :], 1.0).then_inc(setup["silu"], 1)
            eng.wait_ge(setup["silu"], 3)
            eng.reciprocal(c_exp[:, 0, :], c_exp[:, 1, :]).then_inc(setup["silu"], 1)
            eng.reciprocal(c_exp_rem[:, 0, :], c_exp_rem[:, 1, :]).then_inc(setup["silu"], 1)
            eng.wait_ge(setup["silu"], 5)
            eng.tensor_tensor(silu[:, :], cT[:, :], c_exp[:, 0, :], ALU.mult).then_inc(setup["silu"], 1)
            eng.tensor_tensor(silu_rem[0:REM, :], cT_rem[0:REM, :], c_exp_rem[:, 0, :], ALU.mult)\
               .then_inc(setup["silu"], 1)
            eng.wait_ge(setup["gain"], 64)
            eng.wait_ge(setup["const"], CONSTS)
            eng.tensor_scalar(gain[:, :], gain[:, :], float(DIM) ** 0.5, None, ALU.mult).then_inc(setup["picks"], 1)
            eng.tensor_scalar(spread[:, :], spread[:, :], head_gain[:, 0:1], float(HD) ** 0.5, ALU.mult, ALU.mult)\
               .then_inc(setup["picks"], 1)
            eng.wait_ge(setup["picks"], 2)
            for l in range(LAYERS):
                eng.wait_ge(setup["mods_done"], l + 1)
                for main, n, bank in ((mod_main, 128, lin[0][:, 0:128]), (mod_rem, REM, lin[0][0:REM, 128:256])):
                    v = bank.rearrange("p (i w b) -> p i w b", i=2, w=2)
                    d = main[:, l, :, :].rearrange("p (i w) b -> p i w b", w=2)
                    eng.tensor_copy(d[:, :, 0, :], v[:, :, 0, :])
                    if l:
                        ins = eng.tensor_scalar(d[:, :, 1, :], v[:, :, 1, :], 1.0, None, ALU.add)
                    else:
                        eng.tensor_scalar(d[:, 0, 1, :], v[:, 0, 1, :], 1.0, gain[0:n, 0:1], ALU.add, ALU.mult)
                        ins = eng.tensor_scalar(d[:, 1, 1, :], v[:, 1, 1, :], 1.0, gain[0:n, 1:2], ALU.add, ALU.mult)
                    ins.then_inc(setup["mods_kept"], 1)
            eng.wait_ge(setup["mods_kept"], 2 * LAYERS)

            def stand_alone(eng):
                eng.sem_inc(setup["carrier"], 1)

            def statistics(J, l, i):
                pre = ("n1", "n2")[i]
                if i == 0:
                    need(eng, "x_mlp", J, 1, ago=2)
                else:
                    need(eng, "x_attn", J, 1)
                need(eng, pre + "_ready", J, GB - 1, ago=1)
                stand_alone(eng)
                for b in range(GB):
                    eng.bn_stats(stats[i][:, b, :], x[:, bass.ds(J.in_layer(GB) + b, 1), :].rearrange("p o d -> p (o d)"))\
                       .then_inc(S[pre + "_stats"], 1)
                need(eng, pre + "_stats", J, GB - 1)
                stand_alone(eng)
                for b in range(GB):
                    eng.bn_aggr(moments[i][:, b, :], stats[i][:, b, :]).then_inc(S[pre + "_aggr"], 1)
                need(eng, pre + "_aggr", J, GB - 1)
                if l == 0:
                    eng.tensor_tensor(mean_sq[:, 0, :], moments[i][:, :, 0], moments[i][:, :, 0], ALU.mult)\
                       .then_inc(S[pre + "_var"], 1)
                    need(eng, pre + "_var", J, 0)
                    eng.tensor_tensor(mean_sq[:, 1, :], mean_sq[:, 0, :], moments[i][:, :, 1], ALU.add)\
                       .then_inc(S[pre + "_var"], 1)
                    need(eng, pre + "_var", J, 1)
                    eng.tensor_scalar(var[i][:, :], mean_sq[:, 1, :], float(DIM), 1e-24, ALU.mult, ALU.max)\
                       .then_inc(S[pre + "_var"], 1)
                else:
                    eng.tensor_scalar(var[i][:, :], moments[i][:, :, 1], 1e-6, None, ALU.add)\
                       .then_inc(S[pre + "_var"], 3)

            def normalise(J, l, i):
                pre = ("n1", "n2")[i]
                need(eng, pre + "_rstd", J, 0)
                need(eng, ("t1_done", "t2_done")[i], J, 1, ago=1)
                for b in range(GB):
                    src = x[:, bass.ds(J.in_layer(GB) + b, 1), :].rearrange("p o d -> p (o d)")
                    if l == 0:
                        ins = eng.tensor_scalar(normed[i][:, b, :], src, rstd[i][:, b:b + 1], None, ALU.mult)
                    else:
                        ins = eng.tensor_scalar(normed[i][:, b, :], src, moments[i][:, b, 0:1], rstd[i][:, b:b + 1],
                                                ALU.subtract, ALU.mult)
                    ins.then_inc(S[pre + "_ready"], 1)

            def modulated(J, i, kinds="aa"):
                need(eng, ("mods1", "mods2")[i], J, 1)
                need(eng, ("t1_done", "t2_done")[i], J, 1)
                name, k = h_read_by(i, kinds)
                need(eng, name, J, k, ago=1)
                bank = lin[LIN_BANK[("T1_1", "T2_1")[i]]]
                for b in range(2, 4):
                    c = (b - 2) * 256
                    eng.tensor_scalar(hT[i][:, b * TOK:(b + 1) * TOK], bank[:, c:c + TOK],
                                      mods[i][:, 1, b:b + 1], mods[i][:, 0, b:b + 1], ALU.mult, ALU.add)\
                       .then_inc(S[("h1_ready_dve", "h2_ready_dve")[i]], 1)
                    eng.tensor_scalar(hT_rem[i][0:REM, b * TOK:(b + 1) * TOK], bank[0:REM, c + TOK:c + 2 * TOK],
                                      mods_rem[i][:, 1, b:b + 1], mods_rem[i][:, 0, b:b + 1], ALU.mult, ALU.add)\
                       .then_inc(S[("h1_ready_dve", "h2_ready_dve")[i]], 1)

            def mids(J, l):
                if l == 0:
                    for T in range(QKT):
                        need(eng, "qk_done", J, T)
                        if T == 0:
                            need(eng, "qk_scaled", J, QKT - 1, ago=1)
                            need(eng, "qk_sq", J, QKT - 1, ago=1)
                        eng.tensor_copy(qk_raw[:, T, :], lin[LIN_BANK[f"QK{T}"]][0:QKM, :])\
                           .then_inc(S["qk_taken"], 1)
                    need(eng, "norm_done", J, 0)
                    need(eng, "norm_y", J, 0, ago=1)
                    eng.tensor_scalar(norm2[:, :], st_bank[0][0:2 * HEADS, :], 1e-24, None, ALU.max)\
                       .then_inc(S["norm_max"], 1)
                    need(eng, "norm_exp", J, 0)
                    eng.tensor_tensor(norm_t[:, 1, :], norm_y[:, 0, :], norm_y[:, 0, :], ALU.mult)\
                       .then_inc(S["norm_y2"], 1)
                    need(eng, "norm_y2", J, 0)
                    eng.scalar_tensor_tensor(out=norm_t[:, 0, :], in0=norm_t[:, 1, :], scalar=-0.5,
                                             in1=norm2[:, :], op0=ALU.mult, op1=ALU.mult)\
                       .then_inc(S["norm_t"], 1)
                    need(eng, "norm_t", J, 0)
                    need(eng, "spread_done", J, QKT - 1, ago=1)
                    eng.scalar_tensor_tensor(out=norm_y[:, 1, :], in0=norm_t[:, 0, :], scalar=1.5,
                                             in1=norm_y[:, 0, :], op0=ALU.add, op1=ALU.mult)\
                       .then_inc(S["norm_y"], 1)
                    for T in range(QKT):
                        need(eng, "spread_done", J, T)
                        if T == 0:
                            need(eng, "qk_mid", J, QKT - 1, ago=1)
                        eng.tensor_tensor(qk_fit[:, T, :], qk_raw[:, T, :], st_bank[(T + 1) % 2][0:QKM, :], ALU.mult)\
                           .then_inc(S["qk_scaled"], 1)
                for T in range(QKT):
                    need(eng, "qk_high", J, T)
                    if T == 0:
                        need(eng, "qk_low", J, QKT - 1, ago=1)
                    if l == 0:
                        eng.tensor_tensor(qk_rest[:, T, :], qk_fit[:, T, :], part_high[:, T, :], ALU.subtract)\
                           .then_inc(S["qk_rest"], 1)
                    else:
                        eng.tensor_tensor(qk_rest[:, T, :], lin[LIN_BANK[f"QK{T}"]][0:QKM, :],
                                          part_high[:, T, :], ALU.subtract).then_inc(S["qk_taken"], 1)
                    need(eng, "qk_rest" if l == 0 else "qk_taken", J, T)
                    if T == 0:
                        need(eng, "parts_stored", J, 2, ago=1)
                    eng.tensor_copy(part_mid[:, T, :], qk_rest[:, T, :]).then_inc(S["qk_mid"], 1)

            def maximum(J, i):
                b, c = divmod(i, CHUNKS)
                need(eng, "score_done", J, i)
                if c == 0:
                    need(eng, "max_low", J, b, ago=1)
                eng.tensor_reduce(maxima[:, b, CH * c:CH * c + CH],
                                  score_bank[i % 2][:, :].rearrange("p (h k) -> p h k", h=CH), AX_X, ALU.max)\
                   .then_inc(S["max_done"], 1)

            def split_max(J, b):
                need(eng, "max_done", J, (b + 1) * CHUNKS - 1)
                need(eng, "mT_done", J, b, ago=1)
                eng.tensor_copy(max_parts[:, b, 0, :], maxima[:, b, :]).then_inc(S["max_high"], 1)
                need(eng, "max_high", J, b)
                eng.tensor_tensor(max_parts[:, b, 1, :], maxima[:, b, :], max_parts[:, b, 0, :], ALU.subtract)\
                   .then_inc(S["max_low"], 1)

            def divide(G, b):
                need(eng, "o_tok_done", G, b)
                o = o_bank[b % 2][:, :].rearrange("p (h r) -> p h r", r=32)
                if b >= 2:
                    need(eng, "o_normed", G, b - 2)
                    need(eng, "o_flip_done", G, b - 2)
                else:
                    need(eng, "o_normed", G, b + 2, ago=1)
                    need(eng, "o_flip_done", G, b + 2, ago=1)
                eng.reciprocal(o_recip[:, b % 2, :].rearrange("p (h r) -> p h r", r=1), o[:, :, HD:HD + 1])\
                   .then_inc(S["o_recip"], 1)
                need(eng, "o_recip", G, b)
                eng.tensor_tensor(o_tok[:, b % 2, :].rearrange("p (h d) -> p h d", d=HD), o[:, :, 0:HD],
                                  o_recip[:, b % 2, :].rearrange("p (h r) -> p h r", r=1)
                                  .broadcast_to([128, HEADS, HD]), ALU.mult).then_inc(S["o_normed"], 1)

            def residual(G, h, which):
                done, gated_name, x_name, use = (
                    ("proj_done", "proj_gated", "x_attn", "PJ"), ("fc2_done", "mlp_gated", "x_mlp", "M"))[which]
                need(eng, done, G, h)
                if h == 0 and which == 0:
                    need(eng, "gates_loaded", G, 1)
                if which == 0:
                    need(eng, "x_mlp", G, h, ago=1)
                    need(eng, "n1_ready", G, GB - 1)
                else:
                    need(eng, "x_attn", G, h)
                    need(eng, "n2_ready", G, GB - 1)
                eng.tensor_tensor(gated[:, h, :], lin[LIN_BANK[f"{use}{h}"]][:, 0:2 * DIM],
                                  gates[:, which, 2 * h:2 * h + 2, :].rearrange("p b n -> p (b n)"), ALU.mult)\
                   .then_inc(S[gated_name], 1)
                need(eng, gated_name, G, h)
                xs = x[:, bass.ds(G.in_layer(GB) + 2 * h, 2), :].rearrange("p b n -> p (b n)")
                eng.tensor_tensor(xs, xs, gated[:, h, :], ALU.add).then_inc(S[x_name], 1)

            def token_scores(J, b):
                need(eng, "tok_ready", J, b)
                if b:
                    need(eng, "tok_scores", J, b - 1)
                else:
                    need(eng, "tok_scores", J, GB - 1, ago=1)
                shape = [128, HEADS, HEADS, HD]
                q = tok_qkv[:, b, 0:DIM].rearrange("p (h o d) -> p h o d", o=1, d=HD).broadcast_to(shape)
                k = tok_qkv[:, b, DIM:2 * DIM].rearrange("p (o k d) -> p o k d", o=1, d=HD).broadcast_to(shape)
                prod = tok_prod.rearrange("p (h k d) -> p h k d", h=HEADS, d=HD)
                eng.tensor_tensor(prod, q, k, ALU.mult).then_inc(S["tok_prod"], 1)
                need(eng, "tok_prod", J, b)
                if b >= 2:
                    need(eng, "tok_weighted", J, b - 2)
                    need(eng, "tok_sum", J, b - 2)
                else:
                    need(eng, "tok_weighted", J, b + 2, ago=1)
                    need(eng, "tok_sum", J, b + 2, ago=1)
                e = tok_e[:, b % 2, :]
                eng.tensor_reduce(e, tok_prod.rearrange("p (s d) -> p s d", d=HD), AX_X, ALU.add)\
                   .then_inc(S["tok_scores"], 1)
                need(eng, "tok_scores", J, b)
                e3 = e.rearrange("p (h k) -> p h k", h=HEADS)
                eng.tensor_reduce(tok_small[:, b % 2, :], e3, AX_X, ALU.max).then_inc(S["tok_max"], 1)
                need(eng, "tok_max", J, b)
                eng.tensor_tensor(tok_less[:, b % 2, :].rearrange("p (h k) -> p h k", h=HEADS), e3,
                                  tok_small[:, b % 2, :].rearrange("p (h o) -> p h o", o=1)
                                  .broadcast_to([128, HEADS, HEADS]), ALU.subtract).then_inc(S["tok_less"], 1)

            def token_values(J, b):
                need(eng, "tok_exp", J, b)
                eng.tensor_reduce(tok_small[:, 2 + b % 2, :], tok_e[:, b % 2, :].rearrange("p (h k) -> p h k", h=HEADS),
                                  AX_X, ALU.add).then_inc(S["tok_sum"], 1)
                need(eng, "tok_sum", J, b)
                eng.reciprocal(tok_small[:, 4 + b % 2, :], tok_small[:, 2 + b % 2, :]).then_inc(S["tok_recip"], 1)
                need(eng, "tok_weighted", J, b)
                eng.tensor_reduce(tok_o[:, b % 2, :], tok_weighted[b % 2].rearrange("p (s k) -> p s k", k=HEADS),
                                  AX_X, ALU.add).then_inc(S["tok_values"], 1)
                need(eng, "tok_recip", J, b)
                need(eng, "tok_values", J, b)
                if b >= 2:
                    need(eng, "mixed_stored", J, b - 2)
                else:
                    need(eng, "mixed_stored", J, b + 2, ago=1)
                eng.tensor_tensor(tok_o[:, 2 + b % 2, :].rearrange("p (h d) -> p h d", d=HD),
                                  tok_o[:, b % 2, :].rearrange("p (h d) -> p h d", d=HD),
                                  tok_small[:, 4 + b % 2, :].rearrange("p (h o) -> p h o", o=1)
                                  .broadcast_to([128, HEADS, HD]), ALU.mult).then_inc(S["tok_normed"], 1)

            eng.wait_ge(setup["x"], 64)
            first = Group(0)
            statistics(first, 0, 0)
            normalise(first, 0, 0)
            modulated(first, 0)
            mids(first, 0)
            for i in range(AHEAD):
                maximum(first, i)
                if i % CHUNKS == CHUNKS - 1:
                    split_max(first, i // CHUNKS)

            def body(G, l, nxt):
                J = G.plus(1)
                kinds = KINDS[l] + (KINDS[nxt] if nxt is not None else "-")
                if kinds[0] == "a":
                    for i in range(AHEAD, STEPS):
                        maximum(G, i)
                        if i % CHUNKS == CHUNKS - 1:
                            split_max(G, i // CHUNKS)
                    divide(G, 0)
                else:
                    token_values(G, 0)
                    token_scores(G, 2)
                if nxt is not None:
                    statistics(J, nxt, 0)
                if kinds[0] == "a":
                    divide(G, 1)
                else:
                    token_values(G, 1)
                    token_scores(G, 3)
                if nxt is not None:
                    normalise(J, nxt, 0)
                if kinds[0] == "a":
                    divide(G, 2)
                else:
                    token_values(G, 2)
                if nxt is not None:
                    modulated(J, 0, kinds)
                if kinds[0] == "a":
                    divide(G, 3)
                else:
                    token_values(G, 3)
                if kinds[1] == "a":
                    mids(J, nxt)
                residual(G, 0, 0)
                residual(G, 1, 0)
                statistics(G, l, 1)
                normalise(G, l, 1)
                modulated(G, 1)
                for h in range(2):
                    if kinds[1] == "a":
                        for c in range(CHUNKS):
                            maximum(J, h * CHUNKS + c)
                        split_max(J, h)
                    elif kinds[1] == "t":
                        token_scores(J, h)
                    if kinds[1] != "t":
                        residual(G, h, 1)
                if kinds[1] == "t":
                    residual(G, 0, 1)
                    residual(G, 1, 1)

            layers(eng, body)

        @block.tensor
        def _(eng):
            start_with(eng, ("t1_done", "t2_done", "qk_done", "v_done", "score_done", "mT_done", "st_done",
                             "pv_done", "o_tok_done", "o_flip_done", "proj_done", "fc1_done", "fc2_done",
                             "tok_done", "norm_done", "spread_done"))

            def bank_of(use, J, this, nxt):
                before, turns = use_before(use, this, nxt)
                if before is not None:
                    _, name, k = LIN_USES[before]
                    need(eng, name, J, k, ago=(use in OF_NEXT) - (before in OF_NEXT) + turns)
                return lin[LIN_BANK[use]]

            eng.wait_ge(setup["silu"], 7)
            for l in range(LAYERS):
                eng.wait_ge(setup["ada"], 48 * (l + 1))
                if l:
                    eng.wait_ge(setup["mods_kept"], 2 * l)
                    eng.wait_ge(setup["gates_kept"], l)
                for j, k in enumerate((0, 1, 3, 4)):
                    for m, c0, c1 in ((128, 128 * 0, k * DIM), (REM, 128, k * DIM + 128)):
                        o = lin[0][0:m, c0 + j * SEQS:c0 + (j + 1) * SEQS]
                        eng.matmul(o, w_ada[:, c1:c1 + m], silu[:, :], start=True, stop=False)
                        eng.matmul(o, w_ada_rem[:, c1:c1 + m], silu_rem[:, :], start=False, stop=True)
                for w in range(2):
                    o = lin[1][0:SEQS, w * DIM:(w + 1) * DIM]
                    c1 = (2 + 3 * w) * DIM
                    eng.matmul(o, silu[:, :], w_ada[:, c1:c1 + DIM], start=True, stop=False)
                    ins = eng.matmul(o, silu_rem[:, :], w_ada_rem[:, c1:c1 + DIM], start=False, stop=True)
                ins.then_inc(setup["mods_done"], 1)

            def flip_rows(J, i, h, **turn):
                use = ("T1_", "T2_")[i] + str(h)
                need(eng, ("n1_ready", "n2_ready")[i], J, 2 * h + 1)
                bank = bank_of(use, J, **turn)
                for b in (0, 1):
                    src = normed[i][:, 2 * h + b, :]
                    eng.transpose(bank[:, b * 256:b * 256 + TOK], src[:, 0:128], ident[:, :])
                    ins = eng.transpose(bank[0:REM, b * 256 + TOK:(b + 1) * 256], src[:, 128:DIM], ident[:, :])
                ins.then_inc(S[("t1_done", "t2_done")[i]], 1)

            def queries_keys(J, l, T, **turn):
                if T == 0:
                    need(eng, "h1_ready_act", J, 3)
                    need(eng, "h1_ready_dve", J, 3)
                bank = bank_of(f"QK{T}", J, **turn)[0:QKM, :]
                eng.matmul(bank, w_qk[l][:, T * QKM:(T + 1) * QKM], hT[0][:, :], start=True, stop=False)
                eng.matmul(bank, w_qk_rem[l][:, T * QKM:(T + 1) * QKM], hT_rem[0][:, :], start=False, stop=True)\
                   .then_inc(S["qk_done"], 1)

            def head_norms(J):
                need(eng, "exp_done", J, STEPS - 1, ago=1)
                for T in range(QKT):
                    need(eng, "qk_sq", J, T)
                    ins = eng.matmul(st_bank[0][0:2 * HEADS, :], pick[:, T, :], qk_sq[:, T, :], start=T == 0,
                                     stop=T == QKT - 1)
                ins.then_inc(S["norm_done"], 1)
                need(eng, "norm_y", J, 0)
                for T in range(QKT):
                    if T == 2:
                        need(eng, "qk_scaled", J, 0)
                    eng.matmul(st_bank[(T + 1) % 2][0:QKM, :], spread[:, T * QKM:(T + 1) * QKM], norm_y[:, 1, :],
                               start=True, stop=True).then_inc(S["spread_done"], 1)

            def values(J, l, h, **turn):
                bank = bank_of(f"V{h}", J, **turn)
                for b in range(2):
                    tok = slice((2 * h + b) * TOK, (2 * h + b + 1) * TOK)
                    o = bank[:, b * DIM:(b + 1) * DIM]
                    eng.matmul(o, hT[0][:, tok], w_v[l][:, :], start=True, stop=False)
                    ins = eng.matmul(o, hT_rem[0][:, tok], w_v_rem[l][:, :], start=False, stop=True)
                ins.then_inc(S["v_done"], 1)

            def scores(J, i):
                b, c = divmod(i, CHUNKS)
                if i == 0:
                    need(eng, "stack_loaded", J, 11)
                if i >= 2:
                    need(eng, "max_done", J, i - 2)
                else:
                    need(eng, "max_done", J, i - 2 + STEPS, ago=1)
                tok = slice(b * TOK, (b + 1) * TOK)
                for j in range(CH):
                    h = CH * c + j
                    ins = eng.matmul(score_bank[i % 2][:, j * TOK:(j + 1) * TOK], q_stack[0:PARTS, h, tok],
                                     k_stack[0:PARTS, h, tok], start=True, stop=True)
                ins.then_inc(S["score_done"], 1)

            def flip_max(J, b, **turn):
                need(eng, "max_low", J, b)
                bank_of(f"mT{b}", J, **turn)
                eng.transpose(lin_b[LIN_BANK[f"mT{b}"]][0:2 * HEADS, 0:TOK],
                              max_parts[:, b, :, :].rearrange("p i h -> p (i h)"), ident_b[:, :])\
                   .then_inc(S["mT_done"], 1)

            def shifted_scores(G, i):
                b, c = divmod(i, CHUNKS)
                if c == 0:
                    need(eng, f"m_loaded{b}", G, 1)
                if i >= 2:
                    need(eng, "exp_done", G, i - 2)
                else:
                    need(eng, "exp_done", G, i - 2 + STEPS, ago=1)
                tok = slice(b * TOK, (b + 1) * TOK)
                for j in range(CH):
                    h = CH * c + j
                    ins = eng.matmul(st_bank[i % 2][:, j * TOK:(j + 1) * TOK], k_stack[0:STACK, h, tok],
                                     q_stack[0:STACK, h, tok], start=True, stop=True)
                ins.then_inc(S["st_done"], 1)

            def weighted_values(G, i):
                b, c = divmod(i, CHUNKS)
                need(eng, "exp_done", G, i)
                if c == 0:
                    need(eng, "v_ready", G, b // 2)
                    if b >= 2:
                        need(eng, "o_normed", G, b - 2)
                    else:
                        need(eng, "o_normed", G, b + 2, ago=1)
                for j in range(CH):
                    ins = eng.matmul(o_bank[b % 2][32 * j:32 * j + 32, c * TOK:(c + 1) * TOK],
                                     v_aug[:, b, CH * c + j, :], probs[:, i % PBUFS, j * TOK:(j + 1) * TOK],
                                     start=True, stop=True)
                ins.then_inc(S["pv_done"], 1)

            def o_to_tokens(G, b):
                need(eng, "o_copied", G, b)
                for c in range(CHUNKS):
                    ins = eng.transpose(o_bank[b % 2][:, c * TOK:(c + 1) * TOK],
                                        o_feat[:, b % 2, c * TOK:(c + 1) * TOK], ident[:, :])
                ins.then_inc(S["o_tok_done"], 1)

            def flip_o(G, b, **turn):
                if turn["this"] == "a":
                    need(eng, "o_normed", G, b)
                    src = o_tok[:, b % 2, :]
                else:
                    need(eng, f"mixed{b}", G, 0)
                    src = mixed[:, b, :]
                bank = bank_of(f"OD{b}", G, **turn)
                eng.transpose(bank[:, 0:TOK], src[:, 0:128], ident[:, :])
                eng.transpose(bank[0:REM, TOK:2 * TOK], src[:, 128:DIM], ident[:, :])\
                   .then_inc(S["o_flip_done"], 1)

            def token_qkv(J, l, b, **turn):
                if b == 0:
                    need(eng, "h1_ready_act", J, 3)
                    need(eng, "h1_ready_dve", J, 3)
                bank = bank_of(f"Q{b}", J, **turn)
                tok = slice(b * TOK, (b + 1) * TOK)
                for c, w, w_rem in ((slice(0, 2 * DIM), w_qk[l], w_qk_rem[l]),
                                    (slice(2 * DIM, 3 * DIM), w_v[l], w_v_rem[l])):
                    eng.matmul(bank[:, c], hT[0][:, tok], w[:, :], start=True, stop=False)
                    ins = eng.matmul(bank[:, c], hT_rem[0][:, tok], w_rem[:, :], start=False, stop=True)
                ins.then_inc(S["tok_done"], 1)

            def project(G, l, h, **turn):
                need(eng, "oT_ready", G, 2 * h + 1)
                bank = bank_of(f"PJ{h}", G, **turn)
                for b in range(2):
                    tok = slice((2 * h + b) * TOK, (2 * h + b + 1) * TOK)
                    o = bank[:, b * DIM:(b + 1) * DIM]
                    eng.matmul(o, oT[:, tok], w_o[l][:, :], start=True, stop=False)
                    ins = eng.matmul(o, oT_rem[:, tok], w_o_rem[l][:, :], start=False, stop=True)
                ins.then_inc(S["proj_done"], 1)

            def up(G, l, T, **turn):
                if T == 0:
                    need(eng, "h2_ready_act", G, 3)
                    need(eng, "h2_ready_dve", G, 3)
                bank = bank_of(f"F{T}", G, **turn)[0:FCM[T], :]
                cols = slice(T * 128, T * 128 + FCM[T])
                eng.matmul(bank, w_f1[l][:, cols], hT[1][:, :], start=True, stop=False)
                eng.matmul(bank, w_f1_rem[l][:, cols], hT_rem[1][:, :], start=False, stop=True)\
                   .then_inc(S["fc1_done"], 1)

            def down(G, l, bank, b):
                o = bank[:, (b % 2) * DIM:(b % 2 + 1) * DIM]
                for T in range(FCT):
                    if b == 0:
                        need(eng, "gelu_ready", G, T)
                    k = 128 if T < FCT - 1 else FCM[T] + 1
                    ins = eng.matmul(o, gelu[0:k, T, b * TOK:(b + 1) * TOK], w_f2[l][0:k, T, :], start=T == 0,
                                     stop=T == FCT - 1)
                return ins

            eng.wait_ge(setup["weights"], 16 * LAYERS * 15)
            eng.wait_ge(setup["mods_kept"], 2 * LAYERS)
            eng.wait_ge(setup["gates_kept"], LAYERS)
            eng.wait_ge(setup["ones"], 6)
            eng.wait_ge(setup["const"], CONSTS)
            eng.wait_ge(setup["picks"], 2)
            start = dict(this=None, nxt="a")
            first = Group(0)
            flip_rows(first, 0, 0, **start)
            flip_rows(first, 0, 1, **start)
            for T in range(QKT):
                queries_keys(first, 0, T, **start)
            head_norms(first)
            values(first, 0, 0, **start)
            values(first, 0, 1, **start)
            for i in range(AHEAD):
                scores(first, i)
            flip_max(first, 0, **start)
            need(eng, "v_ready", first, 1)

            def body(G, l, nxt):
                J = G.plus(1)
                turn = dict(this=KINDS[l], nxt=None if nxt is None else KINDS[nxt])
                this, nxt_kind = turn["this"], turn["nxt"]
                if this == "a":
                    for i in range(STEPS + LAG):
                        if i < STEPS:
                            shifted_scores(G, i)
                            if i + AHEAD < STEPS:
                                scores(G, i + AHEAD)
                        if i >= LAG:
                            weighted_values(G, i - LAG)
                        if i in (1, 5, 9):
                            flip_max(G, i // 4 + 1, **turn)
                        if i in (7, 11, 15):
                            o_to_tokens(G, i // 4 - 1)
                        if i in (9, 13):
                            flip_o(G, i // 4 - 2, **turn)
                else:
                    flip_o(G, 0, **turn)
                    flip_o(G, 1, **turn)
                if nxt is not None:
                    flip_rows(J, 0, 0, **turn)
                    flip_rows(J, 0, 1, **turn)
                if this == "a":
                    o_to_tokens(G, 3)
                flip_o(G, 2, **turn)
                if nxt_kind == "a":
                    for T in range(QKT):
                        queries_keys(J, nxt, T, **turn)
                elif nxt_kind == "t":
                    for b in range(GB):
                        token_qkv(J, nxt, b, **turn)
                flip_o(G, 3, **turn)
                if nxt == 0:
                    head_norms(J)
                project(G, l, 0, **turn)
                project(G, l, 1, **turn)
                if nxt_kind == "a":
                    values(J, nxt, 0, **turn)
                    values(J, nxt, 1, **turn)
                flip_rows(G, 1, 0, **turn)
                flip_rows(G, 1, 1, **turn)
                for T in range(FCT):
                    up(G, l, T, **turn)
                for h in range(2):
                    bank = bank_of(f"M{h}", G, **turn)
                    for b in (2 * h, 2 * h + 1):
                        if nxt_kind == "a":
                            scores(J, 2 * b)
                        ins = down(G, l, bank, b)
                        if nxt_kind == "a":
                            scores(J, 2 * b + 1)
                    ins.then_inc(S["fc2_done"], 1)
                    if h == 0 and nxt_kind == "a":
                        flip_max(J, 0, **turn)

            layers(eng, body)


def kernel(**inputs):
    import numpy as np
    import concourse.bacc as bacc
    from concourse.bass_utils import run_bass_kernel_spmd

    names = {
        0: ("qkv_w", "qkv_b", "proj_w", "proj_b", "fc1_w", "fc1_b", "fc2_w", "fc2_b", "ada_w", "ada_b"),
        1: ("w_qkv", "b_qkv", "w_proj", "b_proj", "w_fc1", "b_fc1", "w_fc2", "b_fc2", "w_ada", "b_ada"),
        2: ("qkv_w", "qkv_b", "out_w", "out_b", "w1", "b1", "w2", "b2", "ada_w", "ada_b"),
        3: ("qkv_w", "qkv_b", "proj_w", "proj_b", "fc1_w", "fc1_b", "fc2_w", "fc2_b", "ada_w", "ada_b"),
    }
    mine = ("qkv_w", "qkv_b", "o_w", "o_b", "f1_w", "f1_b", "f2_w", "f2_b", "ada_w", "ada_b")
    arrays = {"x": inputs["x"], "cT": np.asarray(inputs["cond_1152"]).T}
    for short in ("g1", "g2", "qg", "kg"):
        arrays[short] = inputs[f"L0_cond_{short}"]
    for l, theirs in names.items():
        for a, b in zip(mine, theirs):
            w = np.asarray(inputs[f"L{l}_cond_{b}"])
            w = w.T if l == 0 and w.ndim == 2 else w
            if a in ("qkv_w", "qkv_b"):
                qk = w[..., :2 * DIM]
                if KINDS[l] == "a":
                    qk = np.swapaxes(qk.reshape(*w.shape[:-1], 2, HEADS, HD), -1, -2).reshape(qk.shape)
                arrays[f"qk{a[3:]}{l}"] = qk
                arrays[f"v{a[3:]}{l}"] = w[..., 2 * DIM:]
            else:
                arrays[f"{a}{l}"] = w

    nc = bacc.Bacc("TRN2", target_bir_lowering=False, num_devices=1)
    feeds, aps = {}, {}
    for name, a in arrays.items():
        a = np.ascontiguousarray(a)
        feeds[f"in_{name}"] = a
        aps[name] = nc.dram_tensor(f"in_{name}", a.shape, mybir.dt.from_np(a.dtype), kind="ExternalInput").ap()
    out = nc.dram_tensor("out_x", (SEQS, TOK, DIM), F32, kind="ExternalOutput").ap()
    blocks_kernel(nc, aps, out)
    r = run_bass_kernel_spmd(nc, [feeds], core_ids=[0])
    return r.results[0]["out_x"]
```

```python
from contextlib import ExitStack

import concourse.bass as bass
from concourse import mybir

F32 = mybir.dt.float32
BF16 = mybir.dt.bfloat16
ALU = mybir.AluOpType
ACT = mybir.ActivationFunctionType
AX_X = mybir.AxisListType.X

LAYERS = 4
KINDS = "aaat"
SEQS, TOK, DIM = 32, 128, 144
HEADS = 16
HD = DIM // HEADS
HIDDEN = 4 * DIM
REM = DIM - 128
COPIES = 7
REM_ROWS = COPIES * REM
MID_ROW, LOW_ROW, BIAS_ROW = 64, 96, 48
GB = 4
GT = GB * TOK
GROUPS = SEQS // GB
QKM = 96
QKT = 2 * DIM // QKM
FCT = 5
FCM = [128, 128, 128, 128, 64]
Q_PARTS = (0, 0, 0, 1, 1, 2)
K_PARTS = (0, 1, 2, 0, 1, 0)
PARTS = len(Q_PARTS) * HD
SCORE_ROWS = 120
MAX_ROW = 126
CH = 4
CHUNKS = HEADS // CH
STEPS = GB * CHUNKS
AHEAD = 3 * CHUNKS
LAG = 2
PBUFS = 4

LIN_USES = {
    "mT2": (0, "mT_copied", 2),
    "T1_0": (1, "h1_ready_act", 3), "T1_1": (0, "h1_ready_dve", 3),
    "mT3": (1, "mT_copied", 3),
    "QK0": (0, "qk_taken", 0), "QK1": (1, "qk_taken", 1), "QK2": (1, "qk_taken", 2),
    "OD0": (0, "oT_ready", 0), "OD1": (0, "oT_ready", 1), "OD2": (1, "oT_ready", 2), "OD3": (1, "oT_ready", 3),
    "Q0": (0, "tok_ready", 0), "Q1": (1, "tok_ready", 1), "Q2": (0, "tok_ready", 2), "Q3": (1, "tok_ready", 3),
    "PJ0": (0, "proj_gated", 0), "V0": (0, "v_ready", 0), "PJ1": (1, "proj_gated", 1), "V1": (0, "v_ready", 1),
    "T2_0": (1, "h2_ready_act", 3), "T2_1": (0, "h2_ready_dve", 3),
    "F0": (1, "gelu_ready", 0), "F1": (0, "gelu_ready", 1), "F2": (1, "gelu_ready", 2),
    "F3": (0, "gelu_ready", 3), "F4": (1, "gelu_ready", 4),
    "M0": (0, "mlp_gated", 0), "mT0": (1, "mT_copied", 0), "M1": (1, "mlp_gated", 1), "mT1": (0, "mT_copied", 1),
}
LIN_BANK = {name: use[0] for name, use in LIN_USES.items()}
OF_NEXT = {"T1_0", "T1_1", "QK0", "QK1", "QK2", "Q0", "Q1", "Q2", "Q3", "V0", "V1", "mT0", "mT1"}


def uses_of(this, nxt):
    flips = ["T1_0", "T1_1"] if nxt else []
    qk = ["QK0", "QK1", "QK2"] if nxt == "a" else []
    tok = ["Q0", "Q1", "Q2", "Q3"] if nxt == "t" else []
    vals = ["V0", "V1"] if nxt == "a" else []
    maxT = ["mT0", "mT1"] if nxt == "a" else []
    if this is None:
        return flips + qk + tok + vals + maxT
    if this == "a":
        start = ["mT2"] + flips + ["mT3"] + qk[:2] + ["OD0"] + qk[2:] + ["OD1", "OD2", "PJ0", "OD3"]
    else:
        start = ["OD0", "OD1"] + flips + ["OD2", "OD3", "PJ0"]
    return (start + vals[:1] + ["PJ1"] + vals[1:] + tok + ["T2_0", "T2_1"]
            + [f"F{T}" for T in range(FCT)] + ["M0"] + maxT[:1] + ["M1"] + maxT[1:])


def use_before(use, this, nxt):
    order = uses_of(this, nxt)
    bank = LIN_BANK[use]
    same = [name for name in order[:order.index(use)] if LIN_BANK[name] == bank]
    if same:
        return same[-1], 0
    if this is None:
        return None, 0
    return [name for name in uses_of("a", this) if LIN_BANK[name] == bank][-1], 1


W_QK, W_V, W_F1 = 0, 2 * DIM, 3 * DIM
W_COLS = 3 * DIM + HIDDEN

ONES = 5 + 1
CONSTS = 4 + 1 + QKM // HEADS + 2 + 1 + 1

PER_GROUP = {
    "n1_stats": GB, "n1_aggr": GB, "n1_var": 3, "n1_rstd": 1, "n1_ready": GB + 1,
    "n2_stats": GB, "n2_aggr": GB, "n2_var": 3, "n2_rstd": 1, "n2_ready": GB + 1,
    "h1_parts": 4, "h2_parts": 4,
    "t1_done": 2, "t2_done": 2,
    "h1_ready_act": 4, "h1_ready_dve": 4, "h2_ready_act": 4, "h2_ready_dve": 4,
    "qk_done": QKT, "qk_taken": QKT, "qk_high": QKT, "qk_mid": QKT, "qk_low": QKT,
    "v_done": 2, "v_ready": 2,
    "score_done": STEPS, "max_done": STEPS, "max_high": GB, "max_low": GB,
    "mT_done": GB, "mT_copied": GB,
    "st_done": STEPS, "exp_done": STEPS, "pv_done": STEPS,
    "o_copied": GB, "o_tok_done": GB, "o_recip": GB, "o_normed": GB, "o_flip_done": GB, "oT_ready": GB,
    "proj_done": 2, "proj_gated": 2, "x_attn": 2,
    "fc1_done": FCT, "gelu_ready": FCT, "fc2_done": 2, "mlp_gated": 2, "x_mlp": 2,
    "mods1": 2, "mods2": 2,
    "tok_done": GB, "tok_ready": GB, "tok_prod": GB, "tok_scores": GB, "tok_max": GB, "tok_less": GB,
    "tok_exp": GB, "tok_sum": GB, "tok_recip": GB, "tok_weighted": GB, "tok_values": GB, "tok_normed": GB,
    "qk_rest": QKT, "qk_sq": QKT, "norm_done": 1, "norm_max": 1, "norm_ln": 1, "norm_exp": 1, "norm_y2": 1, "norm_t": 1,
    "norm_y": 1, "spread_done": QKT, "qk_scaled": QKT,
}
PER_GROUP_DMA = {"parts_stored": 3, "stack_loaded": 6, "m_loaded0": 2, "m_loaded1": 2, "m_loaded2": 2,
                 "m_loaded3": 2, "gates_loaded": 2,
                 "mixed_stored": 4, "mixed0": 1, "mixed1": 1, "mixed2": 1, "mixed3": 1}
TOKEN_ONLY = {name for name in [*PER_GROUP, *PER_GROUP_DMA] if name.startswith(("tok_", "mixed"))}
FIRST_TOKEN_GROUP = KINDS.index("t") * GROUPS


class Group:

    def __init__(self, base, reg=None):
        self.base, self.reg = base, reg

    def plus(self, n):
        return Group(self.base + n, self.reg)

    def times(self, n, more=0):
        whole = self.base * n + more
        return whole if self.reg is None else self.reg * n + whole

    @property
    def is_first(self):
        return self.reg is None and self.base == 0

    def in_layer(self, n):
        if self.reg is None:
            return (self.base % GROUPS) * n
        return self.reg * n + (self.base % GROUPS) * n


def blocks_kernel(nc, t, out):
    ctx = ExitStack()
    with ctx:
        def sb(name, shape, dt=F32):
            return ctx.enter_context(nc.sbuf_tensor(name, shape, dt))

        def ps(name):
            return ctx.enter_context(nc.psum_tensor(name, [128, 512], F32))

        x = sb("x", [128, SEQS, DIM])
        w_h = [sb(f"w_h{l}", [128, W_COLS]) for l in range(LAYERS)]
        w_h_rem = [sb(f"w_h_rem{l}", [128, W_COLS], BF16) for l in range(LAYERS)]
        w_o = [sb(f"w_o{l}", [128, DIM]) for l in range(LAYERS)]
        w_o_rem = [sb(f"w_o_rem{l}", [REM + 1, DIM]) for l in range(LAYERS)]
        w_f2 = [sb(f"w_f2{l}", [128, FCT, DIM]) for l in range(LAYERS)]
        mod_main = sb("mod_main", [128, LAYERS, 4, SEQS])
        mod_rem = sb("mod_rem", [REM_ROWS, LAYERS, 4, SEQS])
        ident = sb("ident", [128, 128])
        ident_b = sb("ident_b", [128, 128], BF16)
        neg_half = sb("neg_half", [128, GB])

        stats = [sb(f"stats{i}", [128, GB, 6]) for i in range(2)]
        moments = [sb(f"moments{i}", [128, GB, 2]) for i in range(2)]
        mean_sq = sb("mean_sq", [128, 2, GB])
        var = [sb(f"var{i}", [128, GB]) for i in range(2)]
        rstd = [sb(f"rstd{i}", [128, GB]) for i in range(2)]
        normed = [sb(f"normed{i}", [128, GB, DIM]) for i in range(2)]
        normed_last = [sb(f"normed_last{i}", [128, GB, REM_ROWS]) for i in range(2)]
        mods = [sb(f"mods{i}", [128, 2, GB]) for i in range(2)]
        mods_rem = [sb(f"mods_rem{i}", [REM_ROWS, 2, GB]) for i in range(2)]
        hT = [sb(f"hT{i}", [128, GT]) for i in range(2)]
        hT_last = [sb(f"hT_last{i}", [REM_ROWS, GT]) for i in range(2)]
        hT_rem = [sb(f"hT_rem{i}", [128, GT], BF16) for i in range(2)]
        h_rest = sb("h_rest", [128, GT])
        part_high = sb("part_high", [QKM, QKT, GT], BF16)
        part_mid = sb("part_mid", [QKM, QKT, GT], BF16)
        part_low = sb("part_low", [QKM, QKT, GT], BF16)
        qk_rest = sb("qk_rest", [QKM, QKT, GT])
        q_room = sb("q_room", [128, HEADS * GT // 2])
        k_room = sb("k_room", [128, HEADS * GT // 2])
        q_stack = q_room[:, :].bitcast(BF16).rearrange("p (h n) -> p h n", h=HEADS)
        k_stack = k_room[:, :].bitcast(BF16).rearrange("p (h n) -> p h n", h=HEADS)
        v_room = sb("v_room", [128, GB * HEADS * 32])
        v_aug = v_room[:, :].rearrange("p (b h r) -> p b h r", b=GB, h=HEADS)
        maxima = sb("maxima", [128, GB, HEADS])
        max_parts = sb("max_parts", [128, GB, 2, HEADS], BF16)
        max_T = sb("max_T", [2 * HEADS, GB, TOK], BF16)
        p_room = sb("p_room", [128, PBUFS * CH * TOK])
        probs = p_room[:, :].rearrange("p (i n) -> p i n", i=PBUFS)
        o_room = sb("o_room", [128, 2 * CHUNKS * TOK])
        o_feat = o_room[:, :].rearrange("p (i n) -> p i n", i=2)
        o_recip = sb("o_recip", [128, 2, HEADS])
        o_tok = sb("o_tok", [128, 2, DIM])
        oT = sb("oT", [128, GT])
        oT_rem = sb("oT_rem", [REM + 1, GT])
        gates = sb("gates", [128, 2, GB, DIM])
        gated = sb("gated", [128, 2, 2 * DIM])
        gelu = sb("gelu", [128, FCT, GT])

        pick = sb("pick", [QKM, QKT, 2 * HEADS])
        spread = sb("spread", [2 * HEADS, 2 * DIM])
        head_gain = sb("head_gain", [2 * HEADS, 1])
        raw_room = sb("raw_room", [128, 2 * QKT * GT])
        raw2 = raw_room[0:QKM, :].rearrange("p (i t n) -> p i t n", i=2, t=QKT)
        qk_raw, qk_sq = raw2[:, 0], raw2[:, 1]
        qk_fit = sb("qk_fit", [QKM, QKT, GT])
        norm2 = sb("norm2", [2 * HEADS, GT])
        mod_last = norm2[0:REM, :].rearrange("p (l i b) -> p l i b", l=LAYERS, i=4)
        norm_y = sb("norm_y_buf", [2 * HEADS, 2, GT])
        norm_t = sb("norm_t_buf", [2 * HEADS, 2, GT])

        MIX = HEADS * HEADS * HD
        tok_qkv = v_room[:, 0:GB * 3 * DIM].rearrange("p (b n) -> p b n", b=GB)
        tok_prod = q_room[:, 0:MIX]
        tok_weighted = [k_room[:, 0:MIX], raw_room[:, 0:MIX]]
        n0 = 2 * HEADS * HEADS
        tok_e = p_room[:, 0:n0].rearrange("p (i n) -> p i n", i=2)
        tok_less = p_room[:, n0:2 * n0].rearrange("p (i n) -> p i n", i=2)
        tok_o = p_room[:, 2 * n0:2 * n0 + 4 * DIM].rearrange("p (i n) -> p i n", i=4)
        n1 = 2 * n0 + 4 * DIM
        tok_small = p_room[:, n1:n1 + 6 * HEADS].rearrange("p (i n) -> p i n", i=6)
        mixed = o_room[:, 0:GB * DIM].rearrange("p (b n) -> p b n", b=GB)

        cT = sb("cT", [128, SEQS])
        cT_rem = sb("cT_rem", [REM + 1, SEQS])
        c_exp = sb("c_exp", [128, 2, SEQS])
        c_exp_rem = sb("c_exp_rem", [REM, 2, SEQS])
        silu = sb("silu", [128, SEQS])
        silu_rem = sb("silu_rem", [REM + 1, SEQS])
        w_ada = [q_room[:, l * 6 * DIM:(l + 1) * 6 * DIM] for l in range(LAYERS)]
        flat = gelu[:, :, :].rearrange("p t n -> p (t n)")
        gate_rows = flat[0:SEQS, 0:LAYERS * 2 * DIM].rearrange("b (l n) -> b l n", l=LAYERS)
        w_ada_rem = [raw_room[0:REM + 1, l * 6 * DIM:(l + 1) * 6 * DIM] for l in range(LAYERS - 1)]
        w_ada_rem.append(flat[0:REM + 1, LAYERS * 2 * DIM:(LAYERS * 2 + 6) * DIM])
        w_stage = [k_room[:, l * W_COLS:(l + 1) * W_COLS] for l in range(LAYERS)]
        w_rest = p_room[:, 0:W_COLS]
        w_parts = p_room[:, W_COLS:2 * W_COLS].bitcast(BF16).rearrange("p (i n) -> p i n", i=2)
        copier = sb("copier", [REM, REM_ROWS])
        part_of = sb("part_of", [128, 3])
        gain = sb("gain", [128, 2])

        score_bank = [ps(f"score_bank{i}") for i in range(2)]
        st_bank = [ps(f"st_bank{i}") for i in range(2)]
        o_bank = [ps(f"o_bank{i}") for i in range(2)]
        lin = [ps(f"lin{i}") for i in range(2)]
        mod_banks = (lin, score_bank, st_bank, o_bank)
        lin_b = [lin[i][:, :].bitcast(BF16) for i in range(2)]

        parts_dram = nc.dram_tensor("parts_dram", [3, 2 * DIM, GT], BF16, kind="Internal").ap()
        gates_dram = nc.dram_tensor("gates_dram", [LAYERS, 2, SEQS, DIM], F32, kind="Internal").ap()

        mix_dram = nc.dram_tensor("mix_dram", [GB, HEADS, TOK, HD], F32, kind="Internal").ap()

        S = {name: ctx.enter_context(nc.semaphore(name)) for name in [*PER_GROUP, *PER_GROUP_DMA]}
        setup = {name: ctx.enter_context(nc.semaphore("set_" + name)) for name in (
            "x", "weights_first", "weights", "stage_clear", "staged", "split", "c", "ada0", "ada1", "ada2", "ada3", "gain", "const", "ones",
            "clear", "c_exp", "silu", "mods_done", "mods_kept", "gates_kept", "gates_stored", "picks", "carrier", "out")}
        block = ctx.enter_context(nc.Block())

        def need(eng, name, group, k, ago=0):
            unit = 1 if name in PER_GROUP else 16
            if name in TOKEN_ONLY:
                group = group.plus(-FIRST_TOKEN_GROUP)
            n = PER_GROUP[name] if name in PER_GROUP else PER_GROUP_DMA[name]
            value = group.times(unit * n, unit * (n * (1 - ago) + k + 1))
            if group.reg is None and value <= 0:
                return
            eng.wait_ge(S[name], value)

        def start_with(eng, names):
            for name in names:
                eng.sem_inc(S[name], PER_GROUP[name] if name in PER_GROUP else 16 * PER_GROUP_DMA[name])

        def layers(eng, body):
            for l in range(LAYERS):
                with eng.Fori(0, GROUPS - 1) as g:
                    body(Group(l * GROUPS, g), l, l)
                body(Group(l * GROUPS + GROUPS - 1), l, l + 1 if l + 1 < LAYERS else None)

        def h_read_by(i, kinds):
            if i == 1:
                return "fc1_done", FCT - 1
            return ("v_done", 1) if kinds[0] == "a" else ("tok_done", GB - 1)

        @block.sync
        def _(eng):
            start_with(eng, PER_GROUP_DMA)
            eng.dma_start(cT[:, :], t["cT"][0:128, :]).then_inc(setup["c"], 16)
            eng.dma_start(cT_rem[0:REM, :], t["cT"][128:DIM, :]).then_inc(setup["c"], 16)
            for l in range(LAYERS):
                eng.dma_start(w_ada[l], t[f"ada{l}"][0:128, :]).then_inc(setup[f"ada{l}"], 16)
                eng.dma_start(w_ada_rem[l], t[f"ada{l}"][128:DIM + 1, :]).then_inc(setup[f"ada{l}"], 16)
            for i, name in enumerate(("g1", "g2")):
                eng.dma_start(gain[:, i:i + 1], t[name].partition_broadcast(128)).then_inc(setup["gain"], 16)
            for i, name in enumerate(("qg", "kg")):
                eng.dma_start(head_gain[i * HEADS:(i + 1) * HEADS, :], t[name].partition_broadcast(HEADS))\
                   .then_inc(setup["gain"], 16)
            eng.wait_ge(setup["gates_kept"], LAYERS)
            eng.dma_start(gates_dram.rearrange("l w b n -> b (l w) n"), gate_rows[:, :, :].rearrange(
                "b l (w n) -> b (l w) n", w=2)).then_inc(setup["gates_stored"], 16)
            eng.wait_ge(setup["gates_stored"], 16)

            def load_gates(J, l):
                for w in range(2):
                    src = gates_dram[l, w].rearrange("b n -> (b n)")[bass.ds(J.in_layer(GB * DIM), GB * DIM)]
                    eng.dma_start(gates[:, w, :, :].rearrange("p b n -> p (b n)"), src.partition_broadcast(128))\
                       .then_inc(S["gates_loaded"], 16)

            def load_stack(J):
                for i, (part, ready) in enumerate(((part_high, "qk_high"), (part_mid, "qk_mid"),
                                                   (part_low, "qk_low"))):
                    need(eng, ready, J, QKT - 1)
                    if i == 0:
                        need(eng, "stack_loaded", J, 5, ago=1)
                    eng.dma_start(parts_dram[i].rearrange("(t p) n -> p t n", p=QKM), part[:, :, :])\
                       .then_inc(S["parts_stored"], 16)
                need(eng, "parts_stored", J, 2)
                need(eng, "st_done", J, STEPS - 1, ago=1)
                rows = parts_dram.rearrange("i (s d h) n -> s i d (h n)", s=2, d=HD)
                at = 0
                for i, n in enumerate((3, 2, 1)):
                    src = rows[0, i].rearrange("(o d) n -> o d n", o=1).broadcast_to([n, HD, HEADS * GT])
                    eng.dma_start(q_stack[at * HD:(at + n) * HD, :, :].rearrange("p h n -> p (h n)"), src)\
                       .then_inc(S["stack_loaded"], 16)
                    src = rows[1, 0:3 - i].rearrange("i d n -> i d n")
                    eng.dma_start(k_stack[at * HD:(at + n) * HD, :, :].rearrange("p h n -> p (h n)"), src)\
                       .then_inc(S["stack_loaded"], 16)
                    at += n

            def mix(J, b):
                need(eng, "o_flip_done", J, b, ago=1)
                eng.sem_inc(setup["carrier"], 1)
                need(eng, "tok_normed", J, b)
                if b == 0:
                    for i in range(GB):
                        need(eng, f"mixed{i}", J, 0, ago=1)
                eng.dma_start(mix_dram[b].rearrange("h t d -> t h d"),
                              tok_o[:, 2 + b % 2, :].rearrange("p (h d) -> p h d", d=HD))\
                   .then_inc(S["mixed_stored"], 16)
                need(eng, "mixed_stored", J, b)
                eng.dma_start(mixed[:, b, :], mix_dram[b].rearrange("h t d -> (h t d)")
                              .rearrange("(r c) -> r c", c=DIM)).then_inc(S[f"mixed{b}"], 16)

            def load_max(J, b):
                need(eng, "mT_copied", J, b)
                for i in range(2):
                    eng.dma_start(q_stack[MAX_ROW + i:MAX_ROW + i + 1, :, b * TOK:(b + 1) * TOK],
                                  max_T[i * HEADS:(i + 1) * HEADS, b, :]).then_inc(S[f"m_loaded{b}"], 16)

            first = Group(0)
            load_gates(first, 0)
            load_stack(first)
            load_max(first, 0)
            load_max(first, 1)

            def body(G, l, nxt):
                if KINDS[l] == "a":
                    load_max(G, 2)
                    load_max(G, 3)
                else:
                    for b in range(GB):
                        mix(G, b)
                if nxt is not None and KINDS[nxt] == "a":
                    load_stack(G.plus(1))
                    load_max(G.plus(1), 0)
                    load_max(G.plus(1), 1)
                need(eng, "x_mlp", G, 1)
                eng.sem_inc(setup["carrier"], 1)
                if l == LAYERS - 1:
                    at = G.in_layer(GB)
                    eng.dma_start(out[bass.ds(at, GB)].rearrange("b t d -> t b d"), x[:, bass.ds(at, GB), :])\
                       .then_inc(setup["out"], 16)
                if nxt is not None:
                    load_gates(G.plus(1), nxt)

            layers(eng, body)
            eng.wait_ge(setup["out"], 16 * GROUPS)

        @block.gpsimd
        def _(eng):
            start_with(eng, ("qk_low", "tok_weighted", "n1_rstd", "n2_rstd", "mods1", "mods2"))
            eng.memset(ident[:, :], 0.0).then_inc(setup["const"], 1)
            eng.memset(pick[:, :, :], 0.0).then_inc(setup["const"], 1)
            eng.memset(spread[:, :], 0.0).then_inc(setup["const"], 1)
            eng.memset(neg_half[:, :], -0.5).then_inc(setup["const"], 1)
            eng.wait_ge(setup["const"], 4)
            eng.affine_select(out=ident[:, :], in_=ident[:, :], compare_op=ALU.not_equal, fill=1.0,
                              base=0, pattern=[[-1, 128]], channel_multiplier=1).then_inc(setup["const"], 1)
            heads = pick[:, :, :].rearrange("p t (s h) -> p t s h", s=2)
            for a in range(QKM // HEADS):
                eng.affine_select(out=heads, in_=heads, compare_op=ALU.not_equal, fill=1.0, base=-a * HEADS,
                                  pattern=[[0, QKT], [0, 2], [-1, HEADS]], channel_multiplier=1)\
                   .then_inc(setup["const"], 1)
                eng.wait_ge(setup["const"], 6 + a)
            eng.affine_select(out=heads[:, :, 0, :], in_=heads[:, :, 0, :], compare_op=ALU.is_ge, fill=0.0,
                              base=DIM - 1, pattern=[[-QKM, QKT], [0, HEADS]], channel_multiplier=-1)\
               .then_inc(setup["const"], 1)
            eng.affine_select(out=heads[:, :, 1, :], in_=heads[:, :, 1, :], compare_op=ALU.is_ge, fill=0.0,
                              base=-DIM, pattern=[[QKM, QKT], [0, HEADS]], channel_multiplier=1)\
               .then_inc(setup["const"], 1)
            rows = spread[:, :].rearrange("m (s d h) -> m s d h", s=2, d=HD)
            eng.affine_select(out=rows, in_=rows, compare_op=ALU.not_equal, fill=1.0, base=0,
                              pattern=[[-HEADS, 2], [0, HD], [-1, HEADS]], channel_multiplier=1)\
               .then_inc(setup["const"], 1)
            eng.tensor_copy(ident_b[:, :], ident[:, :]).then_inc(setup["const"], 1)

            def mods_of(J, l, i):
                need(eng, ("h1_ready_act", "h2_ready_act")[i], J, 3, ago=1)
                need(eng, ("h1_ready_dve", "h2_ready_dve")[i], J, 3, ago=1)
                at = J.in_layer(GB)
                name = ("mods1", "mods2")[i]
                eng.tensor_copy(mods[i][:, :, :], mod_main[:, l, 2 * i:2 * i + 2, bass.ds(at, GB)])\
                   .then_inc(S[name], 1)
                eng.tensor_copy(mods_rem[i][:, :, :], mod_rem[:, l, 2 * i:2 * i + 2, bass.ds(at, GB)])\
                   .then_inc(S[name], 1)

            def rstd_of(J, i):
                need(eng, ("n1_var", "n2_var")[i], J, 2)
                need(eng, ("n1_ready", "n2_ready")[i], J, GB - 1, ago=1)
                eng.tensor_tensor(rstd[i][:, :], var[i][:, :], neg_half[:, :], ALU.pow)\
                   .then_inc(S[("n1_rstd", "n2_rstd")[i]], 1)

            def lows(J):
                for T in range(QKT):
                    need(eng, "qk_mid", J, T)
                    if T == 0:
                        need(eng, "parts_stored", J, 2, ago=1)
                    eng.tensor_tensor(part_low[:, T, :], qk_rest[:, T, :], part_mid[:, T, :], ALU.subtract)\
                       .then_inc(S["qk_low"], 1)

            def weight(J, b):
                need(eng, "tok_exp", J, b)
                if b >= 2:
                    need(eng, "tok_values", J, b - 2)
                else:
                    need(eng, "tok_values", J, b + 2, ago=1)
                shape = [128, HEADS, HD, HEADS]
                e = tok_e[:, b % 2, :].rearrange("p (h o k) -> p h o k", h=HEADS, o=1).broadcast_to(shape)
                v = tok_qkv[:, b, 2 * DIM:3 * DIM].rearrange("p (o k d) -> p o d k", o=1, d=HD).broadcast_to(shape)
                eng.tensor_tensor(tok_weighted[b % 2].rearrange("p (h d k) -> p h d k", h=HEADS, d=HD), e, v,
                                  ALU.mult).then_inc(S["tok_weighted"], 1)

            eng.wait_ge(setup["mods_kept"], 2 * LAYERS + 1)
            eng.wait_ge(setup["const"], CONSTS)
            first = Group(0)
            mods_of(first, 0, 0)
            rstd_of(first, 0)
            eng.memset(q_room[:, :], 0.0).then_inc(setup["clear"], 1)
            lows(first)

            def body(G, l, nxt):
                if KINDS[l] == "t":
                    weight(G, 0)
                    weight(G, 1)
                if nxt is not None:
                    mods_of(G.plus(1), nxt, 0)
                    rstd_of(G.plus(1), 0)
                if KINDS[l] == "t":
                    weight(G, 2)
                    weight(G, 3)
                mods_of(G, l, 1)
                if nxt is not None and KINDS[nxt] == "a":
                    lows(G.plus(1))
                rstd_of(G, 1)

            layers(eng, body)

        @block.scalar
        def _(eng):
            start_with(eng, ("h1_ready_act", "h2_ready_act", "qk_high", "v_ready", "mT_copied", "exp_done",
                             "o_copied", "oT_ready", "gelu_ready", "tok_ready", "tok_exp", "qk_sq", "norm_ln", "norm_exp"))
            for h in range(4):
                n = SEQS // 4
                eng.dma_start(x[:, h * n:(h + 1) * n, :], t["x"][h * n:(h + 1) * n].rearrange("b t d -> t b d"))\
                   .then_inc(setup["x"], 16)
            eng.dma_start(part_of[:, :], t["part_of"]).then_inc(setup["staged"], 16)
            eng.wait_ge(setup["stage_clear"], 1)
            for l in range(LAYERS):
                for r in (0, MID_ROW):
                    src = t[f"h_w{l}"][128:DIM, :].rearrange("(o r) n -> o r n", o=1).broadcast_to([3, REM, W_COLS])
                    eng.dma_start(w_stage[l][r:r + 3 * REM, :], src).then_inc(setup["staged"], 16)
                eng.dma_start(w_stage[l][BIAS_ROW:BIAS_ROW + 3, :], t[f"h_w{l}"][DIM, :].partition_broadcast(3))\
                   .then_inc(setup["staged"], 16)
                done = setup["weights" if l else "weights_first"]
                eng.dma_start(w_h[l][:, :], t[f"h_w{l}"][0:128, :]).then_inc(done, 16)
                eng.dma_start(w_o[l][:, :], t[f"o_w{l}"][0:128, :]).then_inc(done, 16)
                eng.dma_start(w_o_rem[l][:, :], t[f"o_w{l}"][128:DIM + 1, :]).then_inc(done, 16)
                eng.dma_start(w_f2[l][:, 0:4, :], t[f"f2_w{l}"][0:512, :].rearrange("(t p) n -> p t n", p=128))\
                   .then_inc(done, 16)
                eng.dma_start(w_f2[l][0:65, 4, :], t[f"f2_w{l}"][512:HIDDEN + 1, :]).then_inc(done, 16)
            eng.wait_ge(setup["c"], 32)
            eng.activation(c_exp[:, 0, :], cT[:, :], ACT.Exp, scale=-1.0).then_inc(setup["c_exp"], 1)
            eng.activation(c_exp_rem[:, 0, :], cT_rem[0:REM, :], ACT.Exp, scale=-1.0)\
               .then_inc(setup["c_exp"], 1)
            for l in range(LAYERS):
                eng.wait_ge(setup["mods_done"], l + 1)
                eng.activation(gate_rows[:, l, :], mod_banks[l][1][0:SEQS, 0:2 * DIM], ACT.Copy if l else ACT.Tanh)\
                   .then_inc(setup["gates_kept"], 1)

            def modulated(J, i, kinds="aa"):
                need(eng, ("mods1", "mods2")[i], J, 1)
                need(eng, ("t1_done", "t2_done")[i], J, 0)
                name, k = h_read_by(i, kinds)
                need(eng, name, J, k, ago=1)
                need(eng, ("h1_parts", "h2_parts")[i], J, 3, ago=1)
                bank = lin[LIN_BANK[("T1_0", "T2_0")[i]]]
                for b in range(2):
                    eng.activation(hT_last[i][:, b * TOK:(b + 1) * TOK], bank[0:REM_ROWS, b * 256 + TOK:(b + 1) * 256],
                                   ACT.Identity, bias=mods_rem[i][:, 0, b:b + 1],
                                   scale=mods_rem[i][:, 1, b:b + 1])\
                       .then_inc(S[("h1_ready_act", "h2_ready_act")[i]], 1)
                for b in range(2):
                    eng.activation(hT[i][:, b * TOK:(b + 1) * TOK], bank[:, b * 256:b * 256 + TOK], ACT.Identity,
                                   bias=mods[i][:, 0, b:b + 1], scale=mods[i][:, 1, b:b + 1])\
                       .then_inc(S[("h1_ready_act", "h2_ready_act")[i]], 1)

            def squares(J, T):
                need(eng, "qk_taken", J, T)
                eng.activation(qk_sq[:, T, :], qk_raw[:, T, :], ACT.Square).then_inc(S["qk_sq"], 1)

            def head_norms(J):
                need(eng, "norm_max", J, 0)
                eng.activation(norm_t[:, 0, :], norm2[:, :], ACT.Ln).then_inc(S["norm_ln"], 1)
                need(eng, "norm_ln", J, 0)
                eng.activation(norm_y[:, 0, :], norm_t[:, 0, :], ACT.Exp, scale=-0.5)\
                   .then_inc(S["norm_exp"], 1)

            def high(J, l, T):
                if T == 0:
                    need(eng, "parts_stored", J, 2, ago=1)
                if l == 0:
                    need(eng, "qk_scaled", J, T)
                    src = qk_fit[:, T, :]
                else:
                    need(eng, "qk_done", J, T)
                    src = lin[LIN_BANK[f"QK{T}"]][0:QKM, :]
                eng.activation(part_high[:, T, :], src, ACT.Copy).then_inc(S["qk_high"], 1)

            def values(J):
                for h in range(2):
                    need(eng, "v_done", J, h)
                    if h == 0:
                        need(eng, "pv_done", J, STEPS - 1, ago=1)
                    bank = lin[LIN_BANK[f"V{h}"]]
                    eng.activation(v_aug[:, 2 * h:2 * h + 2, :, 0:HD],
                                   bank[:, 0:2 * DIM].rearrange("p (b h d) -> p b h d", b=2, d=HD), ACT.Copy)\
                       .then_inc(S["v_ready"], 1)

            def copy_max(J, b):
                need(eng, "mT_done", J, b)
                need(eng, f"m_loaded{b}", J, 1, ago=1)
                eng.activation(max_T[:, b, :], lin_b[LIN_BANK[f"mT{b}"]][0:2 * HEADS, 0:TOK], ACT.Copy)\
                   .then_inc(S["mT_copied"], 1)

            def copy_o(G, b):
                need(eng, "pv_done", G, (b + 1) * CHUNKS - 1)
                if b >= 2:
                    need(eng, "o_tok_done", G, b - 2)
                else:
                    need(eng, "o_tok_done", G, b + 2, ago=1)
                eng.activation(o_feat[:, b % 2, :], o_bank[b % 2][:, :], ACT.Copy).then_inc(S["o_copied"], 1)

            def copy_oT(G, b):
                need(eng, "o_flip_done", G, b)
                if b == 0:
                    need(eng, "proj_done", G, 1, ago=1)
                bank = lin[LIN_BANK[f"OD{b}"]]
                eng.activation(oT_rem[0:REM, b * TOK:(b + 1) * TOK], bank[0:REM, TOK:2 * TOK], ACT.Copy)
                eng.activation(oT[:, b * TOK:(b + 1) * TOK], bank[:, 0:TOK], ACT.Copy).then_inc(S["oT_ready"], 1)

            def token_qkv(J, b):
                need(eng, "tok_done", J, b)
                need(eng, "tok_weighted", J, b, ago=1)
                eng.activation(tok_qkv[:, b, :], lin[LIN_BANK[f"Q{b}"]][:, 0:3 * DIM], ACT.Copy)\
                   .then_inc(S["tok_ready"], 1)

            def token_exp(J, b):
                need(eng, "tok_less", J, b)
                eng.activation(tok_e[:, b % 2, :], tok_less[:, b % 2, :], ACT.Exp, scale=float(HD) ** -0.5)\
                   .then_inc(S["tok_exp"], 1)

            eng.wait_ge(setup["gates_stored"], 16)
            eng.wait_ge(setup["ones"], ONES)
            eng.wait_ge(setup["const"], CONSTS)
            first = Group(0)
            modulated(first, 0)
            for T in range(QKT):
                squares(first, T)
            head_norms(first)
            for T in range(QKT):
                high(first, 0, T)
            values(first)
            copy_max(first, 0)
            copy_max(first, 1)

            def exponentials(G, nxt, kinds):
                copy_max(G, 2)
                for i in range(STEPS):
                    need(eng, "st_done", G, i)
                    if i >= PBUFS:
                        need(eng, "pv_done", G, i - PBUFS)
                    else:
                        need(eng, "pv_done", G, i - PBUFS + STEPS, ago=1)
                    eng.activation(probs[:, i % PBUFS, :], st_bank[i % 2][:, :], ACT.Exp, scale=float(HD) ** -0.5)\
                       .then_inc(S["exp_done"], 1)
                    if i == 4 and nxt is not None:
                        modulated(G.plus(1), 0, kinds)
                    if i == 6:
                        copy_max(G, 3)
                    if i in (7, 9, 11) and kinds[1] == "a":
                        if nxt == 0:
                            squares(G.plus(1), (i - 7) // 2)
                        else:
                            high(G.plus(1), nxt, (i - 7) // 2)
                    if i >= 6 and i % 4 == 2:
                        copy_o(G, (i - 6) // 4)
                    if i >= 10 and i % 4 == 2:
                        copy_oT(G, (i - 10) // 4)
                copy_o(G, 3)

            def body(G, l, nxt):
                kinds = KINDS[l] + (KINDS[nxt] if nxt is not None else "-")
                if KINDS[l] == "a":
                    exponentials(G, nxt, kinds)
                    if nxt == 0:
                        head_norms(G.plus(1))
                else:
                    token_exp(G, 2)
                    token_exp(G, 3)
                    copy_oT(G, 0)
                    copy_oT(G, 1)
                    if nxt is not None:
                        modulated(G.plus(1), 0, kinds)
                copy_oT(G, 2)
                copy_oT(G, 3)
                if kinds[1] == "a":
                    values(G.plus(1))
                    if nxt == 0:
                        for T in range(QKT):
                            high(G.plus(1), 0, T)
                elif kinds[1] == "t":
                    for b in range(GB):
                        token_qkv(G.plus(1), b)
                modulated(G, 1)
                for T in range(FCT):
                    need(eng, "fc1_done", G, T)
                    if T == 0:
                        need(eng, "fc2_done", G, 1, ago=1)
                    m = FCM[T]
                    eng.activation(gelu[0:m, T, :], lin[LIN_BANK[f"F{T}"]][0:m, :],
                                   ACT.Gelu if l == LAYERS - 1 else ACT.Gelu_apprx_tanh)\
                       .then_inc(S["gelu_ready"], 1)
                if kinds[1] == "a":
                    copy_max(G.plus(1), 0)
                    copy_max(G.plus(1), 1)
                elif kinds[1] == "t":
                    token_exp(G.plus(1), 0)
                    token_exp(G.plus(1), 1)

            layers(eng, body)

        @block.vector
        def _(eng):
            start_with(eng, ("h1_parts", "h2_parts", "n1_stats", "n1_aggr", "n1_var", "n1_ready", "n2_stats", "n2_aggr", "n2_var",
                             "n2_ready", "h1_ready_dve", "h2_ready_dve", "qk_taken", "qk_mid", "max_done",
                             "max_high", "max_low", "o_recip", "o_normed", "proj_gated", "x_attn",
                             "mlp_gated", "x_mlp", "tok_prod", "tok_scores", "tok_max", "tok_less", "tok_sum",
                             "tok_recip", "tok_values", "tok_normed", "qk_rest", "norm_max", "norm_y2", "norm_t", "norm_y", "qk_scaled"))
            eng.memset(k_room[:, :], 0.0).then_inc(setup["stage_clear"], 1)
            for buf in (hT_rem[0], hT_rem[1], oT_rem):
                eng.memset(buf[:, :], 1.0).then_inc(setup["ones"], 1)
            eng.memset(gelu[64:128, FCT - 1, :], 1.0).then_inc(setup["ones"], 1)
            eng.memset(v_aug[:, :, :, :], 1.0).then_inc(setup["ones"], 1)
            eng.wait_ge(setup["c_exp"], 2)
            eng.tensor_scalar(c_exp[:, 1, :], c_exp[:, 0, :], 1.0, None, ALU.add).then_inc(setup["silu"], 1)
            eng.tensor_scalar(c_exp_rem[:, 1, :], c_exp_rem[:, 0, :], 1.0, None, ALU.add).then_inc(setup["silu"], 1)
            eng.memset(silu_rem[:, :], 1.0).then_inc(setup["silu"], 1)
            eng.wait_ge(setup["silu"], 3)
            eng.reciprocal(c_exp[:, 0, :], c_exp[:, 1, :]).then_inc(setup["silu"], 1)
            eng.reciprocal(c_exp_rem[:, 0, :], c_exp_rem[:, 1, :]).then_inc(setup["silu"], 1)
            eng.wait_ge(setup["silu"], 5)
            eng.tensor_tensor(silu[:, :], cT[:, :], c_exp[:, 0, :], ALU.mult).then_inc(setup["silu"], 1)
            eng.tensor_tensor(silu_rem[0:REM, :], cT_rem[0:REM, :], c_exp_rem[:, 0, :], ALU.mult)\
               .then_inc(setup["silu"], 1)
            eng.wait_ge(setup["gain"], 64)
            eng.wait_ge(setup["const"], CONSTS)
            eng.tensor_scalar(gain[:, :], gain[:, :], float(DIM) ** 0.5, None, ALU.mult).then_inc(setup["picks"], 1)
            eng.tensor_scalar(spread[:, :], spread[:, :], head_gain[:, 0:1], float(HD) ** 0.5, ALU.mult, ALU.mult)\
               .then_inc(setup["picks"], 1)
            eng.tensor_copy(copier[:, :].rearrange("p (o n) -> p o n", n=REM), ident[0:REM, 0:REM]
                            .rearrange("p (o n) -> p o n", o=1).broadcast_to([REM, COPIES, REM]))\
               .then_inc(setup["picks"], 1)
            eng.wait_ge(setup["picks"], 3)
            for l in range(LAYERS):
                eng.wait_ge(setup["mods_done"], l + 1)
                for main, n, bank in ((mod_main, 128, mod_banks[l][0][:, 0:128]),
                                      (mod_last, REM, mod_banks[l][0][0:REM, 128:256])):
                    v = bank.rearrange("p (i w b) -> p i w b", i=2, w=2)
                    d = main[:, l, :, :].rearrange("p (i w) b -> p i w b", w=2)
                    eng.tensor_copy(d[:, :, 0, :], v[:, :, 0, :])
                    if l:
                        ins = eng.tensor_scalar(d[:, :, 1, :], v[:, :, 1, :], 1.0, None, ALU.add)
                    else:
                        eng.tensor_scalar(d[:, 0, 1, :], v[:, 0, 1, :], 1.0, gain[0:n, 0:1], ALU.add, ALU.mult)
                        ins = eng.tensor_scalar(d[:, 1, 1, :], v[:, 1, 1, :], 1.0, gain[0:n, 1:2], ALU.add, ALU.mult)
                    ins.then_inc(setup["mods_kept"], 1)
            eng.wait_ge(setup["staged"], 16 * (1 + 3 * LAYERS))
            for l in range(LAYERS):
                if l:
                    eng.wait_ge(setup["split"], 7 * l)
                eng.tensor_copy(w_parts[:, 0, :], w_stage[l]).then_inc(setup["split"], 1)
                eng.wait_ge(setup["split"], 7 * l + 1)
                eng.tensor_tensor(w_rest, w_stage[l], w_parts[:, 0, :], ALU.subtract).then_inc(setup["split"], 1)
                eng.tensor_scalar(w_h_rem[l][:, :], w_parts[:, 0, :], part_of[:, 0:1], None, ALU.mult)\
                   .then_inc(setup["split"], 1)
                eng.wait_ge(setup["split"], 7 * l + 3)
                eng.tensor_copy(w_parts[:, 1, :], w_rest).then_inc(setup["split"], 1)
                eng.wait_ge(setup["split"], 7 * l + 4)
                eng.tensor_tensor(w_rest, w_rest, w_parts[:, 1, :], ALU.subtract).then_inc(setup["split"], 1)
                eng.scalar_tensor_tensor(out=w_h_rem[l][:, :], in0=w_parts[:, 1, :], scalar=part_of[:, 1:2],
                                         in1=w_h_rem[l][:, :], op0=ALU.mult, op1=ALU.add)\
                   .then_inc(setup["split"], 1)
                eng.wait_ge(setup["split"], 7 * l + 6)
                eng.scalar_tensor_tensor(out=w_h_rem[l][:, :], in0=w_rest, scalar=part_of[:, 2:3],
                                         in1=w_h_rem[l][:, :], op0=ALU.mult, op1=ALU.add)\
                   .then_inc(setup["split"], 1)
            eng.wait_ge(setup["mods_done"], LAYERS + 1)
            eng.tensor_copy(mod_rem[:, :, :, :].rearrange("p l i b -> p (l i b)"), lin[0][0:REM_ROWS, :])\
               .then_inc(setup["mods_kept"], 1)
            eng.wait_ge(setup["split"], 7 * LAYERS)
            eng.memset(k_room[:, :].bitcast(BF16), -1.0).then_inc(setup["ones"], 1)
            eng.wait_ge(setup["mods_kept"], 2 * LAYERS + 1)

            def stand_alone(eng):
                eng.sem_inc(setup["carrier"], 1)

            def statistics(J, l, i):
                pre = ("n1", "n2")[i]
                if i == 0:
                    need(eng, "x_mlp", J, 1, ago=2)
                else:
                    need(eng, "x_attn", J, 1)
                need(eng, pre + "_ready", J, GB - 1, ago=1)
                stand_alone(eng)
                for b in range(GB):
                    eng.bn_stats(stats[i][:, b, :], x[:, bass.ds(J.in_layer(GB) + b, 1), :].rearrange("p o d -> p (o d)"))\
                       .then_inc(S[pre + "_stats"], 1)
                need(eng, pre + "_stats", J, GB - 1)
                stand_alone(eng)
                for b in range(GB):
                    eng.bn_aggr(moments[i][:, b, :], stats[i][:, b, :]).then_inc(S[pre + "_aggr"], 1)
                need(eng, pre + "_aggr", J, GB - 1)
                if l == 0:
                    eng.tensor_tensor(mean_sq[:, 0, :], moments[i][:, :, 0], moments[i][:, :, 0], ALU.mult)\
                       .then_inc(S[pre + "_var"], 1)
                    need(eng, pre + "_var", J, 0)
                    eng.tensor_tensor(mean_sq[:, 1, :], mean_sq[:, 0, :], moments[i][:, :, 1], ALU.add)\
                       .then_inc(S[pre + "_var"], 1)
                    need(eng, pre + "_var", J, 1)
                    eng.tensor_scalar(var[i][:, :], mean_sq[:, 1, :], float(DIM), 1e-24, ALU.mult, ALU.max)\
                       .then_inc(S[pre + "_var"], 1)
                else:
                    eng.tensor_scalar(var[i][:, :], moments[i][:, :, 1], 1e-6, None, ALU.add)\
                       .then_inc(S[pre + "_var"], 3)

            def normalise(J, l, i):
                pre = ("n1", "n2")[i]
                need(eng, pre + "_rstd", J, 0)
                need(eng, ("t1_done", "t2_done")[i], J, 1, ago=1)
                for b in range(GB):
                    src = x[:, bass.ds(J.in_layer(GB) + b, 1), :].rearrange("p o d -> p (o d)")
                    if l == 0:
                        ins = eng.tensor_scalar(normed[i][:, b, :], src, rstd[i][:, b:b + 1], None, ALU.mult)
                    else:
                        ins = eng.tensor_scalar(normed[i][:, b, :], src, moments[i][:, b, 0:1], rstd[i][:, b:b + 1],
                                                ALU.subtract, ALU.mult)
                    ins.then_inc(S[pre + "_ready"], 1)
                need(eng, pre + "_ready", J, GB - 1)
                eng.tensor_copy(normed_last[i][:, :, :].rearrange("p b (o n) -> p b o n", n=REM),
                                normed[i][:, :, 128:DIM].rearrange("p b (o n) -> p b o n", o=1)
                                .broadcast_to([128, GB, COPIES, REM])).then_inc(S[pre + "_ready"], 1)

            def modulated(J, i, kinds="aa"):
                need(eng, ("mods1", "mods2")[i], J, 1)
                need(eng, ("t1_done", "t2_done")[i], J, 1)
                name, k = h_read_by(i, kinds)
                need(eng, name, J, k, ago=1)
                ready = S[("h1_ready_dve", "h2_ready_dve")[i]]
                bank = lin[LIN_BANK[("T1_1", "T2_1")[i]]]
                for b in range(2, 4):
                    c = (b - 2) * 256
                    eng.tensor_scalar(hT_last[i][:, b * TOK:(b + 1) * TOK], bank[0:REM_ROWS, c + TOK:c + 2 * TOK],
                                      mods_rem[i][:, 1, b:b + 1], mods_rem[i][:, 0, b:b + 1], ALU.mult, ALU.add)\
                       .then_inc(ready, 1)
                for b in range(2, 4):
                    c = (b - 2) * 256
                    eng.tensor_scalar(hT[i][:, b * TOK:(b + 1) * TOK], bank[:, c:c + TOK],
                                      mods[i][:, 1, b:b + 1], mods[i][:, 0, b:b + 1], ALU.mult, ALU.add)\
                       .then_inc(ready, 1)
                done, other = ("h1_parts", "h2_parts")[i], ("h2_parts", "h1_parts")[i]
                need(eng, ("h1_ready_act", "h2_ready_act")[i], J, 1)
                need(eng, ("h1_ready_dve", "h2_ready_dve")[i], J, 1)
                eng.tensor_copy(hT_rem[i][0:BIAS_ROW, :], hT_last[i][0:BIAS_ROW, :])
                eng.tensor_copy(hT_rem[i][MID_ROW:REM_ROWS, :], hT_last[i][MID_ROW:REM_ROWS, :]).then_inc(S[done], 1)
                need(eng, done, J, 0)
                need(eng, other, J, 3, ago=2 if i == 0 else 0)
                eng.tensor_tensor(h_rest[MID_ROW:REM_ROWS, :], hT_last[i][MID_ROW:REM_ROWS, :],
                                  hT_rem[i][MID_ROW:REM_ROWS, :], ALU.subtract).then_inc(S[done], 1)
                need(eng, done, J, 1)
                eng.tensor_copy(hT_rem[i][MID_ROW:REM_ROWS, :], h_rest[MID_ROW:REM_ROWS, :]).then_inc(S[done], 1)
                need(eng, done, J, 2)
                eng.tensor_tensor(hT_rem[i][LOW_ROW:REM_ROWS, :], h_rest[LOW_ROW:REM_ROWS, :],
                                  hT_rem[i][LOW_ROW:REM_ROWS, :], ALU.subtract).then_inc(S[done], 1)

            def raw(J, T):
                need(eng, "qk_done", J, T)
                if T == 0:
                    need(eng, "qk_scaled", J, QKT - 1, ago=1)
                    need(eng, "qk_sq", J, QKT - 1, ago=1)
                eng.tensor_copy(qk_raw[:, T, :], lin[LIN_BANK[f"QK{T}"]][0:QKM, :]).then_inc(S["qk_taken"], 1)

            def head_norms(J):
                need(eng, "norm_done", J, 0)
                need(eng, "norm_y", J, 0, ago=1)
                eng.tensor_scalar(norm2[:, :], st_bank[0][0:2 * HEADS, :], 1e-24, None, ALU.max)\
                   .then_inc(S["norm_max"], 1)
                need(eng, "norm_exp", J, 0)
                eng.tensor_tensor(norm_t[:, 1, :], norm_y[:, 0, :], norm_y[:, 0, :], ALU.mult)\
                   .then_inc(S["norm_y2"], 1)
                need(eng, "norm_y2", J, 0)
                eng.scalar_tensor_tensor(out=norm_t[:, 0, :], in0=norm_t[:, 1, :], scalar=-0.5,
                                         in1=norm2[:, :], op0=ALU.mult, op1=ALU.mult)\
                   .then_inc(S["norm_t"], 1)
                need(eng, "norm_t", J, 0)
                need(eng, "spread_done", J, QKT - 1, ago=1)
                eng.scalar_tensor_tensor(out=norm_y[:, 1, :], in0=norm_t[:, 0, :], scalar=1.5,
                                         in1=norm_y[:, 0, :], op0=ALU.add, op1=ALU.mult)\
                   .then_inc(S["norm_y"], 1)

            def fit(J):
                for T in range(QKT):
                    need(eng, "spread_done", J, T)
                    if T == 0:
                        need(eng, "qk_mid", J, QKT - 1, ago=1)
                    eng.tensor_tensor(qk_fit[:, T, :], qk_raw[:, T, :], st_bank[(T + 1) % 2][0:QKM, :], ALU.mult)\
                       .then_inc(S["qk_scaled"], 1)

            def mid(J, l, T):
                need(eng, "qk_high", J, T)
                if T == 0:
                    need(eng, "qk_low", J, QKT - 1, ago=1)
                if l == 0:
                    eng.tensor_tensor(qk_rest[:, T, :], qk_fit[:, T, :], part_high[:, T, :], ALU.subtract)\
                       .then_inc(S["qk_rest"], 1)
                else:
                    eng.tensor_tensor(qk_rest[:, T, :], lin[LIN_BANK[f"QK{T}"]][0:QKM, :],
                                      part_high[:, T, :], ALU.subtract).then_inc(S["qk_taken"], 1)
                need(eng, "qk_rest" if l == 0 else "qk_taken", J, T)
                if T == 0:
                    need(eng, "parts_stored", J, 2, ago=1)
                eng.tensor_copy(part_mid[:, T, :], qk_rest[:, T, :]).then_inc(S["qk_mid"], 1)

            def maximum(J, i):
                b, c = divmod(i, CHUNKS)
                need(eng, "score_done", J, i)
                if c == 0:
                    need(eng, "max_low", J, b, ago=1)
                eng.tensor_reduce(maxima[:, b, CH * c:CH * c + CH],
                                  score_bank[i % 2][:, :].rearrange("p (h k) -> p h k", h=CH), AX_X, ALU.max)\
                   .then_inc(S["max_done"], 1)

            def split_max(J, b):
                need(eng, "max_done", J, (b + 1) * CHUNKS - 1)
                need(eng, "mT_done", J, b, ago=1)
                eng.tensor_copy(max_parts[:, b, 0, :], maxima[:, b, :]).then_inc(S["max_high"], 1)
                need(eng, "max_high", J, b)
                eng.tensor_tensor(max_parts[:, b, 1, :], maxima[:, b, :], max_parts[:, b, 0, :], ALU.subtract)\
                   .then_inc(S["max_low"], 1)

            def divide(G, b):
                need(eng, "o_tok_done", G, b)
                o = o_bank[b % 2][:, :].rearrange("p (h r) -> p h r", r=32)
                if b >= 2:
                    need(eng, "o_normed", G, b - 2)
                    need(eng, "o_flip_done", G, b - 2)
                else:
                    need(eng, "o_normed", G, b + 2, ago=1)
                    need(eng, "o_flip_done", G, b + 2, ago=1)
                eng.reciprocal(o_recip[:, b % 2, :].rearrange("p (h r) -> p h r", r=1), o[:, :, HD:HD + 1])\
                   .then_inc(S["o_recip"], 1)
                need(eng, "o_recip", G, b)
                eng.tensor_tensor(o_tok[:, b % 2, :].rearrange("p (h d) -> p h d", d=HD), o[:, :, 0:HD],
                                  o_recip[:, b % 2, :].rearrange("p (h r) -> p h r", r=1)
                                  .broadcast_to([128, HEADS, HD]), ALU.mult).then_inc(S["o_normed"], 1)

            def residual(G, h, which):
                done, gated_name, x_name, use = (
                    ("proj_done", "proj_gated", "x_attn", "PJ"), ("fc2_done", "mlp_gated", "x_mlp", "M"))[which]
                need(eng, done, G, h)
                if h == 0 and which == 0:
                    need(eng, "gates_loaded", G, 1)
                if which == 0:
                    need(eng, "x_mlp", G, h, ago=1)
                    need(eng, "n1_ready", G, GB - 1)
                else:
                    need(eng, "x_attn", G, h)
                    need(eng, "n2_ready", G, GB - 1)
                eng.tensor_tensor(gated[:, h, :], lin[LIN_BANK[f"{use}{h}"]][:, 0:2 * DIM],
                                  gates[:, which, 2 * h:2 * h + 2, :].rearrange("p b n -> p (b n)"), ALU.mult)\
                   .then_inc(S[gated_name], 1)
                need(eng, gated_name, G, h)
                xs = x[:, bass.ds(G.in_layer(GB) + 2 * h, 2), :].rearrange("p b n -> p (b n)")
                eng.tensor_tensor(xs, xs, gated[:, h, :], ALU.add).then_inc(S[x_name], 1)

            def token_scores(J, b):
                need(eng, "tok_ready", J, b)
                if b:
                    need(eng, "tok_scores", J, b - 1)
                else:
                    need(eng, "tok_scores", J, GB - 1, ago=1)
                shape = [128, HEADS, HEADS, HD]
                q = tok_qkv[:, b, 0:DIM].rearrange("p (h o d) -> p h o d", o=1, d=HD).broadcast_to(shape)
                k = tok_qkv[:, b, DIM:2 * DIM].rearrange("p (o k d) -> p o k d", o=1, d=HD).broadcast_to(shape)
                prod = tok_prod.rearrange("p (h k d) -> p h k d", h=HEADS, d=HD)
                eng.tensor_tensor(prod, q, k, ALU.mult).then_inc(S["tok_prod"], 1)
                need(eng, "tok_prod", J, b)
                if b >= 2:
                    need(eng, "tok_weighted", J, b - 2)
                    need(eng, "tok_sum", J, b - 2)
                else:
                    need(eng, "tok_weighted", J, b + 2, ago=1)
                    need(eng, "tok_sum", J, b + 2, ago=1)
                e = tok_e[:, b % 2, :]
                eng.tensor_reduce(e, tok_prod.rearrange("p (s d) -> p s d", d=HD), AX_X, ALU.add)\
                   .then_inc(S["tok_scores"], 1)
                need(eng, "tok_scores", J, b)
                e3 = e.rearrange("p (h k) -> p h k", h=HEADS)
                eng.tensor_reduce(tok_small[:, b % 2, :], e3, AX_X, ALU.max).then_inc(S["tok_max"], 1)
                need(eng, "tok_max", J, b)
                eng.tensor_tensor(tok_less[:, b % 2, :].rearrange("p (h k) -> p h k", h=HEADS), e3,
                                  tok_small[:, b % 2, :].rearrange("p (h o) -> p h o", o=1)
                                  .broadcast_to([128, HEADS, HEADS]), ALU.subtract).then_inc(S["tok_less"], 1)

            def token_values(J, b):
                need(eng, "tok_exp", J, b)
                eng.tensor_reduce(tok_small[:, 2 + b % 2, :], tok_e[:, b % 2, :].rearrange("p (h k) -> p h k", h=HEADS),
                                  AX_X, ALU.add).then_inc(S["tok_sum"], 1)
                need(eng, "tok_sum", J, b)
                eng.reciprocal(tok_small[:, 4 + b % 2, :], tok_small[:, 2 + b % 2, :]).then_inc(S["tok_recip"], 1)
                need(eng, "tok_weighted", J, b)
                eng.tensor_reduce(tok_o[:, b % 2, :], tok_weighted[b % 2].rearrange("p (s k) -> p s k", k=HEADS),
                                  AX_X, ALU.add).then_inc(S["tok_values"], 1)
                need(eng, "tok_recip", J, b)
                need(eng, "tok_values", J, b)
                if b >= 2:
                    need(eng, "mixed_stored", J, b - 2)
                else:
                    need(eng, "mixed_stored", J, b + 2, ago=1)
                eng.tensor_tensor(tok_o[:, 2 + b % 2, :].rearrange("p (h d) -> p h d", d=HD),
                                  tok_o[:, b % 2, :].rearrange("p (h d) -> p h d", d=HD),
                                  tok_small[:, 4 + b % 2, :].rearrange("p (h o) -> p h o", o=1)
                                  .broadcast_to([128, HEADS, HD]), ALU.mult).then_inc(S["tok_normed"], 1)

            eng.wait_ge(setup["x"], 64)
            first = Group(0)
            statistics(first, 0, 0)
            normalise(first, 0, 0)
            modulated(first, 0)
            for T in range(QKT):
                raw(first, T)
            head_norms(first)
            fit(first)
            for T in range(QKT):
                mid(first, 0, T)
            for i in range(AHEAD):
                maximum(first, i)
                if i % CHUNKS == CHUNKS - 1:
                    split_max(first, i // CHUNKS)

            def body(G, l, nxt):
                J = G.plus(1)
                kinds = KINDS[l] + (KINDS[nxt] if nxt is not None else "-")
                if kinds[0] == "a":
                    if nxt is not None:
                        statistics(J, nxt, 0)
                    for i in range(AHEAD, STEPS):
                        maximum(G, i)
                    split_max(G, GB - 1)
                    if nxt is not None:
                        normalise(J, nxt, 0)
                        modulated(J, 0, kinds)
                    for T in range(QKT):
                        if kinds[1] == "a":
                            if nxt == 0:
                                raw(J, T)
                            else:
                                mid(J, nxt, T)
                        if T == 0:
                            divide(G, 0)
                    divide(G, 1)
                    divide(G, 2)
                    divide(G, 3)
                    if nxt == 0:
                        head_norms(J)
                else:
                    token_values(G, 0)
                    token_scores(G, 2)
                    if nxt is not None:
                        statistics(J, nxt, 0)
                    token_values(G, 1)
                    token_scores(G, 3)
                    if nxt is not None:
                        normalise(J, nxt, 0)
                    token_values(G, 2)
                    if nxt is not None:
                        modulated(J, 0, kinds)
                    token_values(G, 3)
                residual(G, 0, 0)
                residual(G, 1, 0)
                statistics(G, l, 1)
                if nxt == 0:
                    fit(J)
                    for T in range(QKT):
                        mid(J, 0, T)
                normalise(G, l, 1)
                modulated(G, 1)
                if kinds[1] == "a":
                    for i in range(AHEAD):
                        maximum(J, i)
                        if i % CHUNKS == CHUNKS - 1:
                            split_max(J, i // CHUNKS)
                        if i == 2 * CHUNKS - 1:
                            residual(G, 0, 1)
                elif kinds[1] == "t":
                    token_scores(J, 0)
                    token_scores(J, 1)
                if kinds[1] != "a":
                    residual(G, 0, 1)
                residual(G, 1, 1)

            layers(eng, body)

        @block.tensor
        def _(eng):
            start_with(eng, ("t1_done", "t2_done", "qk_done", "v_done", "score_done", "mT_done", "st_done",
                             "pv_done", "o_tok_done", "o_flip_done", "proj_done", "fc1_done", "fc2_done",
                             "tok_done", "norm_done", "spread_done"))

            def bank_of(use, J, this, nxt):
                before, turns = use_before(use, this, nxt)
                if before is not None:
                    _, name, k = LIN_USES[before]
                    need(eng, name, J, k, ago=(use in OF_NEXT) - (before in OF_NEXT) + turns)
                return lin[LIN_BANK[use]]

            eng.wait_ge(setup["silu"], 7)
            for l in range(LAYERS):
                eng.wait_ge(setup[f"ada{l}"], 32)
                shifts, rows = mod_banks[l]
                for j, k in enumerate((0, 1, 3, 4)):
                    for m, c0, c1 in ((128, 0, k * DIM), (REM, 128, k * DIM + 128)):
                        o = shifts[0:m, c0 + j * SEQS:c0 + (j + 1) * SEQS]
                        eng.matmul(o, w_ada[l][:, c1:c1 + m], silu[:, :], start=True, stop=False)
                        eng.matmul(o, w_ada_rem[l][:, c1:c1 + m], silu_rem[:, :], start=False, stop=True)
                for w in range(2):
                    o = rows[0:SEQS, w * DIM:(w + 1) * DIM]
                    c1 = (2 + 3 * w) * DIM
                    eng.matmul(o, silu[:, :], w_ada[l][:, c1:c1 + DIM], start=True, stop=False)
                    ins = eng.matmul(o, silu_rem[:, :], w_ada_rem[l][:, c1:c1 + DIM], start=False, stop=True)
                ins.then_inc(setup["mods_done"], 1)
            eng.wait_ge(setup["mods_kept"], 2 * LAYERS)
            eng.matmul(lin[0][0:REM_ROWS, :], copier[:, :], mod_last[:, :, :, :].rearrange("p l i b -> p (l i b)"),
                       start=True, stop=True).then_inc(setup["mods_done"], 1)

            def flip_rows(J, i, h, **turn):
                use = ("T1_", "T2_")[i] + str(h)
                need(eng, ("n1_ready", "n2_ready")[i], J, GB)
                bank = bank_of(use, J, **turn)
                for b in (0, 1):
                    src = normed[i][:, 2 * h + b, :]
                    eng.transpose(bank[:, b * 256:b * 256 + TOK], src[:, 0:128], ident[:, :])
                    ins = eng.transpose(bank[0:REM_ROWS, b * 256 + TOK:(b + 1) * 256],
                                        normed_last[i][:, 2 * h + b, :], ident[:, :])
                ins.then_inc(S[("t1_done", "t2_done")[i]], 1)

            def queries_keys(J, l, T, **turn):
                if T == 0:
                    need(eng, "h1_ready_act", J, 3)
                    need(eng, "h1_ready_dve", J, 3)
                bank = bank_of(f"QK{T}", J, **turn)[0:QKM, :]
                cols = slice(W_QK + T * QKM, W_QK + (T + 1) * QKM)
                eng.matmul(bank, w_h[l][:, cols], hT[0][:, :], start=True, stop=False)
                if T == 0:
                    need(eng, "h1_parts", J, 3)
                eng.matmul(bank, w_h_rem[l][:, cols], hT_rem[0][:, :], start=False, stop=True)\
                   .then_inc(S["qk_done"], 1)

            def head_norms(J):
                need(eng, "exp_done", J, STEPS - 1, ago=1)
                for T in range(QKT):
                    need(eng, "qk_sq", J, T)
                    ins = eng.matmul(st_bank[0][0:2 * HEADS, :], pick[:, T, :], qk_sq[:, T, :], start=T == 0,
                                     stop=T == QKT - 1)
                ins.then_inc(S["norm_done"], 1)

            def spread_norms(J):
                need(eng, "norm_y", J, 0)
                for T in range(QKT):
                    if T == 2:
                        need(eng, "qk_scaled", J, 0)
                    eng.matmul(st_bank[(T + 1) % 2][0:QKM, :], spread[:, T * QKM:(T + 1) * QKM], norm_y[:, 1, :],
                               start=True, stop=True).then_inc(S["spread_done"], 1)

            def values(J, l, h, **turn):
                bank = bank_of(f"V{h}", J, **turn)
                for b in range(2):
                    tok = slice((2 * h + b) * TOK, (2 * h + b + 1) * TOK)
                    o = bank[:, b * DIM:(b + 1) * DIM]
                    cols = slice(W_V, W_V + DIM)
                    eng.matmul(o, hT[0][:, tok], w_h[l][:, cols], start=True, stop=False)
                    ins = eng.matmul(o, hT_rem[0][:, tok], w_h_rem[l][:, cols], start=False, stop=True)
                ins.then_inc(S["v_done"], 1)

            def scores(J, i):
                b, c = divmod(i, CHUNKS)
                if i == 0:
                    need(eng, "stack_loaded", J, 5)
                if i >= 2:
                    need(eng, "max_done", J, i - 2)
                else:
                    need(eng, "max_done", J, i - 2 + STEPS, ago=1)
                tok = slice(b * TOK, (b + 1) * TOK)
                for j in range(CH):
                    h = CH * c + j
                    ins = eng.matmul(score_bank[i % 2][:, j * TOK:(j + 1) * TOK], q_stack[0:SCORE_ROWS, h, tok],
                                     k_stack[0:SCORE_ROWS, h, tok], start=True, stop=True)
                ins.then_inc(S["score_done"], 1)

            def flip_max(J, b, **turn):
                need(eng, "max_low", J, b)
                bank_of(f"mT{b}", J, **turn)
                eng.transpose(lin_b[LIN_BANK[f"mT{b}"]][0:2 * HEADS, 0:TOK],
                              max_parts[:, b, :, :].rearrange("p i h -> p (i h)"), ident_b[:, :])\
                   .then_inc(S["mT_done"], 1)

            def shifted_scores(G, i):
                b, c = divmod(i, CHUNKS)
                if c == 0:
                    need(eng, f"m_loaded{b}", G, 1)
                if i >= 2:
                    need(eng, "exp_done", G, i - 2)
                else:
                    need(eng, "exp_done", G, i - 2 + STEPS, ago=1)
                tok = slice(b * TOK, (b + 1) * TOK)
                for j in range(CH):
                    h = CH * c + j
                    ins = eng.matmul(st_bank[i % 2][:, j * TOK:(j + 1) * TOK], k_stack[:, h, tok],
                                     q_stack[:, h, tok], start=True, stop=True)
                ins.then_inc(S["st_done"], 1)

            def weighted_values(G, i):
                b, c = divmod(i, CHUNKS)
                need(eng, "exp_done", G, i)
                if c == 0:
                    need(eng, "v_ready", G, b // 2)
                    if b >= 2:
                        need(eng, "o_normed", G, b - 2)
                    else:
                        need(eng, "o_normed", G, b + 2, ago=1)
                for j in range(CH):
                    ins = eng.matmul(o_bank[b % 2][32 * j:32 * j + 32, c * TOK:(c + 1) * TOK],
                                     v_aug[:, b, CH * c + j, :], probs[:, i % PBUFS, j * TOK:(j + 1) * TOK],
                                     start=True, stop=True)
                ins.then_inc(S["pv_done"], 1)

            def o_to_tokens(G, b):
                need(eng, "o_copied", G, b)
                for c in range(CHUNKS):
                    ins = eng.transpose(o_bank[b % 2][:, c * TOK:(c + 1) * TOK],
                                        o_feat[:, b % 2, c * TOK:(c + 1) * TOK], ident[:, :])
                ins.then_inc(S["o_tok_done"], 1)

            def flip_o(G, b, **turn):
                if turn["this"] == "a":
                    need(eng, "o_normed", G, b)
                    src = o_tok[:, b % 2, :]
                else:
                    need(eng, f"mixed{b}", G, 0)
                    src = mixed[:, b, :]
                bank = bank_of(f"OD{b}", G, **turn)
                eng.transpose(bank[:, 0:TOK], src[:, 0:128], ident[:, :])
                eng.transpose(bank[0:REM, TOK:2 * TOK], src[:, 128:DIM], ident[:, :])\
                   .then_inc(S["o_flip_done"], 1)

            def token_qkv(J, l, b, **turn):
                if b == 0:
                    need(eng, "h1_ready_act", J, 3)
                    need(eng, "h1_ready_dve", J, 3)
                bank = bank_of(f"Q{b}", J, **turn)
                tok = slice(b * TOK, (b + 1) * TOK)
                eng.matmul(bank[:, 0:3 * DIM], hT[0][:, tok], w_h[l][:, 0:3 * DIM], start=True, stop=False)
                if b == 0:
                    need(eng, "h1_parts", J, 3)
                eng.matmul(bank[:, 0:3 * DIM], hT_rem[0][:, tok], w_h_rem[l][:, 0:3 * DIM], start=False, stop=True)\
                   .then_inc(S["tok_done"], 1)

            def project(G, l, h, **turn):
                need(eng, "oT_ready", G, 2 * h + 1)
                bank = bank_of(f"PJ{h}", G, **turn)
                for b in range(2):
                    tok = slice((2 * h + b) * TOK, (2 * h + b + 1) * TOK)
                    o = bank[:, b * DIM:(b + 1) * DIM]
                    eng.matmul(o, oT[:, tok], w_o[l][:, :], start=True, stop=False)
                    ins = eng.matmul(o, oT_rem[:, tok], w_o_rem[l][:, :], start=False, stop=True)
                ins.then_inc(S["proj_done"], 1)

            def up(G, l, T, **turn):
                def piece(T, w, h, **flags):
                    cols = slice(W_F1 + T * 128, W_F1 + T * 128 + FCM[T])
                    return eng.matmul(lin[LIN_BANK[f"F{T}"]][0:FCM[T], :], w[:, cols], h, **flags)

                if T == 0:
                    need(eng, "h2_ready_act", G, 3)
                    need(eng, "h2_ready_dve", G, 3)
                if T != 1:
                    bank_of(f"F{T}", G, **turn)
                    piece(T, w_h[l], hT[1][:, :], start=True, stop=False)
                if T == 0:
                    bank_of("F1", G, **turn)
                    piece(1, w_h[l], hT[1][:, :], start=True, stop=False)
                    need(eng, "h2_parts", G, 3)
                piece(T, w_h_rem[l], hT_rem[1][:, :], start=False, stop=True).then_inc(S["fc1_done"], 1)

            def down(G, l, bank, b):
                o = bank[:, (b % 2) * DIM:(b % 2 + 1) * DIM]
                for T in range(FCT):
                    if b == 0:
                        need(eng, "gelu_ready", G, T)
                    k = 128 if T < FCT - 1 else FCM[T] + 1
                    ins = eng.matmul(o, gelu[0:k, T, b * TOK:(b + 1) * TOK], w_f2[l][0:k, T, :], start=T == 0,
                                     stop=T == FCT - 1)
                return ins

            eng.wait_ge(setup["weights_first"], 16 * 5)
            eng.wait_ge(setup["split"], 7 * LAYERS)
            eng.wait_ge(setup["clear"], 1)
            eng.wait_ge(setup["mods_kept"], 2 * LAYERS + 1)
            eng.wait_ge(setup["gates_kept"], LAYERS)
            eng.wait_ge(setup["ones"], ONES)
            eng.wait_ge(setup["const"], CONSTS)
            eng.wait_ge(setup["picks"], 3)
            start = dict(this=None, nxt="a")
            first = Group(0)
            flip_rows(first, 0, 0, **start)
            flip_rows(first, 0, 1, **start)
            for T in range(QKT):
                queries_keys(first, 0, T, **start)
            head_norms(first)
            spread_norms(first)
            values(first, 0, 0, **start)
            values(first, 0, 1, **start)
            for i in range(AHEAD):
                scores(first, i)
            flip_max(first, 0, **start)
            flip_max(first, 1, **start)

            def body(G, l, nxt):
                J = G.plus(1)
                turn = dict(this=KINDS[l], nxt=None if nxt is None else KINDS[nxt])
                this, nxt_kind = turn["this"], turn["nxt"]
                if this == "a":
                    flip_max(G, 2, **turn)
                    for i in range(STEPS + LAG):
                        if i < STEPS:
                            shifted_scores(G, i)
                            if i + AHEAD < STEPS:
                                scores(G, i + AHEAD)
                        if i >= LAG:
                            weighted_values(G, i - LAG)
                        if i == 3 and nxt is not None:
                            flip_rows(J, 0, 0, **turn)
                            flip_rows(J, 0, 1, **turn)
                        if i == 5:
                            flip_max(G, 3, **turn)
                        if i in (6, 8, 10) and nxt_kind == "a":
                            queries_keys(J, nxt, (i - 6) // 2, **turn)
                        if i in (7, 11, 15):
                            o_to_tokens(G, i // 4 - 1)
                        if i in (9, 13):
                            flip_o(G, i // 4 - 2, **turn)
                    if nxt == 0:
                        head_norms(J)
                    flip_o(G, 2, **turn)
                    o_to_tokens(G, 3)
                else:
                    flip_o(G, 0, **turn)
                    flip_o(G, 1, **turn)
                    if nxt is not None:
                        flip_rows(J, 0, 0, **turn)
                        flip_rows(J, 0, 1, **turn)
                    flip_o(G, 2, **turn)
                    flip_o(G, 3, **turn)
                project(G, l, 0, **turn)
                if this == "a":
                    flip_o(G, 3, **turn)
                if nxt_kind == "a":
                    values(J, nxt, 0, **turn)
                project(G, l, 1, **turn)
                if nxt_kind == "a":
                    values(J, nxt, 1, **turn)
                elif nxt_kind == "t":
                    for b in range(GB):
                        token_qkv(J, nxt, b, **turn)
                if nxt == 0:
                    spread_norms(J)
                flip_rows(G, 1, 0, **turn)
                flip_rows(G, 1, 1, **turn)
                for T in range(FCT):
                    up(G, l, T, **turn)
                    if T > 0 and nxt_kind == "a":
                        scores(J, T - 1)
                for h in range(2):
                    bank = bank_of(f"M{h}", G, **turn)
                    for b in (2 * h, 2 * h + 1):
                        if nxt_kind == "a":
                            scores(J, CHUNKS + 2 * b)
                        ins = down(G, l, bank, b)
                        if nxt_kind == "a":
                            scores(J, CHUNKS + 2 * b + 1)
                            if b == 0:
                                flip_max(J, 0, **turn)
                    ins.then_inc(S["fc2_done"], 1)
                if nxt_kind == "a":
                    flip_max(J, 1, **turn)

            eng.wait_ge(setup["weights"], 16 * 5 * (LAYERS - 1))
            layers(eng, body)


def kernel(**inputs):
    import numpy as np
    import concourse.bacc as bacc
    from concourse.bass_utils import run_bass_kernel_spmd

    names = {
        0: ("qkv_w", "qkv_b", "proj_w", "proj_b", "fc1_w", "fc1_b", "fc2_w", "fc2_b", "ada_w", "ada_b"),
        1: ("w_qkv", "b_qkv", "w_proj", "b_proj", "w_fc1", "b_fc1", "w_fc2", "b_fc2", "w_ada", "b_ada"),
        2: ("qkv_w", "qkv_b", "out_w", "out_b", "w1", "b1", "w2", "b2", "ada_w", "ada_b"),
        3: ("qkv_w", "qkv_b", "proj_w", "proj_b", "fc1_w", "fc1_b", "fc2_w", "fc2_b", "ada_w", "ada_b"),
    }
    mine = ("qkv_w", "qkv_b", "o_w", "o_b", "f1_w", "f1_b", "f2_w", "f2_b", "ada_w", "ada_b")
    arrays = {"x": inputs["x"], "cT": np.asarray(inputs["cond_1152"]).T}
    part_of = np.zeros((128, 3), np.float32)
    for part, rows in enumerate(((0, MID_ROW, LOW_ROW), (REM, MID_ROW + REM), (2 * REM,))):
        for r in rows:
            part_of[r:r + REM, part] = 1
        part_of[BIAS_ROW + part, part] = 1
    arrays["part_of"] = part_of
    for short in ("g1", "g2", "qg", "kg"):
        arrays[short] = inputs[f"L0_cond_{short}"]
    for l, theirs in names.items():
        w = {}
        for a, b in zip(mine, theirs):
            w[a] = np.asarray(inputs[f"L{l}_cond_{b}"])
            w[a] = w[a].T if l == 0 and w[a].ndim == 2 else w[a]
        full = {a: np.concatenate([w[f"{a}_w"], w[f"{a}_b"][None]]) for a in ("qkv", "o", "f1", "f2", "ada")}
        qk, v = full["qkv"][:, :2 * DIM], full["qkv"][:, 2 * DIM:]
        if KINDS[l] == "a":
            qk = np.swapaxes(qk.reshape(DIM + 1, 2, HEADS, HD), -1, -2).reshape(qk.shape)
        arrays[f"h_w{l}"] = np.concatenate([qk, v, full["f1"]], axis=1)
        arrays[f"o_w{l}"], arrays[f"f2_w{l}"], arrays[f"ada{l}"] = full["o"], full["f2"], full["ada"]

    nc = bacc.Bacc("TRN2", target_bir_lowering=False, num_devices=1)
    feeds, aps = {}, {}
    for name, a in arrays.items():
        a = np.ascontiguousarray(a)
        feeds[f"in_{name}"] = a
        aps[name] = nc.dram_tensor(f"in_{name}", a.shape, mybir.dt.from_np(a.dtype), kind="ExternalInput").ap()
    out = nc.dram_tensor("out_x", (SEQS, TOK, DIM), F32, kind="ExternalOutput").ap()
    blocks_kernel(nc, aps, out)
    r = run_bass_kernel_spmd(nc, [feeds], core_ids=[0])
    return r.results[0]["out_x"]
```

```python
from contextlib import ExitStack

import concourse.bass as bass
from concourse import mybir

F32 = mybir.dt.float32
BF16 = mybir.dt.bfloat16
ALU = mybir.AluOpType
ACT = mybir.ActivationFunctionType
AX_X = mybir.AxisListType.X

LAYERS = 4
KINDS = "aaat"
SEQS, TOK, DIM = 32, 128, 144
HEADS = 16
HD = DIM // HEADS
HIDDEN = 4 * DIM
REM = DIM - 128
COPIES = 7
REM_ROWS = COPIES * REM
MID_ROW, LOW_ROW, BIAS_ROW = 64, 96, 48
GB = 4
GT = GB * TOK
GROUPS = SEQS // GB
QKM = 96
QKT = 2 * DIM // QKM
FCT = 5
FCM = [128, 128, 128, 128, 64]
Q_PARTS = (0, 0, 0, 1, 1, 2)
K_PARTS = (0, 1, 2, 0, 1, 0)
PARTS = len(Q_PARTS) * HD
SCORE_ROWS = 120
MAX_ROW = 126
CH = 4
CHUNKS = HEADS // CH
STEPS = GB * CHUNKS
AHEAD = 3 * CHUNKS
LAG = 2
PBUFS = 4

LIN_USES = {
    "T1_0": (0, "h1_ready_act", 3), "T1_1": (1, "h1_ready_dve", 3),
    "OD0": (0, "oT_ready", 0), "OD1": (1, "oT_ready", 1), "PJ0": (0, "proj_gated", 0),
    "OD2": (1, "oT_ready", 2), "V0": (0, "v_ready", 0), "OD3": (1, "oT_ready", 3), "PJ1": (1, "proj_gated", 1),
    "T2_0": (0, "h2_ready_act", 3), "V1": (1, "v_ready", 1),
    "Q0": (1, "tok_ready", 0), "Q1": (0, "tok_ready", 1), "Q2": (1, "tok_ready", 2), "Q3": (0, "tok_ready", 3),
    "T2_1": (1, "h2_ready_act", 7), "M0": (0, "mlp_gated", 0), "M1": (0, "mlp_gated", 1),
    "mT0": (1, "mT_copied", 0), "mT1": (1, "mT_copied", 1), "mT2": (1, "mT_copied", 2), "mT3": (0, "mT_copied", 3),
}
for _h in range(2):
    for _T in range(FCT):
        LIN_USES[f"F{_h}{_T}"] = ((_T + _h) % 2, "gelu_ready", _h * FCT + _T)
LIN_BANK = {name: use[0] for name, use in LIN_USES.items()}
OF_NEXT = {"T1_0", "T1_1", "Q0", "Q1", "Q2", "Q3", "V0", "V1", "mT0", "mT1"}


def uses_of(this, nxt):
    flips = ["T1_0", "T1_1"] if nxt else []
    tok = ["Q0", "Q1", "Q2", "Q3"] if nxt == "t" else []
    vals = ["V0", "V1"] if nxt == "a" else []
    maxT = ["mT0", "mT1"] if nxt == "a" else []
    if this is None:
        return flips + tok + vals + maxT
    if this == "a":
        start = ["mT2"] + flips + ["mT3", "OD0", "OD1"]
    else:
        start = flips + ["OD0"] + tok[:2] + ["OD1"]
        tok = tok[2:]
    hidden = [[f"F{h}{T}" for T in range(FCT)] for h in range(2)]
    return (start + ["PJ0", "OD2"] + vals[:1] + ["OD3", "PJ1", "T2_0"] + vals[1:] + tok + hidden[0] + ["T2_1", "M0"]
            + hidden[1] + ["M1"] + maxT)


def use_before(use, this, nxt):
    order = uses_of(this, nxt)
    bank = LIN_BANK[use]
    same = [name for name in order[:order.index(use)] if LIN_BANK[name] == bank]
    if same:
        return same[-1], 0
    if this is None:
        return None, 0
    return [name for name in uses_of("a", this) if LIN_BANK[name] == bank][-1], 1


W_QK, W_V, W_F1 = 0, 2 * DIM, 3 * DIM
W_COLS = 3 * DIM + HIDDEN

ONES = 6
CONSTS = 4 + 1 + QKM // HEADS + 2 + 1 + 1

PER_GROUP = {
    "exp_table": 1, "gelu_table": 1,
    "n1_stats": GB, "n1_aggr": GB, "n1_var": 3, "n1_rstd": 1, "n1_ready": GB + 1,
    "n2_stats": GB, "n2_aggr": GB, "n2_var": 6, "n2_rstd": 2, "n2_ready": GB + 2,
    "h1_parts": 4, "h2_parts": 8,
    "t1_done": 2, "t2_done": 2,
    "h1_ready_act": 4, "h1_ready_dve": 4, "h2_ready_act": 8,
    "qk_done": QKT, "qk_taken": QKT, "qk_high": QKT, "qk_mid": QKT, "qk_low": QKT,
    "v_done": 2, "v_ready": 2,
    "score_done": STEPS, "max_done": STEPS, "max_high": GB, "max_low": GB,
    "mT_done": GB, "mT_copied": GB,
    "st_done": STEPS, "exp_done": STEPS, "pv_done": STEPS,
    "o_copied": GB, "o_tok_done": GB, "o_recip": GB, "o_normed": GB, "o_flip_done": GB, "oT_ready": GB,
    "proj_done": 2, "proj_gated": 2, "x_attn": 2,
    "fc1_done": 2 * FCT, "gelu_ready": 2 * FCT, "fc2_done": 2, "mlp_gated": 2, "x_mlp": 2,
    "mods1": 2, "mods2": 2,
    "tok_done": GB, "tok_ready": GB, "tok_prod": GB, "tok_scores": GB, "tok_max": GB, "tok_less": GB,
    "tok_exp": GB, "tok_sum": GB, "tok_recip": GB, "tok_weighted": GB, "tok_values": GB, "tok_normed": GB,
    "qk_rest": QKT, "qk_sq": QKT, "norm_done": 1, "norm_max": 1, "norm_ln": 1, "norm_exp": 1, "norm_y2": 1, "norm_t": 1,
    "norm_y": 1, "spread_done": QKT, "qk_scaled": QKT,
}
PER_GROUP_DMA = {"parts_stored": 3, "stack_loaded": 6, "m_loaded0": 2, "m_loaded1": 2, "m_loaded2": 2,
                 "m_loaded3": 2, "gates_loaded": 2,
                 "mixed_stored": 4, "mixed0": 1, "mixed1": 1, "mixed2": 1, "mixed3": 1}
TOKEN_ONLY = {name for name in [*PER_GROUP, *PER_GROUP_DMA] if name.startswith(("tok_", "mixed"))}
FIRST_TOKEN_GROUP = KINDS.index("t") * GROUPS


GELU = [ACT.Gelu_apprx_tanh, ACT.Gelu_apprx_tanh, ACT.Gelu_apprx_tanh, ACT.Gelu]


MINUS_ONES = -1.0058441162109375


class Piece:

    def __init__(self, i, h):
        n = GB if i == 0 else GB // 2
        self.seqs = range(h * n, (h + 1) * n)
        self.here = slice(h * n, (h + 1) * n)
        self.tokens = slice(h * n * TOK, (h + 1) * n * TOK)
        self.last_seq = (h + 1) * n - 1
        self.var = 3 * h
        self.rstd = h
        self.normed = h * (n + 1) + n - 1
        self.ready = h * (n + 1) + n
        self.parts = 4 * h


class Group:

    def __init__(self, base, reg=None):
        self.base, self.reg = base, reg

    def plus(self, n):
        return Group(self.base + n, self.reg)

    def times(self, n, more=0):
        whole = self.base * n + more
        return whole if self.reg is None else self.reg * n + whole

    @property
    def is_first(self):
        return self.reg is None and self.base == 0

    def in_layer(self, n):
        if self.reg is None:
            return (self.base % GROUPS) * n
        return self.reg * n + (self.base % GROUPS) * n


def blocks_kernel(nc, t, out):
    ctx = ExitStack()
    with ctx:
        def sb(name, shape, dt=F32):
            return ctx.enter_context(nc.sbuf_tensor(name, shape, dt))

        def ps(name):
            return ctx.enter_context(nc.psum_tensor(name, [128, 512], F32))

        x = sb("x", [128, SEQS, DIM])
        w_h = [sb(f"w_h{l}", [128, W_COLS]) for l in range(LAYERS)]
        w_h_rem = [sb(f"w_h_rem{l}", [128, W_COLS], BF16) for l in range(LAYERS)]
        w_o = [sb(f"w_o{l}", [128, DIM]) for l in range(LAYERS)]
        w_o_rem = [sb(f"w_o_rem{l}", [REM + 1, DIM]) for l in range(LAYERS)]
        w_f2 = [sb(f"w_f2{l}", [128, FCT, DIM]) for l in range(LAYERS)]
        mod_main = sb("mod_main", [128, LAYERS, 4, SEQS])
        mod_rem = sb("mod_rem", [REM_ROWS, LAYERS, 4, SEQS])
        ident = sb("ident", [128, 128])
        ident_b = sb("ident_b", [128, 128], BF16)
        neg_half = sb("neg_half", [128, GB])

        stats = [sb(f"stats{i}", [128, GB, 6]) for i in range(2)]
        moments = [sb(f"moments{i}", [128, GB, 2]) for i in range(2)]
        mean_sq = sb("mean_sq", [128, 2, GB])
        var = [sb(f"var{i}", [128, GB]) for i in range(2)]
        rstd = [sb(f"rstd{i}", [128, GB]) for i in range(2)]
        normed = [sb(f"normed{i}", [128, GB, DIM]) for i in range(2)]
        normed_last = [sb(f"normed_last{i}", [128, GB, REM_ROWS]) for i in range(2)]
        mods = [sb(f"mods{i}", [128, 2, GB]) for i in range(2)]
        mods_rem = [sb(f"mods_rem{i}", [REM_ROWS, 2, GB]) for i in range(2)]
        hT = [sb(f"hT{i}", [128, GT]) for i in range(2)]
        hT_last = [sb(f"hT_last{i}", [REM_ROWS, GT]) for i in range(2)]
        hT_rem = [sb(f"hT_rem{i}", [128, GT], BF16) for i in range(2)]
        h_rest = sb("h_rest", [128, GT])
        part_high = sb("part_high", [QKM, QKT, GT], BF16)
        part_mid = sb("part_mid", [QKM, QKT, GT], BF16)
        part_low = sb("part_low", [QKM, QKT, GT], BF16)
        qk_rest = sb("qk_rest", [QKM, QKT, GT])
        q_room = sb("q_room", [128, HEADS * GT // 2])
        k_room = sb("k_room", [128, HEADS * GT // 2])
        q_stack = q_room[:, :].bitcast(BF16).rearrange("p (h n) -> p h n", h=HEADS)
        k_stack = k_room[:, :].bitcast(BF16).rearrange("p (h n) -> p h n", h=HEADS)
        v_room = sb("v_room", [128, GB * HEADS * 32])
        v_aug = v_room[:, :].rearrange("p (b h r) -> p b h r", b=GB, h=HEADS)
        maxima = sb("maxima", [128, GB, HEADS])
        max_parts = sb("max_parts", [128, GB, 2, HEADS], BF16)
        max_T = sb("max_T", [2 * HEADS, GB, TOK], BF16)
        p_room = sb("p_room", [128, PBUFS * CH * TOK])
        probs = p_room[:, :].rearrange("p (i n) -> p i n", i=PBUFS)
        o_room = sb("o_room", [128, 2 * CHUNKS * TOK])
        o_feat = o_room[:, :].rearrange("p (i n) -> p i n", i=2)
        o_recip = sb("o_recip", [128, 2, HEADS])
        o_tok = sb("o_tok", [128, 2, DIM])
        oT = sb("oT", [128, GT])
        oT_rem = sb("oT_rem", [REM + 1, GT])
        gates = sb("gates", [128, 2, GB, DIM])
        gated = sb("gated", [128, 2, 2 * DIM])
        gelu = sb("gelu", [128, FCT, GT])

        pick = sb("pick", [QKM, QKT, 2 * HEADS])
        spread = sb("spread", [2 * HEADS, 2 * DIM])
        head_gain = sb("head_gain", [2 * HEADS, 1])
        raw_room = sb("raw_room", [128, 2 * QKT * GT])
        raw2 = raw_room[0:QKM, :].rearrange("p (i t n) -> p i t n", i=2, t=QKT)
        qk_raw, qk_sq = raw2[:, 0], raw2[:, 1]
        qk_fit = sb("qk_fit", [QKM, QKT, GT])
        norm2 = sb("norm2", [2 * HEADS, GT])
        mod_last = norm2[0:REM, :].rearrange("p (l i b) -> p l i b", l=LAYERS, i=4)
        norm_y = sb("norm_y_buf", [2 * HEADS, 2, GT])
        norm_t = sb("norm_t_buf", [2 * HEADS, 2, GT])

        MIX = HEADS * HEADS * HD
        tok_qkv = v_room[:, 0:GB * 3 * DIM].rearrange("p (b n) -> p b n", b=GB)
        tok_prod = q_room[:, 0:MIX]
        tok_weighted = [k_room[:, 0:MIX], raw_room[:, 0:MIX]]
        n0 = 2 * HEADS * HEADS
        tok_e = p_room[:, 0:n0].rearrange("p (i n) -> p i n", i=2)
        tok_less = p_room[:, n0:2 * n0].rearrange("p (i n) -> p i n", i=2)
        tok_o = p_room[:, 2 * n0:2 * n0 + 2 * DIM].rearrange("p (i n) -> p i n", i=2)
        n1 = 2 * n0 + 2 * DIM
        tok_small = p_room[:, n1:n1 + 8 * HEADS].rearrange("p (i n) -> p i n", i=8)
        mixed = o_room[:, 0:GB * DIM].rearrange("p (b n) -> p b n", b=GB)

        table_use = sb("table_use", [1, 3])
        cT = sb("cT", [128, SEQS])
        cT_rem = sb("cT_rem", [REM + 1, SEQS])
        c_exp = sb("c_exp", [128, 2, SEQS])
        c_exp_rem = sb("c_exp_rem", [REM, 2, SEQS])
        silu = sb("silu", [128, SEQS])
        silu_rem = sb("silu_rem", [REM + 1, SEQS])
        w_ada = [q_room[:, l * 6 * DIM:(l + 1) * 6 * DIM] for l in range(LAYERS)]
        flat = gelu[:, :, :].rearrange("p t n -> p (t n)")
        gate_rows = flat[0:SEQS, 0:LAYERS * 2 * DIM].rearrange("b (l n) -> b l n", l=LAYERS)
        w_ada_rem = [raw_room[0:REM + 1, l * 6 * DIM:(l + 1) * 6 * DIM] for l in range(LAYERS - 1)]
        w_ada_rem.append(flat[0:REM + 1, LAYERS * 2 * DIM:(LAYERS * 2 + 6) * DIM])
        w_stage = [k_room[:, l * W_COLS:(l + 1) * W_COLS] for l in range(LAYERS)]
        w_rest = p_room[:, 0:W_COLS]
        w_parts = p_room[:, W_COLS:2 * W_COLS].bitcast(BF16).rearrange("p (i n) -> p i n", i=2)
        copier = sb("copier", [REM, REM_ROWS])
        part_of = sb("part_of", [128, 3])
        gain = sb("gain", [128, 2])

        score_bank = [ps(f"score_bank{i}") for i in range(2)]
        st_bank = [ps(f"st_bank{i}") for i in range(2)]
        o_bank = [ps(f"o_bank{i}") for i in range(2)]
        lin = [ps(f"lin{i}") for i in range(2)]
        mod_banks = (lin, score_bank, st_bank, o_bank)
        lin_b = [lin[i][:, :].bitcast(BF16) for i in range(2)]

        parts_dram = nc.dram_tensor("parts_dram", [3, 2 * DIM, GT], BF16, kind="Internal").ap()
        gates_dram = nc.dram_tensor("gates_dram", [LAYERS, 2, SEQS, DIM], F32, kind="Internal").ap()

        mix_dram = nc.dram_tensor("mix_dram", [GB, HEADS, TOK, HD], F32, kind="Internal").ap()

        S = {name: ctx.enter_context(nc.semaphore(name)) for name in [*PER_GROUP, *PER_GROUP_DMA]}
        setup = {name: ctx.enter_context(nc.semaphore("set_" + name)) for name in (
            "x", "weights_first", "weights", "stage_clear", "part_of", "staged0", "staged1", "staged2", "staged3", "split", "c", "ada0", "ada1", "ada2", "ada3", "gain", "const", "ones",
            "clear", "c_exp", "silu", "mods_done", "mods_kept", "gates_kept", "gates_stored", "picks", "carrier", "out")}
        block = ctx.enter_context(nc.Block())

        def need(eng, name, group, k, ago=0):
            unit = 1 if name in PER_GROUP else 16
            if name in TOKEN_ONLY:
                group = group.plus(-FIRST_TOKEN_GROUP)
            n = PER_GROUP[name] if name in PER_GROUP else PER_GROUP_DMA[name]
            value = group.times(unit * n, unit * (n * (1 - ago) + k + 1))
            if group.reg is None and value <= 0:
                return
            eng.wait_ge(S[name], value)

        def start_with(eng, names):
            for name in names:
                eng.sem_inc(S[name], PER_GROUP[name] if name in PER_GROUP else 16 * PER_GROUP_DMA[name])

        def layers(eng, body):
            for l in range(LAYERS):
                with eng.Fori(0, GROUPS - 1) as g:
                    body(Group(l * GROUPS, g), l, l)
                body(Group(l * GROUPS + GROUPS - 1), l, l + 1 if l + 1 < LAYERS else None)

        def layers_from_after_next(eng, body):
            for l in range(LAYERS):
                with eng.Fori(0, GROUPS - 2) as g:
                    body(Group(l * GROUPS, g), l, l, l)
                following = l + 1 if l + 1 < LAYERS else None
                body(Group(l * GROUPS + GROUPS - 2), l, l, following)
                body(Group(l * GROUPS + GROUPS - 1), l, following, following)

        def h_read_by(i, kinds):
            if i == 1:
                return "fc1_done", 2 * FCT - 1
            return ("v_done", 1) if kinds[0] == "a" else ("tok_done", GB - 1)

        @block.sync
        def _(eng):
            start_with(eng, PER_GROUP_DMA)
            eng.dma_start(cT[:, :], t["cT"][0:128, :]).then_inc(setup["c"], 16)
            eng.dma_start(cT_rem[0:REM, :], t["cT"][128:DIM, :]).then_inc(setup["c"], 16)
            for l in range(LAYERS):
                eng.dma_start(w_ada[l], t[f"ada{l}"][0:128, :]).then_inc(setup[f"ada{l}"], 16)
                eng.dma_start(w_ada_rem[l], t[f"ada{l}"][128:DIM + 1, :]).then_inc(setup[f"ada{l}"], 16)
            for i, name in enumerate(("g1", "g2")):
                eng.dma_start(gain[:, i:i + 1], t[name].partition_broadcast(128)).then_inc(setup["gain"], 16)
            for i, name in enumerate(("qg", "kg")):
                eng.dma_start(head_gain[i * HEADS:(i + 1) * HEADS, :], t[name].partition_broadcast(HEADS))\
                   .then_inc(setup["gain"], 16)
            eng.wait_ge(setup["gates_kept"], LAYERS)
            eng.dma_start(gates_dram.rearrange("l w b n -> b (l w) n"), gate_rows[:, :, :].rearrange(
                "b l (w n) -> b (l w) n", w=2)).then_inc(setup["gates_stored"], 16)
            eng.wait_ge(setup["gates_stored"], 16)

            def load_gates(J, l):
                for w in range(2):
                    src = gates_dram[l, w].rearrange("b n -> (b n)")[bass.ds(J.in_layer(GB * DIM), GB * DIM)]
                    eng.dma_start(gates[:, w, :, :].rearrange("p b n -> p (b n)"), src.partition_broadcast(128))\
                       .then_inc(S["gates_loaded"], 16)

            def load_stack(J):
                for i, (part, ready) in enumerate(((part_high, "qk_high"), (part_mid, "qk_mid"),
                                                   (part_low, "qk_low"))):
                    need(eng, ready, J, QKT - 1)
                    if i == 0:
                        need(eng, "stack_loaded", J, 5, ago=1)
                    eng.dma_start(parts_dram[i].rearrange("(t p) n -> p t n", p=QKM), part[:, :, :])\
                       .then_inc(S["parts_stored"], 16)
                need(eng, "parts_stored", J, 2)
                need(eng, "st_done", J, STEPS - 1, ago=1)
                rows = parts_dram.rearrange("i (s d h) n -> s i d (h n)", s=2, d=HD)
                at = 0
                for i, n in enumerate((3, 2, 1)):
                    src = rows[0, i].rearrange("(o d) n -> o d n", o=1).broadcast_to([n, HD, HEADS * GT])
                    eng.dma_start(q_stack[at * HD:(at + n) * HD, :, :].rearrange("p h n -> p (h n)"), src)\
                       .then_inc(S["stack_loaded"], 16)
                    src = rows[1, 0:3 - i].rearrange("i d n -> i d n")
                    eng.dma_start(k_stack[at * HD:(at + n) * HD, :, :].rearrange("p h n -> p (h n)"), src)\
                       .then_inc(S["stack_loaded"], 16)
                    at += n

            def mix(J, b):
                need(eng, "o_flip_done", J, b, ago=1)
                eng.sem_inc(setup["carrier"], 1)
                need(eng, "tok_normed", J, b)
                if b == 0:
                    for i in range(GB):
                        need(eng, f"mixed{i}", J, 0, ago=1)
                eng.dma_start(mix_dram[b].rearrange("h t d -> t h d"),
                              tok_o[:, b % 2, :].rearrange("p (h d) -> p h d", d=HD))\
                   .then_inc(S["mixed_stored"], 16)
                need(eng, "mixed_stored", J, b)
                eng.dma_start(mixed[:, b, :], mix_dram[b].rearrange("h t d -> (h t d)")
                              .rearrange("(r c) -> r c", c=DIM)).then_inc(S[f"mixed{b}"], 16)

            def load_max(J, b):
                need(eng, "mT_copied", J, b)
                for i in range(2):
                    eng.dma_start(q_stack[MAX_ROW + i:MAX_ROW + i + 1, :, b * TOK:(b + 1) * TOK],
                                  max_T[i * HEADS:(i + 1) * HEADS, b, :]).then_inc(S[f"m_loaded{b}"], 16)

            first = Group(0)
            load_gates(first, 0)
            eng.wait_ge(setup["clear"], 2)
            load_stack(first)
            load_max(first, 0)
            load_max(first, 1)

            def body(G, l, nxt):
                if KINDS[l] == "a":
                    load_max(G, 2)
                    load_max(G, 3)
                else:
                    for b in range(GB):
                        mix(G, b)
                if nxt is not None and KINDS[nxt] == "a":
                    load_stack(G.plus(1))
                    load_max(G.plus(1), 0)
                    load_max(G.plus(1), 1)
                need(eng, "x_mlp", G, 1)
                eng.sem_inc(setup["carrier"], 1)
                if l == LAYERS - 1:
                    at = G.in_layer(GB)
                    eng.dma_start(out[bass.ds(at, GB)].rearrange("b t d -> t b d"), x[:, bass.ds(at, GB), :])\
                       .then_inc(setup["out"], 16)
                if nxt is not None:
                    load_gates(G.plus(1), nxt)

            layers(eng, body)
            eng.wait_ge(setup["out"], 16 * GROUPS)

        @block.gpsimd
        def _(eng):
            start_with(eng, ("x_mlp", "qk_low", "tok_weighted", "n1_rstd", "n2_rstd", "mods1", "mods2"))
            eng.memset(ident[:, :], 0.0).then_inc(setup["const"], 1)
            eng.memset(pick[:, :, :], 0.0).then_inc(setup["const"], 1)
            eng.memset(spread[:, :], 0.0).then_inc(setup["const"], 1)
            eng.memset(neg_half[:, :], -0.5).then_inc(setup["const"], 1)
            eng.wait_ge(setup["const"], 4)
            eng.affine_select(out=ident[:, :], in_=ident[:, :], compare_op=ALU.not_equal, fill=1.0,
                              base=0, pattern=[[-1, 128]], channel_multiplier=1).then_inc(setup["const"], 1)
            heads = pick[:, :, :].rearrange("p t (s h) -> p t s h", s=2)
            for a in range(QKM // HEADS):
                eng.affine_select(out=heads, in_=heads, compare_op=ALU.not_equal, fill=1.0, base=-a * HEADS,
                                  pattern=[[0, QKT], [0, 2], [-1, HEADS]], channel_multiplier=1)\
                   .then_inc(setup["const"], 1)
                eng.wait_ge(setup["const"], 6 + a)
            eng.affine_select(out=heads[:, :, 0, :], in_=heads[:, :, 0, :], compare_op=ALU.is_ge, fill=0.0,
                              base=DIM - 1, pattern=[[-QKM, QKT], [0, HEADS]], channel_multiplier=-1)\
               .then_inc(setup["const"], 1)
            eng.affine_select(out=heads[:, :, 1, :], in_=heads[:, :, 1, :], compare_op=ALU.is_ge, fill=0.0,
                              base=-DIM, pattern=[[QKM, QKT], [0, HEADS]], channel_multiplier=1)\
               .then_inc(setup["const"], 1)
            rows = spread[:, :].rearrange("m (s d h) -> m s d h", s=2, d=HD)
            eng.affine_select(out=rows, in_=rows, compare_op=ALU.not_equal, fill=1.0, base=0,
                              pattern=[[-HEADS, 2], [0, HD], [-1, HEADS]], channel_multiplier=1)\
               .then_inc(setup["const"], 1)
            eng.tensor_copy(ident_b[:, :], ident[:, :]).then_inc(setup["const"], 1)

            def mods_of(J, l, i):
                need(eng, ("h1_ready_act", "h2_ready_act")[i], J, 3, ago=1)
                need(eng, ("h1_ready_dve", "h2_ready_act")[i], J, (3, 7)[i], ago=1)
                at = J.in_layer(GB)
                name = ("mods1", "mods2")[i]
                eng.tensor_copy(mods[i][:, :, :], mod_main[:, l, 2 * i:2 * i + 2, bass.ds(at, GB)])\
                   .then_inc(S[name], 1)
                eng.tensor_copy(mods_rem[i][:, :, :], mod_rem[:, l, 2 * i:2 * i + 2, bass.ds(at, GB)])\
                   .then_inc(S[name], 1)

            def rstd_of(J, i, h=0):
                piece = Piece(i, h)
                need(eng, ("n1_var", "n2_var")[i], J, piece.var + 2)
                need(eng, ("n1_ready", "n2_ready")[i], J, piece.normed, ago=1)
                eng.tensor_tensor(rstd[i][:, piece.here], var[i][:, piece.here], neg_half[:, piece.here], ALU.pow)\
                   .then_inc(S[("n1_rstd", "n2_rstd")[i]], 1)

            def add_mlp(G, h):
                need(eng, "mlp_gated", G, h)
                xs = x[:, bass.ds(G.in_layer(GB) + 2 * h, 2), :].rearrange("p b n -> p (b n)")
                eng.tensor_tensor(xs, xs, gated[:, h, :], ALU.add).then_inc(S["x_mlp"], 1)

            def lows(J):
                for T in range(QKT):
                    need(eng, "qk_mid", J, T)
                    if T == 0:
                        need(eng, "parts_stored", J, 2, ago=1)
                    eng.tensor_tensor(part_low[:, T, :], qk_rest[:, T, :], part_mid[:, T, :], ALU.subtract)\
                       .then_inc(S["qk_low"], 1)

            def weight(J, b):
                need(eng, "tok_exp", J, b)
                if b >= 2:
                    need(eng, "tok_values", J, b - 2)
                else:
                    need(eng, "tok_values", J, b + 2, ago=1)
                shape = [128, HEADS, HD, HEADS]
                e = tok_e[:, b % 2, :].rearrange("p (h o k) -> p h o k", h=HEADS, o=1).broadcast_to(shape)
                v = tok_qkv[:, b, 2 * DIM:3 * DIM].rearrange("p (o k d) -> p o d k", o=1, d=HD).broadcast_to(shape)
                eng.tensor_tensor(tok_weighted[b % 2].rearrange("p (h d k) -> p h d k", h=HEADS, d=HD), e, v,
                                  ALU.mult).then_inc(S["tok_weighted"], 1)

            eng.wait_ge(setup["mods_kept"], 2 * LAYERS + 1)
            eng.wait_ge(setup["const"], CONSTS)
            first = Group(0)
            mods_of(first, 0, 0)
            rstd_of(first, 0)
            rstd_of(first.plus(1), 0)
            eng.memset(q_room[:, :], 0.0).then_inc(setup["clear"], 1)
            eng.wait_ge(setup["split"], 7 * LAYERS)
            eng.wait_ge(setup["clear"], 1)
            eng.memset(k_room[:, :], MINUS_ONES).then_inc(setup["clear"], 1)
            lows(first)

            def body(G, l, nxt, after):
                J = G.plus(1)
                if nxt is not None:
                    mods_of(J, nxt, 0)
                mods_of(G, l, 1)
                if KINDS[l] == "t":
                    weight(G, 2)
                    weight(G, 3)
                if nxt and KINDS[nxt] == "a":
                    lows(J)
                if KINDS[l] == "a" and after is not None:
                    rstd_of(G.plus(2), 0)
                rstd_of(G, 1, 0)
                if KINDS[l] == "t" and after is not None:
                    rstd_of(G.plus(2), 0)
                if nxt == 0:
                    lows(J)
                rstd_of(G, 1, 1)
                if nxt is not None and KINDS[nxt] == "t":
                    weight(J, 0)
                    weight(J, 1)
                add_mlp(G, 0)
                add_mlp(G, 1)

            layers_from_after_next(eng, body)

        @block.scalar
        def _(eng):
            start_with(eng, ("exp_table", "gelu_table", "h1_ready_act", "h2_ready_act", "qk_high", "v_ready", "mT_copied", "exp_done",
                             "o_copied", "oT_ready", "gelu_ready", "tok_ready", "tok_exp", "qk_sq", "norm_ln", "norm_exp"))
            eng.wait_ge(setup["c"], 32)
            eng.activation(c_exp[:, 0, :], cT[:, :], ACT.Exp, scale=-1.0).then_inc(setup["c_exp"], 1)
            eng.activation(c_exp_rem[:, 0, :], cT_rem[0:REM, :], ACT.Exp, scale=-1.0)\
               .then_inc(setup["c_exp"], 1)
            for h in range(4):
                n = SEQS // 4
                eng.dma_start(x[:, h * n:(h + 1) * n, :], t["x"][h * n:(h + 1) * n].rearrange("b t d -> t b d"))\
                   .then_inc(setup["x"], 16)
            eng.dma_start(part_of[:, :], t["part_of"]).then_inc(setup["part_of"], 16)
            eng.wait_ge(setup["stage_clear"], 1)
            for l in range(LAYERS):
                for r in (0, MID_ROW):
                    src = t[f"h_w{l}"][128:DIM, :].rearrange("(o r) n -> o r n", o=1).broadcast_to([3, REM, W_COLS])
                    eng.dma_start(w_stage[l][r:r + 3 * REM, :], src).then_inc(setup[f"staged{l}"], 16)
                eng.dma_start(w_stage[l][BIAS_ROW:BIAS_ROW + 3, :], t[f"h_w{l}"][DIM, :].partition_broadcast(3))\
                   .then_inc(setup[f"staged{l}"], 16)
                done = setup["weights" if l else "weights_first"]
                eng.dma_start(w_h[l][:, :], t[f"h_w{l}"][0:128, :]).then_inc(done, 16)
                eng.dma_start(w_o[l][:, :], t[f"o_w{l}"][0:128, :]).then_inc(done, 16)
                eng.dma_start(w_o_rem[l][:, :], t[f"o_w{l}"][128:DIM + 1, :]).then_inc(done, 16)
                eng.dma_start(w_f2[l][:, 0:4, :], t[f"f2_w{l}"][0:512, :].rearrange("(t p) n -> p t n", p=128))\
                   .then_inc(done, 16)
                eng.dma_start(w_f2[l][0:65, 4, :], t[f"f2_w{l}"][512:HIDDEN + 1, :]).then_inc(done, 16)
            for l in range(LAYERS):
                eng.wait_ge(setup["mods_done"], l + 1)
                eng.activation(gate_rows[:, l, :], mod_banks[l][1][0:SEQS, 0:2 * DIM], ACT.Copy if l else ACT.Tanh)\
                   .then_inc(setup["gates_kept"], 1)

            def first_use(name, G, func):
                need(eng, name, G, 0, ago=1)
                k = ("exp_table", "gelu_table").index(name)
                eng.activation(table_use[:, 1 + k:2 + k], table_use[:, 0:1], func).then_inc(S[name], 1)

            def modulated(J, i, h=0, kinds="aa"):
                need(eng, ("mods1", "mods2")[i], J, 1)
                need(eng, ("t1_done", "t2_done")[i], J, h)
                if h == 0:
                    name, k = h_read_by(i, kinds)
                    need(eng, name, J, k, ago=1)
                    need(eng, ("h1_parts", "h2_parts")[i], J, (3, 7)[i], ago=1)
                bank = lin[LIN_BANK[("T1_", "T2_")[i] + str(h)]]
                for b in (2 * h, 2 * h + 1):
                    c = (b % 2) * 256
                    eng.activation(hT_last[i][:, b * TOK:(b + 1) * TOK], bank[0:REM_ROWS, c + TOK:c + 256],
                                   ACT.Identity, bias=mods_rem[i][:, 0, b:b + 1],
                                   scale=mods_rem[i][:, 1, b:b + 1])\
                       .then_inc(S[("h1_ready_act", "h2_ready_act")[i]], 1)
                for b in (2 * h, 2 * h + 1):
                    c = (b % 2) * 256
                    eng.activation(hT[i][:, b * TOK:(b + 1) * TOK], bank[:, c:c + TOK], ACT.Identity,
                                   bias=mods[i][:, 0, b:b + 1], scale=mods[i][:, 1, b:b + 1])\
                       .then_inc(S[("h1_ready_act", "h2_ready_act")[i]], 1)

            def squares(J, T):
                need(eng, "qk_taken", J, T)
                eng.activation(qk_sq[:, T, :], qk_raw[:, T, :], ACT.Square).then_inc(S["qk_sq"], 1)

            def head_norms(J):
                need(eng, "norm_max", J, 0)
                eng.activation(norm_t[:, 0, :], norm2[:, :], ACT.Ln).then_inc(S["norm_ln"], 1)
                need(eng, "norm_ln", J, 0)
                eng.activation(norm_y[:, 0, :], norm_t[:, 0, :], ACT.Exp, scale=-0.5)\
                   .then_inc(S["norm_exp"], 1)

            def high(J, l, T):
                if T == 0:
                    need(eng, "parts_stored", J, 2, ago=1)
                if l == 0:
                    need(eng, "qk_scaled", J, T)
                    src = qk_fit[:, T, :]
                else:
                    need(eng, "qk_done", J, T)
                    src = score_bank[T % 2][0:QKM, :]
                eng.activation(part_high[:, T, :], src, ACT.Copy).then_inc(S["qk_high"], 1)

            def values(J, h):
                need(eng, "v_done", J, h)
                if h == 0:
                    need(eng, "pv_done", J, STEPS - 1, ago=1)
                bank = lin[LIN_BANK[f"V{h}"]]
                eng.activation(v_aug[:, 2 * h:2 * h + 2, :, 0:HD],
                               bank[:, 0:2 * DIM].rearrange("p (b h d) -> p b h d", b=2, d=HD), ACT.Copy)\
                   .then_inc(S["v_ready"], 1)

            def copy_max(J, b):
                need(eng, "mT_done", J, b)
                need(eng, f"m_loaded{b}", J, 1, ago=1)
                eng.activation(max_T[:, b, :], lin_b[LIN_BANK[f"mT{b}"]][0:2 * HEADS, 0:TOK], ACT.Copy)\
                   .then_inc(S["mT_copied"], 1)

            def copy_o(G, b):
                need(eng, "pv_done", G, (b + 1) * CHUNKS - 1)
                if b >= 2:
                    need(eng, "o_tok_done", G, b - 2)
                else:
                    need(eng, "o_tok_done", G, b + 2, ago=1)
                eng.activation(o_feat[:, b % 2, :], o_bank[b % 2][:, :], ACT.Copy).then_inc(S["o_copied"], 1)

            def copy_oT(G, b):
                need(eng, "o_flip_done", G, b)
                if b == 0:
                    need(eng, "proj_done", G, 1, ago=1)
                bank = lin[LIN_BANK[f"OD{b}"]]
                eng.activation(oT_rem[0:REM, b * TOK:(b + 1) * TOK], bank[0:REM, TOK:2 * TOK], ACT.Copy)
                eng.activation(oT[:, b * TOK:(b + 1) * TOK], bank[:, 0:TOK], ACT.Copy).then_inc(S["oT_ready"], 1)

            def token_qkv(J, b):
                need(eng, "tok_done", J, b)
                need(eng, "tok_weighted", J, b, ago=1)
                eng.activation(tok_qkv[:, b, :], lin[LIN_BANK[f"Q{b}"]][:, 0:3 * DIM], ACT.Copy)\
                   .then_inc(S["tok_ready"], 1)

            def token_exp(J, b):
                need(eng, "tok_less", J, b)
                eng.activation(tok_e[:, b % 2, :], tok_less[:, b % 2, :], ACT.Exp, scale=float(HD) ** -0.5)\
                   .then_inc(S["tok_exp"], 1)

            eng.wait_ge(setup["gates_stored"], 16)
            eng.wait_ge(setup["ones"], ONES)
            eng.wait_ge(setup["const"], CONSTS)
            first = Group(0)
            modulated(first, 0)
            for T in range(QKT):
                squares(first, T)
            head_norms(first)
            for T in range(QKT):
                high(first, 0, T)
            values(first, 0)
            values(first, 1)
            copy_max(first, 0)
            copy_max(first, 1)

            def exponentials(G, l, nxt, kinds):
                copy_max(G, 2)
                for i in range(STEPS):
                    need(eng, "st_done", G, i)
                    if i >= PBUFS:
                        need(eng, "pv_done", G, i - PBUFS)
                    else:
                        need(eng, "pv_done", G, i - PBUFS + STEPS, ago=1)
                    eng.activation(probs[:, i % PBUFS, :], st_bank[i % 2][:, :], ACT.Exp, scale=float(HD) ** -0.5)\
                       .then_inc(S["exp_done"], 1)
                    if i == 5:
                        copy_max(G, 3)
                    if i == 2 and nxt is not None:
                        modulated(G.plus(1), 0, kinds=kinds)
                    if i in (8, 9, 12) and kinds[1] == "a":
                        T = (8, 9, 12).index(i)
                        if nxt == 0:
                            squares(G.plus(1), T)
                        else:
                            high(G.plus(1), nxt, T)
                    if i >= 6 and i % 4 == 2:
                        copy_o(G, (i - 6) // 4)
                    if i >= 10 and i % 4 == 2:
                        copy_oT(G, (i - 10) // 4)
                if nxt == 0:
                    head_norms(G.plus(1))
                else:
                    first_use("gelu_table", G, GELU[l])
                copy_o(G, 3)

            def body(G, l, nxt):
                kinds = KINDS[l] + (KINDS[nxt] if nxt is not None else "-")
                if KINDS[l] == "a":
                    exponentials(G, l, nxt, kinds)
                    if nxt == 0:
                        first_use("gelu_table", G, GELU[l])
                else:
                    if nxt is not None:
                        modulated(G.plus(1), 0, kinds=kinds)
                    token_exp(G, 3)
                    copy_oT(G, 0)
                    if nxt is not None:
                        token_qkv(G.plus(1), 0)
                        token_qkv(G.plus(1), 1)
                    copy_oT(G, 1)
                copy_oT(G, 2)
                if kinds[1] == "a":
                    values(G.plus(1), 0)
                if nxt == 0:
                    high(G.plus(1), 0, 0)
                    high(G.plus(1), 0, 1)
                copy_oT(G, 3)
                if nxt == 0:
                    high(G.plus(1), 0, 2)
                modulated(G, 1, 0)
                if kinds[1] == "a":
                    values(G.plus(1), 1)
                elif kinds[1] == "t":
                    for b in range(0 if kinds[0] == "a" else 2, GB):
                        token_qkv(G.plus(1), b)
                    if kinds[0] == "t":
                        token_exp(G.plus(1), 0)
                for h in range(2):
                    half = slice(h * GT // 2, (h + 1) * GT // 2)
                    need(eng, "fc2_done", G, h, ago=1)
                    for T in range(FCT):
                        need(eng, "fc1_done", G, h * FCT + T)
                        m = FCM[T]
                        eng.activation(gelu[0:m, T, half], lin[LIN_BANK[f"F{h}{T}"]][0:m, 0:GT // 2],
                                       GELU[l]).then_inc(S["gelu_ready"], 1)
                    if h == 0:
                        modulated(G, 1, 1)
                        if kinds == "tt":
                            token_exp(G.plus(1), 1)
                first_use("exp_table", G, ACT.Exp)
                if kinds[1] == "a":
                    copy_max(G.plus(1), 0)
                    copy_max(G.plus(1), 1)
                elif kinds[1] == "t":
                    if kinds[0] == "a":
                        token_exp(G.plus(1), 0)
                        token_exp(G.plus(1), 1)
                    token_exp(G.plus(1), 2)

            layers(eng, body)

        @block.vector
        def _(eng):
            start_with(eng, ("h1_parts", "h2_parts", "n1_stats", "n1_aggr", "n1_var", "n1_ready", "n2_stats", "n2_aggr", "n2_var",
                             "n2_ready", "h1_ready_dve", "qk_taken", "qk_mid", "max_done",
                             "max_high", "max_low", "o_recip", "o_normed", "proj_gated", "x_attn",
                             "mlp_gated", "tok_prod", "tok_scores", "tok_max", "tok_less", "tok_sum",
                             "tok_recip", "tok_normed", "qk_rest", "norm_max", "norm_y2", "norm_t", "norm_y", "qk_scaled"))
            eng.memset(k_room[:, :], 0.0).then_inc(setup["stage_clear"], 1)
            for buf in (hT_rem[0], hT_rem[1], oT_rem):
                eng.memset(buf[:, :], 1.0).then_inc(setup["ones"], 1)
            eng.memset(gelu[64:128, FCT - 1, :], 1.0).then_inc(setup["ones"], 1)
            eng.memset(table_use[:, :], 0.0).then_inc(setup["ones"], 1)
            eng.memset(v_aug[:, :, :, :], 1.0).then_inc(setup["ones"], 1)
            eng.wait_ge(setup["c_exp"], 2)
            eng.tensor_scalar(c_exp[:, 1, :], c_exp[:, 0, :], 1.0, None, ALU.add).then_inc(setup["silu"], 1)
            eng.tensor_scalar(c_exp_rem[:, 1, :], c_exp_rem[:, 0, :], 1.0, None, ALU.add).then_inc(setup["silu"], 1)
            eng.memset(silu_rem[:, :], 1.0).then_inc(setup["silu"], 1)
            eng.wait_ge(setup["silu"], 3)
            eng.reciprocal(c_exp[:, 0, :], c_exp[:, 1, :]).then_inc(setup["silu"], 1)
            eng.reciprocal(c_exp_rem[:, 0, :], c_exp_rem[:, 1, :]).then_inc(setup["silu"], 1)
            eng.wait_ge(setup["silu"], 5)
            eng.tensor_tensor(silu[:, :], cT[:, :], c_exp[:, 0, :], ALU.mult).then_inc(setup["silu"], 1)
            eng.tensor_tensor(silu_rem[0:REM, :], cT_rem[0:REM, :], c_exp_rem[:, 0, :], ALU.mult)\
               .then_inc(setup["silu"], 1)
            eng.wait_ge(setup["gain"], 64)
            eng.wait_ge(setup["const"], CONSTS)
            eng.tensor_scalar(gain[:, :], gain[:, :], float(DIM) ** 0.5, None, ALU.mult).then_inc(setup["picks"], 1)
            eng.tensor_scalar(spread[:, :], spread[:, :], head_gain[:, 0:1], float(HD) ** 0.5, ALU.mult, ALU.mult)\
               .then_inc(setup["picks"], 1)
            eng.tensor_copy(copier[:, :].rearrange("p (o n) -> p o n", n=REM), ident[0:REM, 0:REM]
                            .rearrange("p (o n) -> p o n", o=1).broadcast_to([REM, COPIES, REM]))\
               .then_inc(setup["picks"], 1)
            eng.wait_ge(setup["picks"], 3)
            def stand_alone(eng):
                eng.sem_inc(setup["carrier"], 1)

            def statistics(J, l, i, h=0):
                pre, piece = ("n1", "n2")[i], Piece(i, h)
                if i == 0:
                    need(eng, "x_mlp", J, 1, ago=3)
                else:
                    need(eng, "x_attn", J, h)
                need(eng, pre + "_ready", J, piece.normed, ago=1)
                stand_alone(eng)
                for b in piece.seqs:
                    eng.bn_stats(stats[i][:, b, :], x[:, bass.ds(J.in_layer(GB) + b, 1), :].rearrange("p o d -> p (o d)"))\
                       .then_inc(S[pre + "_stats"], 1)
                need(eng, pre + "_stats", J, piece.last_seq)
                stand_alone(eng)
                for b in piece.seqs:
                    eng.bn_aggr(moments[i][:, b, :], stats[i][:, b, :]).then_inc(S[pre + "_aggr"], 1)
                need(eng, pre + "_aggr", J, piece.last_seq)
                at = piece.here
                if l == 0:
                    eng.tensor_tensor(mean_sq[:, 0, at], moments[i][:, at, 0], moments[i][:, at, 0], ALU.mult)\
                       .then_inc(S[pre + "_var"], 1)
                    need(eng, pre + "_var", J, piece.var)
                    eng.tensor_tensor(mean_sq[:, 1, at], mean_sq[:, 0, at], moments[i][:, at, 1], ALU.add)\
                       .then_inc(S[pre + "_var"], 1)
                    need(eng, pre + "_var", J, piece.var + 1)
                    eng.tensor_scalar(var[i][:, at], mean_sq[:, 1, at], float(DIM), 1e-24, ALU.mult, ALU.max)\
                       .then_inc(S[pre + "_var"], 1)
                else:
                    eng.tensor_scalar(var[i][:, at], moments[i][:, at, 1], 1e-6, None, ALU.add)\
                       .then_inc(S[pre + "_var"], 3)

            def normalise(J, l, i, h=0):
                pre, piece = ("n1", "n2")[i], Piece(i, h)
                need(eng, pre + "_rstd", J, piece.rstd)
                need(eng, ("t1_done", "t2_done")[i], J, 1 if i == 0 else h, ago=1)
                for b in piece.seqs:
                    src = x[:, bass.ds(J.in_layer(GB) + b, 1), :].rearrange("p o d -> p (o d)")
                    if l == 0:
                        ins = eng.tensor_scalar(normed[i][:, b, :], src, rstd[i][:, b:b + 1], None, ALU.mult)
                    else:
                        ins = eng.tensor_scalar(normed[i][:, b, :], src, moments[i][:, b, 0:1], rstd[i][:, b:b + 1],
                                                ALU.subtract, ALU.mult)
                    ins.then_inc(S[pre + "_ready"], 1)
                need(eng, pre + "_ready", J, piece.normed)
                n = len(piece.seqs)
                eng.tensor_copy(normed_last[i][:, piece.here, :].rearrange("p b (o n) -> p b o n", n=REM),
                                normed[i][:, piece.here, 128:DIM].rearrange("p b (o n) -> p b o n", o=1)
                                .broadcast_to([128, n, COPIES, REM])).then_inc(S[pre + "_ready"], 1)

            def modulated(J, kinds="aa"):
                need(eng, "mods1", J, 1)
                need(eng, "t1_done", J, 1)
                name, k = h_read_by(0, kinds)
                need(eng, name, J, k, ago=1)
                bank = lin[LIN_BANK["T1_1"]]
                for b in range(2, 4):
                    c = (b - 2) * 256
                    eng.tensor_scalar(hT_last[0][:, b * TOK:(b + 1) * TOK], bank[0:REM_ROWS, c + TOK:c + 2 * TOK],
                                      mods_rem[0][:, 1, b:b + 1], mods_rem[0][:, 0, b:b + 1], ALU.mult, ALU.add)\
                       .then_inc(S["h1_ready_dve"], 1)
                for b in range(2, 4):
                    c = (b - 2) * 256
                    eng.tensor_scalar(hT[0][:, b * TOK:(b + 1) * TOK], bank[:, c:c + TOK],
                                      mods[0][:, 1, b:b + 1], mods[0][:, 0, b:b + 1], ALU.mult, ALU.add)\
                       .then_inc(S["h1_ready_dve"], 1)

            def last_parts(J, i, h=0):
                done, other, piece = ("h1_parts", "h2_parts")[i], ("h2_parts", "h1_parts")[i], Piece(i, h)
                k, tok = piece.parts, piece.tokens
                need(eng, ("h1_ready_act", "h2_ready_act")[i], J, 4 * h + 1)
                if i == 0:
                    need(eng, "h1_ready_dve", J, 1)
                if i == 1 and h == 0:
                    need(eng, "fc1_done", J, 2 * FCT - 1, ago=1)
                eng.tensor_copy(hT_rem[i][0:BIAS_ROW, tok], hT_last[i][0:BIAS_ROW, tok])
                eng.tensor_copy(hT_rem[i][MID_ROW:REM_ROWS, tok], hT_last[i][MID_ROW:REM_ROWS, tok])\
                   .then_inc(S[done], 1)
                need(eng, done, J, k)
                if h == 0:
                    need(eng, other, J, (7, 3)[i], ago=2 if i == 0 else 0)
                eng.tensor_tensor(h_rest[MID_ROW:REM_ROWS, tok], hT_last[i][MID_ROW:REM_ROWS, tok],
                                  hT_rem[i][MID_ROW:REM_ROWS, tok], ALU.subtract).then_inc(S[done], 1)
                need(eng, done, J, k + 1)
                eng.tensor_copy(hT_rem[i][MID_ROW:REM_ROWS, tok], h_rest[MID_ROW:REM_ROWS, tok])\
                   .then_inc(S[done], 1)
                need(eng, done, J, k + 2)
                eng.tensor_tensor(hT_rem[i][LOW_ROW:REM_ROWS, tok], h_rest[LOW_ROW:REM_ROWS, tok],
                                  hT_rem[i][LOW_ROW:REM_ROWS, tok], ALU.subtract).then_inc(S[done], 1)

            def raw(J, T):
                need(eng, "qk_done", J, T)
                if T == 0:
                    need(eng, "qk_scaled", J, QKT - 1, ago=1)
                    need(eng, "qk_sq", J, QKT - 1, ago=1)
                eng.tensor_copy(qk_raw[:, T, :], score_bank[T % 2][0:QKM, :]).then_inc(S["qk_taken"], 1)

            def head_norms(J):
                need(eng, "norm_done", J, 0)
                need(eng, "norm_y", J, 0, ago=1)
                eng.tensor_scalar(norm2[:, :], score_bank[1][0:2 * HEADS, :], 1e-24, None, ALU.max)\
                   .then_inc(S["norm_max"], 1)

            def newton(J):
                need(eng, "norm_exp", J, 0)
                eng.tensor_tensor(norm_t[:, 1, :], norm_y[:, 0, :], norm_y[:, 0, :], ALU.mult)\
                   .then_inc(S["norm_y2"], 1)
                need(eng, "norm_y2", J, 0)
                eng.scalar_tensor_tensor(out=norm_t[:, 0, :], in0=norm_t[:, 1, :], scalar=-0.5,
                                         in1=norm2[:, :], op0=ALU.mult, op1=ALU.mult)\
                   .then_inc(S["norm_t"], 1)
                need(eng, "norm_t", J, 0)
                need(eng, "spread_done", J, QKT - 1, ago=1)
                eng.scalar_tensor_tensor(out=norm_y[:, 1, :], in0=norm_t[:, 0, :], scalar=1.5,
                                         in1=norm_y[:, 0, :], op0=ALU.add, op1=ALU.mult)\
                   .then_inc(S["norm_y"], 1)

            def fit(J):
                for T in range(QKT):
                    need(eng, "spread_done", J, T)
                    if T == 0:
                        need(eng, "qk_mid", J, QKT - 1, ago=1)
                    eng.tensor_tensor(qk_fit[:, T, :], qk_raw[:, T, :], score_bank[T % 2][0:QKM, :], ALU.mult)\
                       .then_inc(S["qk_scaled"], 1)

            def mid(J, l, T):
                need(eng, "qk_high", J, T)
                if T == 0:
                    need(eng, "qk_low", J, QKT - 1, ago=1)
                if l == 0:
                    eng.tensor_tensor(qk_rest[:, T, :], qk_fit[:, T, :], part_high[:, T, :], ALU.subtract)\
                       .then_inc(S["qk_rest"], 1)
                else:
                    eng.tensor_tensor(qk_rest[:, T, :], score_bank[T % 2][0:QKM, :],
                                      part_high[:, T, :], ALU.subtract).then_inc(S["qk_taken"], 1)
                need(eng, "qk_rest" if l == 0 else "qk_taken", J, T)
                if T == 0:
                    need(eng, "parts_stored", J, 2, ago=1)
                eng.tensor_copy(part_mid[:, T, :], qk_rest[:, T, :]).then_inc(S["qk_mid"], 1)

            def mid_or_raw(J, l, T):
                if l == 0:
                    raw(J, T)
                else:
                    mid(J, l, T)

            def maximum(J, i):
                b, c = divmod(i, CHUNKS)
                need(eng, "score_done", J, i)
                if c == 0:
                    need(eng, "max_low", J, b, ago=1)
                eng.tensor_reduce(maxima[:, b, CH * c:CH * c + CH],
                                  score_bank[i % 2][:, :].rearrange("p (h k) -> p h k", h=CH), AX_X, ALU.max)\
                   .then_inc(S["max_done"], 1)

            def split_max(J, b):
                need(eng, "max_done", J, (b + 1) * CHUNKS - 1)
                need(eng, "mT_done", J, b, ago=1)
                eng.tensor_copy(max_parts[:, b, 0, :], maxima[:, b, :]).then_inc(S["max_high"], 1)
                need(eng, "max_high", J, b)
                eng.tensor_tensor(max_parts[:, b, 1, :], maxima[:, b, :], max_parts[:, b, 0, :], ALU.subtract)\
                   .then_inc(S["max_low"], 1)

            def divide(G, b):
                need(eng, "o_tok_done", G, b)
                o = o_bank[b % 2][:, :].rearrange("p (h r) -> p h r", r=32)
                if b >= 2:
                    need(eng, "o_normed", G, b - 2)
                    need(eng, "o_flip_done", G, b - 2)
                else:
                    need(eng, "o_normed", G, b + 2, ago=1)
                    need(eng, "o_flip_done", G, b + 2, ago=1)
                eng.reciprocal(o_recip[:, b % 2, :].rearrange("p (h r) -> p h r", r=1), o[:, :, HD:HD + 1])\
                   .then_inc(S["o_recip"], 1)
                need(eng, "o_recip", G, b)
                eng.tensor_tensor(o_tok[:, b % 2, :].rearrange("p (h d) -> p h d", d=HD), o[:, :, 0:HD],
                                  o_recip[:, b % 2, :].rearrange("p (h r) -> p h r", r=1)
                                  .broadcast_to([128, HEADS, HD]), ALU.mult).then_inc(S["o_normed"], 1)

            def residual(G, h, which):
                done, gated_name, x_name, use = (
                    ("proj_done", "proj_gated", "x_attn", "PJ"), ("fc2_done", "mlp_gated", "x_mlp", "M"))[which]
                need(eng, done, G, h)
                if h == 0 and which == 0:
                    need(eng, "gates_loaded", G, 1)
                if which == 0:
                    need(eng, "x_mlp", G, h, ago=1)
                    need(eng, "n1_ready", G, GB - 1)
                else:
                    need(eng, "x_attn", G, h)
                    need(eng, "n2_ready", G, Piece(1, h).normed)
                eng.tensor_tensor(gated[:, h, :], lin[LIN_BANK[f"{use}{h}"]][:, 0:2 * DIM],
                                  gates[:, which, 2 * h:2 * h + 2, :].rearrange("p b n -> p (b n)"), ALU.mult)\
                   .then_inc(S[gated_name], 1)
                if which == 1:
                    return
                need(eng, gated_name, G, h)
                xs = x[:, bass.ds(G.in_layer(GB) + 2 * h, 2), :].rearrange("p b n -> p (b n)")
                eng.tensor_tensor(xs, xs, gated[:, h, :], ALU.add).then_inc(S[x_name], 1)

            def token_scores(J, b):
                need(eng, "tok_ready", J, b)
                if b:
                    need(eng, "tok_scores", J, b - 1)
                else:
                    need(eng, "tok_scores", J, GB - 1, ago=1)
                shape = [128, HEADS, HEADS, HD]
                q = tok_qkv[:, b, 0:DIM].rearrange("p (h o d) -> p h o d", o=1, d=HD).broadcast_to(shape)
                k = tok_qkv[:, b, DIM:2 * DIM].rearrange("p (o k d) -> p o k d", o=1, d=HD).broadcast_to(shape)
                prod = tok_prod.rearrange("p (h k d) -> p h k d", h=HEADS, d=HD)
                eng.tensor_tensor(prod, q, k, ALU.mult).then_inc(S["tok_prod"], 1)
                need(eng, "tok_prod", J, b)
                if b >= 2:
                    need(eng, "tok_weighted", J, b - 2)
                    need(eng, "tok_sum", J, b - 2)
                else:
                    need(eng, "tok_weighted", J, b + 2, ago=1)
                    need(eng, "tok_sum", J, b + 2, ago=1)
                e = tok_e[:, b % 2, :]
                eng.tensor_reduce(e, tok_prod.rearrange("p (s d) -> p s d", d=HD), AX_X, ALU.add)\
                   .then_inc(S["tok_scores"], 1)
                need(eng, "tok_scores", J, b)
                e3 = e.rearrange("p (h k) -> p h k", h=HEADS)
                eng.tensor_reduce(tok_small[:, b % 2, :], e3, AX_X, ALU.max).then_inc(S["tok_max"], 1)
                need(eng, "tok_max", J, b)
                eng.tensor_tensor(tok_less[:, b % 2, :].rearrange("p (h k) -> p h k", h=HEADS), e3,
                                  tok_small[:, b % 2, :].rearrange("p (h o) -> p h o", o=1)
                                  .broadcast_to([128, HEADS, HEADS]), ALU.subtract).then_inc(S["tok_less"], 1)

            def token_denominators(J, b):
                need(eng, "tok_exp", J, b)
                eng.tensor_reduce(tok_small[:, 2 + b % 2, :], tok_e[:, b % 2, :].rearrange("p (h k) -> p h k", h=HEADS),
                                  AX_X, ALU.add).then_inc(S["tok_sum"], 1)
                need(eng, "tok_sum", J, b)
                eng.reciprocal(tok_small[:, 4 + b, :], tok_small[:, 2 + b % 2, :]).then_inc(S["tok_recip"], 1)

            def token_outputs(J, b):
                need(eng, "tok_recip", J, b)
                need(eng, "tok_values", J, b)
                if b >= 2:
                    need(eng, "mixed_stored", J, b - 2)
                else:
                    need(eng, "mixed_stored", J, b + 2, ago=1)
                eng.tensor_tensor(tok_o[:, b % 2, :].rearrange("p (h d) -> p h d", d=HD),
                                  o_bank[b % 2][:, 0:DIM].rearrange("p (h d) -> p h d", d=HD),
                                  tok_small[:, 4 + b, :].rearrange("p (h o) -> p h o", o=1)
                                  .broadcast_to([128, HEADS, HD]), ALU.mult).then_inc(S["tok_normed"], 1)

            eng.wait_ge(setup["x"], 64)
            first = Group(0)
            statistics(first, 0, 0)
            eng.wait_ge(setup["part_of"], 16)
            for l in range(LAYERS):
                eng.wait_ge(setup[f"staged{l}"], 48)
                if l:
                    eng.wait_ge(setup["split"], 7 * l)
                eng.tensor_copy(w_parts[:, 0, :], w_stage[l]).then_inc(setup["split"], 1)
                eng.wait_ge(setup["split"], 7 * l + 1)
                eng.tensor_tensor(w_rest, w_stage[l], w_parts[:, 0, :], ALU.subtract).then_inc(setup["split"], 1)
                eng.tensor_scalar(w_h_rem[l][:, :], w_parts[:, 0, :], part_of[:, 0:1], None, ALU.mult)\
                   .then_inc(setup["split"], 1)
                eng.wait_ge(setup["split"], 7 * l + 3)
                eng.tensor_copy(w_parts[:, 1, :], w_rest).then_inc(setup["split"], 1)
                eng.wait_ge(setup["split"], 7 * l + 4)
                eng.tensor_tensor(w_rest, w_rest, w_parts[:, 1, :], ALU.subtract).then_inc(setup["split"], 1)
                eng.scalar_tensor_tensor(out=w_h_rem[l][:, :], in0=w_parts[:, 1, :], scalar=part_of[:, 1:2],
                                         in1=w_h_rem[l][:, :], op0=ALU.mult, op1=ALU.add)\
                   .then_inc(setup["split"], 1)
                eng.wait_ge(setup["split"], 7 * l + 6)
                eng.scalar_tensor_tensor(out=w_h_rem[l][:, :], in0=w_rest, scalar=part_of[:, 2:3],
                                         in1=w_h_rem[l][:, :], op0=ALU.mult, op1=ALU.add)\
                   .then_inc(setup["split"], 1)
                eng.wait_ge(setup["mods_done"], l + 1)
                for main, n, bank in ((mod_main, 128, mod_banks[l][0][:, 0:128]),
                                      (mod_last, REM, mod_banks[l][0][0:REM, 128:256])):
                    v = bank.rearrange("p (i w b) -> p i w b", i=2, w=2)
                    d = main[:, l, :, :].rearrange("p (i w) b -> p i w b", w=2)
                    eng.tensor_copy(d[:, :, 0, :], v[:, :, 0, :])
                    if l:
                        ins = eng.tensor_scalar(d[:, :, 1, :], v[:, :, 1, :], 1.0, None, ALU.add)
                    else:
                        eng.tensor_scalar(d[:, 0, 1, :], v[:, 0, 1, :], 1.0, gain[0:n, 0:1], ALU.add, ALU.mult)
                        ins = eng.tensor_scalar(d[:, 1, 1, :], v[:, 1, 1, :], 1.0, gain[0:n, 1:2], ALU.add, ALU.mult)
                    ins.then_inc(setup["mods_kept"], 1)
            eng.wait_ge(setup["mods_done"], LAYERS + 1)
            eng.tensor_copy(mod_rem[:, :, :, :].rearrange("p l i b -> p (l i b)"), lin[0][0:REM_ROWS, :])\
               .then_inc(setup["mods_kept"], 1)
            eng.wait_ge(setup["mods_kept"], 2 * LAYERS + 1)
            normalise(first, 0, 0)
            statistics(first.plus(1), 0, 0)
            modulated(first)
            last_parts(first, 0)
            normalise(first.plus(1), 0, 0)
            for T in range(QKT):
                raw(first, T)
            head_norms(first)
            newton(first)
            fit(first)
            for T in range(QKT):
                mid(first, 0, T)
            for i in range(AHEAD):
                maximum(first, i)
                if i % CHUNKS == CHUNKS - 1:
                    split_max(first, i // CHUNKS)

            def body(G, l, nxt, after):
                J = G.plus(1)
                kinds = KINDS[l] + (KINDS[nxt] if nxt is not None else "-")
                if kinds[0] == "a":
                    for i in range(AHEAD, STEPS):
                        maximum(G, i)
                    if nxt is not None:
                        modulated(J, kinds)
                    split_max(G, GB - 1)
                    if nxt is not None:
                        last_parts(J, 0)
                    take = mid_or_raw if kinds[1] == "a" else None
                    divide(G, 0)
                    if take:
                        take(J, nxt, 0)
                        take(J, nxt, 1)
                    divide(G, 1)
                    if take:
                        take(J, nxt, 2)
                    if after is not None:
                        statistics(G.plus(2), after, 0)
                    if nxt == 0:
                        head_norms(J)
                    divide(G, 2)
                    if after is not None and nxt != 0:
                        normalise(G.plus(2), after, 0)
                    if nxt == 0:
                        newton(J)
                    residual(G, 0, 0)
                    divide(G, 3)
                    statistics(G, l, 1, 0)
                    normalise(G, l, 1, 0)
                    if after is not None and nxt == 0:
                        normalise(G.plus(2), after, 0)
                    if nxt == 0:
                        fit(J)
                        for T in range(QKT):
                            mid(J, 0, T)
                else:
                    token_outputs(G, 0)
                    token_scores(G, 3)
                    token_outputs(G, 1)
                    if nxt is not None:
                        modulated(J, kinds)
                        last_parts(J, 0)
                    token_denominators(G, 2)
                    token_denominators(G, 3)
                    token_outputs(G, 2)
                    token_outputs(G, 3)
                    residual(G, 0, 0)
                    statistics(G, l, 1, 0)
                    if after is not None:
                        statistics(G.plus(2), after, 0)
                    normalise(G, l, 1, 0)
                    if after is not None:
                        normalise(G.plus(2), after, 0)
                    if nxt is not None:
                        token_scores(J, 0)
                residual(G, 1, 0)
                last_parts(G, 1, 0)
                statistics(G, l, 1, 1)
                early = kinds[1] == "a" and nxt != 0
                if early:
                    maximum(J, 0)
                normalise(G, l, 1, 1)
                if early:
                    maximum(J, 1)
                if kinds == "tt":
                    token_scores(J, 1)
                last_parts(G, 1, 1)
                residual(G, 0, 1)
                if kinds[1] == "a":
                    for i in range(2 if early else 0, AHEAD):
                        maximum(J, i)
                        if i % CHUNKS == CHUNKS - 1:
                            split_max(J, i // CHUNKS)
                elif kinds == "at":
                    token_scores(J, 0)
                    token_scores(J, 1)
                if kinds[1] == "t":
                    token_denominators(J, 0)
                    token_denominators(J, 1)
                    token_scores(J, 2)
                residual(G, 1, 1)

            layers_from_after_next(eng, body)

        @block.tensor
        def _(eng):
            start_with(eng, ("tok_values", "t1_done", "t2_done", "qk_done", "v_done", "score_done", "mT_done", "st_done",
                             "pv_done", "o_tok_done", "o_flip_done", "proj_done", "fc1_done", "fc2_done",
                             "tok_done", "norm_done", "spread_done"))

            def bank_of(use, J, this, nxt):
                before, turns = use_before(use, this, nxt)
                if before is not None:
                    _, name, k = LIN_USES[before]
                    need(eng, name, J, k, ago=(use in OF_NEXT) - (before in OF_NEXT) + turns)
                return lin[LIN_BANK[use]]

            eng.wait_ge(setup["silu"], 7)
            for l in range(LAYERS):
                eng.wait_ge(setup[f"ada{l}"], 32)
                shifts, rows = mod_banks[l]
                for j, k in enumerate((0, 1, 3, 4)):
                    for m, c0, c1 in ((128, 0, k * DIM), (REM, 128, k * DIM + 128)):
                        o = shifts[0:m, c0 + j * SEQS:c0 + (j + 1) * SEQS]
                        eng.matmul(o, w_ada[l][:, c1:c1 + m], silu[:, :], start=True, stop=False)
                        eng.matmul(o, w_ada_rem[l][:, c1:c1 + m], silu_rem[:, :], start=False, stop=True)
                for w in range(2):
                    o = rows[0:SEQS, w * DIM:(w + 1) * DIM]
                    c1 = (2 + 3 * w) * DIM
                    eng.matmul(o, silu[:, :], w_ada[l][:, c1:c1 + DIM], start=True, stop=False)
                    ins = eng.matmul(o, silu_rem[:, :], w_ada_rem[l][:, c1:c1 + DIM], start=False, stop=True)
                ins.then_inc(setup["mods_done"], 1)
            eng.wait_ge(setup["mods_kept"], 2 * LAYERS)
            eng.matmul(lin[0][0:REM_ROWS, :], copier[:, :], mod_last[:, :, :, :].rearrange("p l i b -> p (l i b)"),
                       start=True, stop=True).then_inc(setup["mods_done"], 1)

            def flip_rows(J, i, h, **turn):
                use = ("T1_", "T2_")[i] + str(h)
                need(eng, ("n1_ready", "n2_ready")[i], J, Piece(i, 0 if i == 0 else h).ready)
                bank = bank_of(use, J, **turn)
                for b in (0, 1):
                    src = normed[i][:, 2 * h + b, :]
                    eng.transpose(bank[:, b * 256:b * 256 + TOK], src[:, 0:128], ident[:, :])
                    ins = eng.transpose(bank[0:REM_ROWS, b * 256 + TOK:(b + 1) * 256],
                                        normed_last[i][:, 2 * h + b, :], ident[:, :])
                ins.then_inc(S[("t1_done", "t2_done")[i]], 1)

            def queries_keys(J, l, T, long=True, short=True):
                bank = score_bank[T % 2][0:QKM, :]
                cols = slice(W_QK + T * QKM, W_QK + (T + 1) * QKM)
                if long:
                    if T == 0:
                        need(eng, "h1_ready_act", J, 3)
                        need(eng, "h1_ready_dve", J, 3)
                    if T < 2:
                        need(eng, "max_done", J, STEPS - 2 + T, ago=1)
                    else:
                        need(eng, "qk_taken", J, 0)
                    eng.matmul(bank, w_h[l][:, cols], hT[0][:, :], start=True, stop=False)
                if short:
                    if T == 0:
                        need(eng, "h1_parts", J, 3)
                    eng.matmul(bank, w_h_rem[l][:, cols], hT_rem[0][:, :], start=False, stop=True)\
                       .then_inc(S["qk_done"], 1)

            def head_norms(J):
                need(eng, "qk_taken", J, 1)
                for T in range(QKT):
                    need(eng, "qk_sq", J, T)
                    ins = eng.matmul(score_bank[1][0:2 * HEADS, :], pick[:, T, :], qk_sq[:, T, :], start=T == 0,
                                     stop=T == QKT - 1)
                ins.then_inc(S["norm_done"], 1)

            def spread_norms(J):
                need(eng, "norm_y", J, 0)
                for T in range(QKT):
                    if T == 0:
                        need(eng, "qk_taken", J, 2)
                    if T == 2:
                        need(eng, "qk_scaled", J, 0)
                    eng.matmul(score_bank[T % 2][0:QKM, :], spread[:, T * QKM:(T + 1) * QKM], norm_y[:, 1, :],
                               start=True, stop=True).then_inc(S["spread_done"], 1)

            def values(J, l, h, **turn):
                bank = bank_of(f"V{h}", J, **turn)
                for b in range(2):
                    tok = slice((2 * h + b) * TOK, (2 * h + b + 1) * TOK)
                    o = bank[:, b * DIM:(b + 1) * DIM]
                    cols = slice(W_V, W_V + DIM)
                    eng.matmul(o, hT[0][:, tok], w_h[l][:, cols], start=True, stop=False)
                    ins = eng.matmul(o, hT_rem[0][:, tok], w_h_rem[l][:, cols], start=False, stop=True)
                ins.then_inc(S["v_done"], 1)

            def scores(J, i):
                b, c = divmod(i, CHUNKS)
                if i == 0:
                    need(eng, "stack_loaded", J, 5)
                if i >= 2:
                    need(eng, "max_done", J, i - 2)
                else:
                    need(eng, "max_done", J, i - 2 + STEPS, ago=1)
                tok = slice(b * TOK, (b + 1) * TOK)
                for j in range(CH):
                    h = CH * c + j
                    ins = eng.matmul(score_bank[i % 2][:, j * TOK:(j + 1) * TOK], q_stack[0:SCORE_ROWS, h, tok],
                                     k_stack[0:SCORE_ROWS, h, tok], start=True, stop=True)
                ins.then_inc(S["score_done"], 1)

            def flip_max(J, b, **turn):
                need(eng, "max_low", J, b)
                bank_of(f"mT{b}", J, **turn)
                eng.transpose(lin_b[LIN_BANK[f"mT{b}"]][0:2 * HEADS, 0:TOK],
                              max_parts[:, b, :, :].rearrange("p i h -> p (i h)"), ident_b[:, :])\
                   .then_inc(S["mT_done"], 1)

            def shifted_scores(G, i):
                b, c = divmod(i, CHUNKS)
                if c == 0:
                    need(eng, f"m_loaded{b}", G, 1)
                if i >= 2:
                    need(eng, "exp_done", G, i - 2)
                else:
                    need(eng, "exp_done", G, i - 2 + STEPS, ago=1)
                tok = slice(b * TOK, (b + 1) * TOK)
                for j in range(CH):
                    h = CH * c + j
                    ins = eng.matmul(st_bank[i % 2][:, j * TOK:(j + 1) * TOK], k_stack[:, h, tok],
                                     q_stack[:, h, tok], start=True, stop=True)
                ins.then_inc(S["st_done"], 1)

            def weighted_values(G, i):
                b, c = divmod(i, CHUNKS)
                need(eng, "exp_done", G, i)
                if c == 0:
                    need(eng, "v_ready", G, b // 2)
                    if b >= 2:
                        need(eng, "o_normed", G, b - 2)
                    else:
                        need(eng, "o_normed", G, b + 2, ago=1)
                for j in range(CH):
                    ins = eng.matmul(o_bank[b % 2][32 * j:32 * j + 32, c * TOK:(c + 1) * TOK],
                                     v_aug[:, b, CH * c + j, :], probs[:, i % PBUFS, j * TOK:(j + 1) * TOK],
                                     start=True, stop=True)
                ins.then_inc(S["pv_done"], 1)

            def o_to_tokens(G, b):
                need(eng, "o_copied", G, b)
                for c in range(CHUNKS):
                    ins = eng.transpose(o_bank[b % 2][:, c * TOK:(c + 1) * TOK],
                                        o_feat[:, b % 2, c * TOK:(c + 1) * TOK], ident[:, :])
                ins.then_inc(S["o_tok_done"], 1)

            def flip_o(G, b, **turn):
                if turn["this"] == "a":
                    need(eng, "o_normed", G, b)
                    src = o_tok[:, b % 2, :]
                else:
                    need(eng, f"mixed{b}", G, 0)
                    src = mixed[:, b, :]
                bank = bank_of(f"OD{b}", G, **turn)
                eng.transpose(bank[:, 0:TOK], src[:, 0:128], ident[:, :])
                eng.transpose(bank[0:REM, TOK:2 * TOK], src[:, 128:DIM], ident[:, :])\
                   .then_inc(S["o_flip_done"], 1)

            def token_qkv(J, l, b, **turn):
                if b == 0:
                    need(eng, "h1_ready_act", J, 3)
                    need(eng, "h1_ready_dve", J, 3)
                bank = bank_of(f"Q{b}", J, **turn)
                tok = slice(b * TOK, (b + 1) * TOK)
                eng.matmul(bank[:, 0:3 * DIM], hT[0][:, tok], w_h[l][:, 0:3 * DIM], start=True, stop=False)
                if b == 0:
                    need(eng, "h1_parts", J, 3)
                eng.matmul(bank[:, 0:3 * DIM], hT_rem[0][:, tok], w_h_rem[l][:, 0:3 * DIM], start=False, stop=True)\
                   .then_inc(S["tok_done"], 1)

            def token_sums(J, b):
                need(eng, "tok_weighted", J, b)
                if b >= 2:
                    need(eng, "tok_normed", J, b - 2)
                else:
                    need(eng, "tok_normed", J, b + 2, ago=1)
                w = tok_weighted[b % 2].rearrange("p (s k) -> p k s", k=HEADS)
                for k in range(HEADS):
                    ins = eng.matmul(o_bank[b % 2][:, 0:DIM], ident[:, :], w[:, k, :], start=k == 0,
                                     stop=k == HEADS - 1)
                ins.then_inc(S["tok_values"], 1)

            def project(G, l, h, **turn):
                need(eng, "oT_ready", G, 2 * h + 1)
                bank = bank_of(f"PJ{h}", G, **turn)
                for b in range(2):
                    tok = slice((2 * h + b) * TOK, (2 * h + b + 1) * TOK)
                    o = bank[:, b * DIM:(b + 1) * DIM]
                    eng.matmul(o, oT[:, tok], w_o[l][:, :], start=True, stop=False)
                    ins = eng.matmul(o, oT_rem[:, tok], w_o_rem[l][:, :], start=False, stop=True)
                ins.then_inc(S["proj_done"], 1)

            def up(G, l, h, **turn):
                tok = slice(h * GT // 2, (h + 1) * GT // 2)

                def product(T, w, act, **flags):
                    cols = slice(W_F1 + T * 128, W_F1 + T * 128 + FCM[T])
                    return eng.matmul(lin[LIN_BANK[f"F{h}{T}"]][0:FCM[T], 0:GT // 2], w[:, cols], act[:, tok], **flags)

                need(eng, "h2_ready_act", G, 4 * h + 3)
                for T in range(FCT):
                    if T != 1 or h:
                        bank_of(f"F{h}{T}", G, **turn)
                        product(T, w_h[l], hT[1], start=True, stop=False)
                    if T == 0:
                        if h == 0:
                            bank_of(f"F{h}1", G, **turn)
                            product(1, w_h[l], hT[1], start=True, stop=False)
                        need(eng, "h2_parts", G, Piece(1, h).parts + 3)
                    product(T, w_h_rem[l], hT_rem[1], start=False, stop=True).then_inc(S["fc1_done"], 1)
                    yield T

            def down(G, l, b, **turn):
                h = b // 2
                if b % 2 == 0:
                    bank_of(f"M{h}", G, **turn)
                o = lin[LIN_BANK[f"M{h}"]][:, (b % 2) * DIM:(b % 2 + 1) * DIM]
                for T in range(FCT):
                    if b % 2 == 0:
                        need(eng, "gelu_ready", G, h * FCT + T)
                    k = 128 if T < FCT - 1 else FCM[T] + 1
                    ins = eng.matmul(o, gelu[0:k, T, b * TOK:(b + 1) * TOK], w_f2[l][0:k, T, :], start=T == 0,
                                     stop=T == FCT - 1)
                if b % 2:
                    ins.then_inc(S["fc2_done"], 1)

            eng.wait_ge(setup["weights_first"], 16 * 5)
            eng.wait_ge(setup["split"], 7)
            eng.wait_ge(setup["mods_kept"], 2 * LAYERS + 1)
            eng.wait_ge(setup["gates_kept"], LAYERS)
            eng.wait_ge(setup["ones"], ONES)
            eng.wait_ge(setup["const"], CONSTS)
            eng.wait_ge(setup["picks"], 3)
            start = dict(this=None, nxt="a")
            first = Group(0)
            flip_rows(first, 0, 0, **start)
            flip_rows(first, 0, 1, **start)
            for T in range(QKT):
                queries_keys(first, 0, T)
            head_norms(first)
            spread_norms(first)
            values(first, 0, 0, **start)
            values(first, 0, 1, **start)
            eng.wait_ge(setup["clear"], 2)
            for i in range(AHEAD):
                scores(first, i)
            flip_max(first, 0, **start)
            flip_max(first, 1, **start)

            def body(G, l, nxt):
                J = G.plus(1)
                turn = dict(this=KINDS[l], nxt=None if nxt is None else KINDS[nxt])
                this, nxt_kind = turn["this"], turn["nxt"]
                if this == "a":
                    flip_max(G, 2, **turn)
                    for i in range(STEPS + LAG):
                        if i < STEPS:
                            shifted_scores(G, i)
                            if i + AHEAD < STEPS:
                                scores(G, i + AHEAD)
                        if i >= LAG:
                            weighted_values(G, i - LAG)
                        if i == 1 and nxt is not None:
                            flip_rows(J, 0, 0, **turn)
                            flip_rows(J, 0, 1, **turn)
                        if i == 5:
                            flip_max(G, 3, **turn)
                        if nxt_kind == "a":
                            if i in (5, 6):
                                queries_keys(J, nxt, i - 5, short=False)
                            if i == 8:
                                queries_keys(J, nxt, 0, long=False)
                                queries_keys(J, nxt, 1, long=False)
                            if i == 11:
                                queries_keys(J, nxt, 2)
                        if i == 13 and nxt == 0:
                            head_norms(J)
                        if i in (7, 11, 15):
                            o_to_tokens(G, i // 4 - 1)
                        if i in (9, 13):
                            flip_o(G, i // 4 - 2, **turn)
                        if i == 15:
                            project(G, l, 0, **turn)
                    flip_o(G, 2, **turn)
                    o_to_tokens(G, 3)
                else:
                    if nxt is not None:
                        flip_rows(J, 0, 0, **turn)
                        flip_rows(J, 0, 1, **turn)
                    token_sums(G, 1)
                    flip_o(G, 0, **turn)
                    token_sums(G, 2)
                    if nxt is not None:
                        token_qkv(J, nxt, 0, **turn)
                        token_qkv(J, nxt, 1, **turn)
                    flip_o(G, 1, **turn)
                    token_sums(G, 3)
                    project(G, l, 0, **turn)
                    flip_o(G, 2, **turn)
                if nxt == 0:
                    spread_norms(J)
                if nxt_kind == "a":
                    values(J, nxt, 0, **turn)
                flip_o(G, 3, **turn)
                project(G, l, 1, **turn)
                flip_rows(G, 1, 0, **turn)
                if nxt_kind == "a":
                    values(J, nxt, 1, **turn)
                elif nxt_kind == "t":
                    for b in range(0 if this == "a" else 2, GB):
                        token_qkv(J, nxt, b, **turn)
                ahead = iter(range(AHEAD))

                def some_scores(n):
                    if nxt_kind == "a":
                        for _ in range(n):
                            scores(J, next(ahead))

                early = 0 if nxt == 0 else 1
                for T in up(G, l, 0, **turn):
                    some_scores(early * (T in (1, 2)))
                flip_rows(G, 1, 1, **turn)
                down(G, l, 0, **turn)
                some_scores(early)
                down(G, l, 1, **turn)
                some_scores(early)
                for T in up(G, l, 1, **turn):
                    some_scores(1)
                down(G, l, 2, **turn)
                some_scores(1 if early else 3)
                if nxt_kind == "a":
                    flip_max(J, 0, **turn)
                down(G, l, 3, **turn)
                some_scores(2 if early else 4)
                if nxt_kind == "t":
                    if this == "a":
                        need(eng, "o_normed", G, GB - 1)
                    token_sums(J, 0)
                if nxt_kind == "a":
                    flip_max(J, 1, **turn)

            eng.wait_ge(setup["weights"], 16 * 5 * (LAYERS - 1))
            eng.wait_ge(setup["split"], 7 * LAYERS)
            layers(eng, body)


def kernel(**inputs):
    import numpy as np
    import concourse.bacc as bacc
    from concourse.bass_utils import run_bass_kernel_spmd

    names = {
        0: ("qkv_w", "qkv_b", "proj_w", "proj_b", "fc1_w", "fc1_b", "fc2_w", "fc2_b", "ada_w", "ada_b"),
        1: ("w_qkv", "b_qkv", "w_proj", "b_proj", "w_fc1", "b_fc1", "w_fc2", "b_fc2", "w_ada", "b_ada"),
        2: ("qkv_w", "qkv_b", "out_w", "out_b", "w1", "b1", "w2", "b2", "ada_w", "ada_b"),
        3: ("qkv_w", "qkv_b", "proj_w", "proj_b", "fc1_w", "fc1_b", "fc2_w", "fc2_b", "ada_w", "ada_b"),
    }
    mine = ("qkv_w", "qkv_b", "o_w", "o_b", "f1_w", "f1_b", "f2_w", "f2_b", "ada_w", "ada_b")
    arrays = {"x": inputs["x"], "cT": np.asarray(inputs["cond_1152"]).T}
    part_of = np.zeros((128, 3), np.float32)
    for part, rows in enumerate(((0, MID_ROW, LOW_ROW), (REM, MID_ROW + REM), (2 * REM,))):
        for r in rows:
            part_of[r:r + REM, part] = 1
        part_of[BIAS_ROW + part, part] = 1
    arrays["part_of"] = part_of
    for short in ("g1", "g2", "qg", "kg"):
        arrays[short] = inputs[f"L0_cond_{short}"]
    for l, theirs in names.items():
        w = {}
        for a, b in zip(mine, theirs):
            w[a] = np.asarray(inputs[f"L{l}_cond_{b}"])
            w[a] = w[a].T if l == 0 and w[a].ndim == 2 else w[a]
        full = {a: np.concatenate([w[f"{a}_w"], w[f"{a}_b"][None]]) for a in ("qkv", "o", "f1", "f2", "ada")}
        qk, v = full["qkv"][:, :2 * DIM], full["qkv"][:, 2 * DIM:]
        if KINDS[l] == "a":
            qk = np.swapaxes(qk.reshape(DIM + 1, 2, HEADS, HD), -1, -2).reshape(qk.shape)
        arrays[f"h_w{l}"] = np.concatenate([qk, v, full["f1"]], axis=1)
        arrays[f"o_w{l}"], arrays[f"f2_w{l}"], arrays[f"ada{l}"] = full["o"], full["f2"], full["ada"]

    nc = bacc.Bacc("TRN2", target_bir_lowering=False, num_devices=1)
    feeds, aps = {}, {}
    for name, a in arrays.items():
        a = np.ascontiguousarray(a)
        feeds[f"in_{name}"] = a
        aps[name] = nc.dram_tensor(f"in_{name}", a.shape, mybir.dt.from_np(a.dtype), kind="ExternalInput").ap()
    out = nc.dram_tensor("out_x", (SEQS, TOK, DIM), F32, kind="ExternalOutput").ap()
    blocks_kernel(nc, aps, out)
    r = run_bass_kernel_spmd(nc, [feeds], core_ids=[0])
    return r.results[0]["out_x"]
```
